# Optimizing a Trainium2 kernel written in Bass

```python
import numpy as np
import jax
import jax.numpy as jnp

def _softmax(x, axis=-1):
    return jax.nn.softmax(x, axis=axis)

def _gelu(x):
    return jax.nn.gelu(x, approximate=True)

def _silu(x):
    return jax.nn.silu(x)

def _sigmoid(x):
    return jax.nn.sigmoid(x)

def _layernorm(x, axis=-1, eps=1e-05):
    m = jnp.mean(x, axis=axis, keepdims=True)
    v = jnp.var(x, axis=axis, keepdims=True)
    return (x - m) / jnp.sqrt(v + eps)

def _scatter_add(tgt, idx, src, axis=0):
    return tgt.at[idx].add(src)

def _segment_sum(src, seg, n):
    return jax.ops.segment_sum(src, seg, n)
kernel_name = 'mk_seq_postln_d2_jaxref_r4_f4770d'

def setup_inputs(seed: int=0):
    np.random.seed(seed)
    _w = jnp.asarray

    def _L0_attn_setup():
        import jax, jax.numpy as jnp
        import numpy as np
        import math
        DIM = 256
        NUM_HEADS = 16
        HEAD_DIM = DIM // NUM_HEADS
        B, S = (2, 512)
        key = jax.random.key(seed)
        ks = jax.random.split(key, 9)
        sc = 0.02
        return {'x': jax.random.normal(ks[0], (B, S, DIM), jnp.float32), 'Wq': jax.random.normal(ks[1], (DIM, DIM), jnp.float32) * sc, 'bq': jax.random.normal(ks[2], (DIM,), jnp.float32) * sc, 'Wk': jax.random.normal(ks[3], (DIM, DIM), jnp.float32) * sc, 'bk': jax.random.normal(ks[4], (DIM,), jnp.float32) * sc, 'Wv': jax.random.normal(ks[5], (DIM, DIM), jnp.float32) * sc, 'bv': jax.random.normal(ks[6], (DIM,), jnp.float32) * sc, 'Wo': jax.random.normal(ks[7], (DIM, DIM), jnp.float32) * sc, 'bo': jax.random.normal(ks[8], (DIM,), jnp.float32) * sc}
    _L0_attn_in = _L0_attn_setup()

    def _L0_ffn_setup():
        import math
        import jax, jax.numpy as jnp
        import numpy as np
        B, S, D, H, E, K = (4, 512, 256, 1024, 8, 2)
        CAPACITY_RATIO = 1.05
        key = jax.random.key(seed)
        k0, k1, k2, k3 = jax.random.split(key, 4)
        x = jax.random.normal(k0, (B, S, D), jnp.float32)
        Wg = jax.random.normal(k1, (D, E), jnp.float32) * 0.02
        W1 = jax.random.normal(k2, (E, D, H), jnp.float32) * 0.02
        b1 = jnp.zeros((E, H), jnp.float32)
        W2 = jax.random.normal(k3, (E, H, D), jnp.float32) * 0.02
        b2 = jnp.zeros((E, D), jnp.float32)
        return {'x': x, 'Wg': Wg, 'W1': W1, 'b1': b1, 'W2': W2, 'b2': b2}
    _L0_ffn_in = _L0_ffn_setup()

    def _L1_attn_setup():
        import jax, jax.numpy as jnp
        import numpy as np
        B, L, D, H = (4, 1024, 256, 16)
        Dh = D // H
        DECAY_INIT, DECAY_RANGE = (5.0, 1.0)
        LN_EPS = 1e-05

        def _retention_scan(v, lam):
            a = jnp.broadcast_to(lam[None, None, :, None], v.shape)

            def combine(c1, c2):
                a1, b1 = c1
                a2, b2 = c2
                return (a1 * a2, a2 * b1 + b2)
            _, s = jax.lax.associative_scan(combine, (a, v), axis=1)
            return s

        def _layernorm(x, gamma, beta):
            mu = jnp.mean(x, axis=-1, keepdims=True)
            var = jnp.mean(jnp.square(x - mu), axis=-1, keepdims=True)
            return (x - mu) * jax.lax.rsqrt(var + LN_EPS) * gamma + beta
        key = jax.random.key(seed)
        ks = jax.random.split(key, 5)
        s = 1.0 / np.sqrt(D)
        x = jax.random.normal(ks[0], (B, L, D), dtype=jnp.float32)
        Wq = jax.random.normal(ks[1], (D, D), dtype=jnp.float32) * s
        Wv = jax.random.normal(ks[2], (D, D), dtype=jnp.float32) * s
        Wo = jax.random.normal(ks[3], (D, D), dtype=jnp.float32) * s
        Wg = jax.random.normal(ks[4], (D, D), dtype=jnp.float32) * s
        beta = DECAY_INIT + DECAY_RANGE * (jnp.arange(H, dtype=jnp.float32) / H)
        ln_gamma = jnp.ones((D,), dtype=jnp.float32)
        ln_beta = jnp.zeros((D,), dtype=jnp.float32)
        return {'x': x, 'Wq': Wq, 'Wv': Wv, 'Wo': Wo, 'Wg': Wg, 'beta': beta, 'ln_gamma': ln_gamma, 'ln_beta': ln_beta}
    _L1_attn_in = _L1_attn_setup()

    def _L1_ffn_setup():
        import jax, jax.numpy as jnp
        import numpy as np
        DIM = 256
        HIDDEN = 768
        SCALE = 1.0 / 127.0

        def _dequant(w_int, dtype):
            return w_int.astype(dtype) * jnp.asarray(SCALE, dtype)
        key = jax.random.key(seed)
        k_x, k_g, k_u, k_d = jax.random.split(key, 4)
        x = jax.random.normal(k_x, (4, 512, DIM), dtype=jnp.float32)
        w_gate = jax.random.randint(k_g, (HIDDEN, DIM), -127, 128, dtype=jnp.int32)
        w_up = jax.random.randint(k_u, (HIDDEN, DIM), -127, 128, dtype=jnp.int32)
        w_down = jax.random.randint(k_d, (DIM, HIDDEN), -127, 128, dtype=jnp.int32)
        return {'x': x, 'w_gate': w_gate, 'w_up': w_up, 'w_down': w_down}
    _L1_ffn_in = _L1_ffn_setup()
    _d = {'L0_attn_x': _L0_attn_in['x'], 'L0_attn_Wq': _L0_attn_in['Wq'], 'L0_attn_bq': _L0_attn_in['bq'], 'L0_attn_Wk': _L0_attn_in['Wk'], 'L0_attn_bk': _L0_attn_in['bk'], 'L0_attn_Wv': _L0_attn_in['Wv'], 'L0_attn_bv': _L0_attn_in['bv'], 'L0_attn_Wo': _L0_attn_in['Wo'], 'L0_attn_bo': _L0_attn_in['bo'], 'L0_ffn_Wg': _L0_ffn_in['Wg'], 'L0_ffn_W1': _L0_ffn_in['W1'], 'L0_ffn_b1': _L0_ffn_in['b1'], 'L0_ffn_W2': _L0_ffn_in['W2'], 'L0_ffn_b2': _L0_ffn_in['b2'], 'L1_attn_Wq': _L1_attn_in['Wq'], 'L1_attn_Wv': _L1_attn_in['Wv'], 'L1_attn_Wo': _L1_attn_in['Wo'], 'L1_attn_Wg': _L1_attn_in['Wg'], 'L1_attn_beta': _L1_attn_in['beta'], 'L1_attn_ln_gamma': _L1_attn_in['ln_gamma'], 'L1_attn_ln_beta': _L1_attn_in['ln_beta'], 'L1_ffn_w_gate': _L1_ffn_in['w_gate'], 'L1_ffn_w_up': _L1_ffn_in['w_up'], 'L1_ffn_w_down': _L1_ffn_in['w_down']}
    _x0 = _d['L0_attn_x']
    _d['L0_attn_x'] = jax.random.normal(jax.random.fold_in(jax.random.key(seed), 1), (8, 1024, 256), dtype=_x0.dtype)
    del _x0
    return _d

def reference(L0_attn_x, L0_attn_Wq, L0_attn_bq, L0_attn_Wk, L0_attn_bk, L0_attn_Wv, L0_attn_bv, L0_attn_Wo, L0_attn_bo, L0_ffn_Wg, L0_ffn_W1, L0_ffn_b1, L0_ffn_W2, L0_ffn_b2, L1_attn_Wq, L1_attn_Wv, L1_attn_Wo, L1_attn_Wg, L1_attn_beta, L1_attn_ln_gamma, L1_attn_ln_beta, L1_ffn_w_gate, L1_ffn_w_up, L1_ffn_w_down):

    def _L0_attn_ref(x, Wq, bq, Wk, bk, Wv, bv, Wo, bo):
        import jax, jax.numpy as jnp
        import numpy as np
        import math
        DIM = 256
        NUM_HEADS = 16
        HEAD_DIM = DIM // NUM_HEADS
        B, S = (2, 512)
        b, s, d = x.shape
        h, hd = (NUM_HEADS, HEAD_DIM)

        def split_heads(t):
            return t.reshape(b, s, h, hd).transpose(0, 2, 1, 3)
        q = split_heads(x @ Wq + bq)
        k = split_heads(x @ Wk + bk)
        v = split_heads(x @ Wv + bv)
        scores = jnp.einsum('bhqd,bhkd->bhqk', q, k) / math.sqrt(hd)
        causal = jnp.tril(jnp.ones((s, s), dtype=bool))
        scores = jnp.where(causal[None, None], scores, jnp.asarray(-10000.0, scores.dtype))
        probs = jax.nn.softmax(scores, axis=-1)
        ctx = jnp.einsum('bhqk,bhkd->bhqd', probs, v)
        ctx = ctx.transpose(0, 2, 1, 3).reshape(b, s, d)
        return ctx @ Wo + bo

    def _L0_ffn_ref(x, Wg, W1, b1, W2, b2):
        import math
        import jax, jax.numpy as jnp
        import numpy as np
        B, S, D, H, E, K = (4, 512, 256, 1024, 8, 2)
        CAPACITY_RATIO = 1.05
        b, s, d = x.shape
        e = Wg.shape[1]
        n = b * s
        cap = int(math.ceil(n * K / e * CAPACITY_RATIO))
        xf = x.reshape(n, d)
        probs = jax.nn.softmax(xf @ Wg, axis=-1)
        topv, topi = jax.lax.top_k(probs, K)
        gates = topv / jnp.sum(topv, axis=-1, keepdims=True)
        eidx = topi.reshape(-1)
        oh = jax.nn.one_hot(eidx, e, dtype=jnp.int32)
        pos = jnp.sum(jnp.cumsum(oh, axis=0) * oh, axis=-1) - 1
        keep = pos < cap
        dest = jnp.where(keep, eidx * cap + pos, e * cap)
        xr = jnp.repeat(xf, K, axis=0)
        buf = jnp.zeros((e * cap + 1, d), x.dtype).at[dest].set(xr)
        expert_in = buf[:e * cap].reshape(e, cap, d)
        h = jax.nn.gelu(jnp.einsum('ecd,edh->ech', expert_in, W1) + b1[:, None, :])
        y = jnp.einsum('ech,ehd->ecd', h, W2) + b2[:, None, :]
        yf = jnp.concatenate([y.reshape(e * cap, d), jnp.zeros((1, d), y.dtype)], axis=0)
        gathered = yf[dest]
        w = (gates.reshape(-1) * keep.astype(gates.dtype))[:, None]
        out = (gathered * w).reshape(n, K, d).sum(axis=1).reshape(b, s, d)
        return out

    def _L1_attn_ref(x, Wq, Wv, Wo, Wg, beta, ln_gamma, ln_beta):
        import jax, jax.numpy as jnp
        import numpy as np
        B, L, D, H = (4, 1024, 256, 16)
        Dh = D // H
        DECAY_INIT, DECAY_RANGE = (5.0, 1.0)
        LN_EPS = 1e-05

        def _retention_scan(v, lam):
            a = jnp.broadcast_to(lam[None, None, :, None], v.shape)

            def combine(c1, c2):
                a1, b1 = c1
                a2, b2 = c2
                return (a1 * a2, a2 * b1 + b2)
            _, s = jax.lax.associative_scan(combine, (a, v), axis=1)
            return s

        def _layernorm(x, gamma, beta):
            mu = jnp.mean(x, axis=-1, keepdims=True)
            var = jnp.mean(jnp.square(x - mu), axis=-1, keepdims=True)
            return (x - mu) * jax.lax.rsqrt(var + LN_EPS) * gamma + beta
        b, l, d = x.shape
        tiny = jnp.finfo(jnp.float32).tiny
        lam = jnp.clip(1.0 - jnp.exp2(-beta), tiny, 1.0 - 1e-09)
        q = (x @ Wq.T).reshape(b, l, H, Dh)
        v = (x @ Wv.T).reshape(b, l, H, Dh)
        state = _retention_scan(v, lam)
        ret = (q * state).reshape(b, l, d)
        y = _layernorm(ret, ln_gamma, ln_beta)
        g = jax.nn.silu(x @ Wg.T)
        out = y * g @ Wo.T
        return out

    def _L1_ffn_ref(x, w_gate, w_up, w_down):
        import jax, jax.numpy as jnp
        import numpy as np
        DIM = 256
        HIDDEN = 768
        SCALE = 1.0 / 127.0

        def _dequant(w_int, dtype):
            return w_int.astype(dtype) * jnp.asarray(SCALE, dtype)
        wg = _dequant(w_gate, x.dtype)
        wu = _dequant(w_up, x.dtype)
        wd = _dequant(w_down, x.dtype)
        gate = jnp.einsum('bsd,hd->bsh', x, wg)
        up = jnp.einsum('bsd,hd->bsh', x, wu)
        h = jax.nn.silu(gate) * up
        return jnp.einsum('bsh,dh->bsd', h, wd)
    x = L0_attn_x
    x = _layernorm(x + _L0_attn_ref(x, L0_attn_Wq, L0_attn_bq, L0_attn_Wk, L0_attn_bk, L0_attn_Wv, L0_attn_bv, L0_attn_Wo, L0_attn_bo), axis=-1)
    x = _layernorm(x + _L0_ffn_ref(x, L0_ffn_Wg, L0_ffn_W1, L0_ffn_b1, L0_ffn_W2, L0_ffn_b2), axis=-1)
    x = _layernorm(x + _L1_attn_ref(x, L1_attn_Wq, L1_attn_Wv, L1_attn_Wo, L1_attn_Wg, L1_attn_beta, L1_attn_ln_gamma, L1_attn_ln_beta), axis=-1)
    x = _layernorm(x + _L1_ffn_ref(x, L1_ffn_w_gate, L1_ffn_w_up, L1_ffn_w_down), axis=-1)
    return x

_drawn_inputs = setup_inputs


def setup_inputs(seed=0):
    import zlib

    import numpy as np

    out = dict(_drawn_inputs(seed))
    spreads = {'L0_ffn_b1': (0.0, 0.1),
     'L0_ffn_b2': (0.0, 0.1),
     'L1_attn_ln_gamma': (1.0, 0.2),
     'L1_attn_ln_beta': (0.0, 0.1)}
    factors = {'L0_attn_Wq': 8.0, 'L0_attn_bq': 8.0, 'L0_attn_Wk': 8.0, 'L0_attn_bk': 8.0}
    for name, (base, spread) in spreads.items():
        noise = np.random.default_rng([zlib.crc32(name.encode()), seed]).standard_normal(out[name].shape)
        drawn = base * np.exp(spread * noise) if base else spread * noise
        out[name] = jnp.asarray(drawn.astype(out[name].dtype))
    for name, factor in factors.items():
        out[name] = (out[name] * factor).astype(out[name].dtype)
    return out
```

```python
from contextlib import ExitStack

import numpy as np

import concourse.bass as bass
from concourse import mybir

F32 = mybir.dt.float32
F32R = mybir.dt.float32r
BF16 = mybir.dt.bfloat16
I32 = mybir.dt.int32
U32 = mybir.dt.uint32
ALU = mybir.AluOpType
ACT = mybir.ActivationFunctionType
AX_X = mybir.AxisListType.X

P = 128
NB, S, D = 8, 1024, 256
NH, HD = 16, 16
KC = D // P
NT = S // P
HALF = 512
UH = NH // 2
GH = 4
VS = HD + 1
VW = (NH - 1) * VS + 32
NE, TOPK = 8, 2
CAP = 2151
SLOTS = 2160
EPS = 1e-5
HUGE = 1.0e30

Q_PARTS = (0, 0, 1, 0, 2, 1)
K_PARTS = (0, 1, 0, 2, 0, 1)
NSTACK = len(Q_PARTS) * HD
NROWS = NSTACK + 3

STEPS = 24


def step_block(s):
    grp, r = divmod(s, 12)
    c = 0 if r < 4 else 1
    kb = r if r < 4 else r - 4
    return grp, c, kb, max(0, kb - 4 * c) * P, kb == 4 * c + 3


def max_tiles():
    tiles = [(t, 0, (t + 1) * P, t) for t in range(4)]
    tiles += [(t, 0, HALF, t) for t in range(4, 8)]
    tiles += [(t, HALF, (t - 3) * P, t + 4) for t in range(4, 8)]
    return tiles


MAX_TILES = max_tiles()
GROUP_TILES = [(h, tile) for h in range(GH) for tile in MAX_TILES]

PER_SEQ = {"qk": 8, "v": 4, "g": 8, "m": 4, "ct": 4, "wo": 4, "xt": 4, "lg": 1, "pf": 1}


G_OPS, M_OPS, WO_OPS, LG_OPS, PF_OPS = 2, 5, 5, 14, 28


def spread(n, steps):
    out, at = {}, 0
    for i, s in enumerate(steps):
        k = n * (i + 1) // len(steps)
        out[s] = (at, k)
        at = k
    return out


TILES_THIS = spread(48, range(0, 7))
TILES_NEXT = spread(48, range(10, 19))


def items_of(g, first, last):
    it = {}

    def put(step, place, kind, const, *what):
        it.setdefault((step, place), []).append((kind, const) + what)

    nxt = not (last and g == 1)
    db, g2 = (0, 1) if g == 0 else (1, 0)
    if nxt:
        for j, (s, pl) in enumerate(((0, 0), (0, 1), (1, 1), (2, 0))):
            put(s, pl, "qk", 8 * db + 4 * g2 + j, db, g2, j)
    if not (first and g == 0):
        put(1, 0, "g", 4 * g - 1, 1 - g, 1, 1)
    put(5, 0, "g", 4 * g, g, 0, 0)
    put(13, 0, "g", 4 * g + 1, g, 0, 1)
    put(17, 0, "g", 4 * g + 2, g, 1, 0)
    put(8, 0, "m", 2 * g + 1, 0, g, 1)
    if nxt:
        put(20, 0, "m", 4 * db + 2 * g2, db, g2, 0)
    if g == 1 and not last:
        for j, s in enumerate((6, 7, 9, 10)):
            put(s, 1, "v", 4 + j, j)
    if g == 0 and not first:
        for j, (s, pl) in enumerate(((2, 1), (3, 0), (3, 1), (4, 0))):
            put(s, pl, "ct", j - 4, j)
        for j, (s, pl) in enumerate(((5, 1), (6, 0), (6, 1), (7, 0))):
            put(s, pl, "wo", j - 4, j)
        for j, (s, pl) in enumerate(((11, 0), (11, 1), (12, 0), (12, 1))):
            put(s, pl, "xt", j - 4, j)
        put(14, 0, "lg", -1)
        put(18, 0, "pf", -1)
    return it


TAIL = ([("g", 7, 1, 1, 1)] + [("ct", j + 0, j) for j in range(4)] + [("wo", j, j) for j in range(4)]
        + [("xt", j, j) for j in range(4)] + [("lg", 0), ("pf", 0)])
HEAD = ([("qk", j, 0, 0, j) for j in range(4)] + [("v", j, j) for j in range(4)])


def count(b, per_seq, const):
    return b * per_seq + const


def wait_apart(eng, semaphore, value):
    if not isinstance(value, int):
        value = eng.to_reg(value)
        eng.wait_ge(semaphore, 1)
    eng.wait_ge(semaphore, value)


def phase_attention(nc, T):
    with ExitStack() as ctx:
        def sb(name, shape, dt=F32):
            return ctx.enter_context(nc.sbuf_tensor("a_" + name, shape, dt))

        def sem(name):
            return ctx.enter_context(nc.semaphore("a_" + name))

        cf = sb("cf", [P, 4 * P + 64])
        identF = cf[:, 0:P]
        cb = sb("cb", [P, 5 * P], BF16)
        identB, maskK, maskQ, before, onesB = (cb[:, i * P:(i + 1) * P] for i in range(5))
        desc = cf[:, 4 * P:4 * P + 64]
        wq, wk, wv, wo = (sb(n, [P, KC, D]) for n in ("wq", "wk", "wv", "wo"))
        wg = sb("wg", [P, KC, NE])
        bqk = sb("bqk", [P, 2, KC])
        bqk_in = sb("bqk_in", [P, 2, KC])
        bv = sb("bv", [P, D])
        bo = sb("bo", [P, D])
        xT = sb("xT", [P, KC, S])
        qk_stack = [[sb(f"stack{s}{t}", [NROWS, UH, S], BF16) for t in range(2)] for s in range(2)]
        v_now = sb("v_now", [P, NT, VW])
        v_next = sb("v_next", [P, NT, VW])
        probs = [sb(f"probs{i}", [P, GH, HALF]) for i in range(2)]
        qf = [sb(f"qf{i}", [P, HALF]) for i in range(2)]
        parts = [sb(f"parts{i}", [P, 3, HALF], BF16) for i in range(2)]
        rest = [sb(f"rest{i}", [P, HALF]) for i in range(2)]
        pmax = sb("pmax", [P, 2, GH, 12])
        mcol = sb("mcol", [P, P])
        nmax = sb("nmax", [32, P])
        nrest = sb("nrest", [32, P])
        nparts = sb("nparts", [32, 3, P], BF16)
        ctx_raw = sb("ctx_raw", [P, HALF])
        rden = sb("rden", [P, 4, GH])
        ctxn = sb("ctxn", [P, NT, D])
        actT = sb("actT", [P, KC, S])
        xb = sb("xb", [P, NT, D])
        x1 = sb("x1", [P, NT, D])
        stats = sb("stats", [P, NT, 6])
        mv = sb("mv", [P, NT, 2])
        vare = sb("vare", [P, NT])
        mhalf = sb("mhalf", [P, NT])
        rstd = sb("rstd", [P, NT])
        zeros = sb("zeros", [P, 2304])
        lg = sb("lg", [P, NT, NE])
        lg2 = sb("lg2", [P, NT, NE])
        sel = sb("sel", [P, NT, NE])
        oh = [sb(f"oh{k}", [P, NT, NE]) for k in range(2)]
        ohb = sb("ohb", [P, NT, NE], BF16)
        top = sb("top", [P, NT, 2])
        pick = sb("pick", [P, NT, 2])
        dlt = sb("dlt", [P, NT])
        expd = sb("expd", [P, NT])
        den = sb("den", [P, NT])
        gates = sb("gates", [P, NT, 2])
        tot = sb("tot", [P, NT, NE])
        base = sb("base", [P, NT + 1, NE])
        pos = sb("pos", [P, NT, NE])
        posk = sb("posk", [P, NT, 2])
        keep = sb("keep", [P, NT, 2])
        drop = sb("drop", [P, NT, 2])
        dest = sb("dest", [P, NT, 2])
        dst_s = sb("dst_s", [P, NT, 2])
        dst_g = sb("dst_g", [P, NT, 2])
        idx_s = sb("idx_s", [P, NT, 2], I32)
        idx_g = sb("idx_g", [P, NT, 2], I32)

        st = ctx.enter_context(nc.psum_tensor("a_st", [P, 4, HALF], F32))
        pv = ctx.enter_context(nc.psum_tensor("a_pv", [P, HALF], F32))
        mx = ctx.enter_context(nc.psum_tensor("a_mx", [P, 2, HALF], F32))
        misc = ctx.enter_context(nc.psum_tensor("a_misc", [P, HALF], F32))

        consts_in = sem("consts_in")
        consts_ready = sem("consts_ready")
        biases_ready = sem("biases_ready")
        ones_ready = sem("ones_ready")
        xT_in = sem("xT_in")
        x_in = sem("x_in")
        xb_ready = sem("xb_ready")
        ready = {k: sem(k + "_ready") for k in PER_SEQ}
        act_took = {k: sem(k + "_copied") for k in ("qk", "ct", "xt")}
        v_taken = sem("v_taken")
        qf_ready = sem("qf_ready")
        split_seq = sem("split_seq")
        parts_out = [sem(f"parts_out{i}") for i in range(2)]
        stack_in = sem("stack_in")
        v_switched = sem("v_switched")
        st_ready = sem("st_ready")
        probs_ready = sem("probs_ready")
        pv_done = sem("pv_done")
        mx_ready = sem("mx_ready")
        mx_done = sem("mx_done")
        mcol_seq = sem("mcol_seq")
        m_seq = sem("m_seq")
        mrow_out = sem("mrow_out")
        mrow_in = sem("mrow_in")
        raw_ready = sem("raw_ready")
        g_seq = sem("g_seq")
        wo_seq = sem("wo_seq")
        ve_ready = sem("ve_ready")
        rstd_ready = sem("rstd_ready")
        x1_ready = sem("x1_ready")
        x1_out = sem("x1_out")
        lg_seq = sem("lg_seq")
        pf_seq = sem("pf_seq")
        expd_ready = sem("expd_ready")
        scat = sem("scat")
        route_out = sem("route_out")
        zero_ready = sem("zero_ready")
        cleared = sem("cleared")
        zero_out = sem("zero_out")

        N_CONST = 10
        N_ZERO = 15 + 1
        STACK_DMAS = 4 * 6
        taken = {"qk": (act_took["qk"], 1, 1), "ct": (act_took["ct"], 1, 1), "xt": (act_took["xt"], 1, 1),
                 "v": (v_taken, 1, 1), "g": (g_seq, G_OPS, G_OPS), "m": (m_seq, M_OPS, 1),
                 "wo": (wo_seq, WO_OPS, 1), "lg": (lg_seq, LG_OPS, 1), "pf": (pf_seq, PF_OPS, 11)}

        block = ctx.enter_context(nc.Block())

        @block.sync
        def _(sp):
            sp.dma_start(xT[:], T["xT"][0].rearrange("(k p) n -> p k n", p=P)).then_inc(xT_in, 16)
            for dst, src in ((cf[:], T["consts"]), (bqk_in[:], T["bqk"]), (bv[:], T["bv"]), (bo[:], T["bo"]),
                             (wq[:], T["wq"].rearrange("(k p) n -> p k n", p=P)),
                             (wk[:], T["wk"].rearrange("(k p) n -> p k n", p=P)),
                             (wv[:], T["wv"].rearrange("(k p) n -> p k n", p=P)),
                             (wo[:], T["wo"].rearrange("(k p) n -> p k n", p=P)),
                             (wg[:], T["wg"].rearrange("(k p) n -> p k n", p=P))):
                sp.dma_start(dst, src).then_inc(consts_in, 16)

            def parts_write(b, const, j, g2):
                t, n = j % 2, j // 2
                wait_apart(sp, split_seq, count(b, 3 * 8, 3 * (const + 1)))
                sp.dma_start(T["qk_scr"][g2, j].rearrange("r p n -> p r n"), parts[const % 2][:]).then_inc(parts_out[const % 2], 16)

            def stack_read(b, const, j, g2):
                t, n = j % 2, j // 2
                wait_apart(sp, parts_out[const % 2], count(b, 16 * 4, 16 * (const // 2 + 1)))
                for r, part in enumerate((Q_PARTS, K_PARTS)[t]):
                    sp.dma_start(qk_stack[g2][t][r * HD:(r + 1) * HD, :, n * HALF:(n + 1) * HALF],
                                 T["qk_scr"][g2, j, part].rearrange("(i d) n -> d i n", d=HD)).then_inc(stack_in, 16)

            def m_rows(b, const, g2, grp):
                wait_apart(sp, m_seq, count(b, M_OPS * 4, M_OPS * (const + 1)))
                sp.dma_start(T["m_scr"][g2, grp].rearrange("r (a n) -> a r n", a=32), nparts[:]).then_inc(mrow_out, 16)
                wait_apart(sp, mrow_out, count(b, 16 * 4, 16 * (const + 1)))
                sp.dma_start(qk_stack[g2][0][NSTACK:NROWS, grp * GH:(grp + 1) * GH, :],
                             T["m_scr"][g2, grp].rearrange("r (h n) -> r h n", h=GH)).then_inc(mrow_in, 16)

            def stores(b, kind, const):
                if kind == "xt0":
                    wait_apart(sp, x1_ready, b + const + 1)
                    sp.dma_start(T["x1"][b + const].rearrange("(t p) d -> p t d", p=P), x1[:]).then_inc(x1_out, 16)
                if kind == "pf":
                    wait_apart(sp, pf_seq, count(b, PF_OPS, PF_OPS * (const + 1)))
                    sp.dma_start(T["gates"][b + const], gates[:]).then_inc(route_out, 16)
                    sp.dma_start(T["dest"][b + const], idx_g[:]).then_inc(route_out, 16)

            pend = []

            def qk_io(b, item):
                kind, const, db, g2, j = item
                if j == 0:
                    pass
                parts_write(b, const, j, g2)
                if pend:
                    stack_read(*pend.pop())
                pend.append((b, const, j, g2))

            def flush():
                if pend:
                    stack_read(*pend.pop())

            def body(b, first, last):
                for g in range(2):
                    items = items_of(g, first, last)
                    for s in range(STEPS):
                        if s == 0 and not (first and g == 0):
                            wait_apart(sp, pv_done, count(b, 48, 24 * g))
                        for pl in (0, 1):
                            for it in items.get((s, pl), []):
                                if it[0] == "qk":
                                    qk_io(b, it)
                                    if it[4] == 3:
                                        flush()
                                if it[0] == "m":
                                    m_rows(b, it[1], it[3], it[4])
                                if it[0] == "xt" and it[2] == 0:
                                    stores(b, "xt0", -1)
                                if it[0] == "pf":
                                    stores(b, "pf", -1)
                        if g == 0 and s == 4 and not last:
                            wait_apart(sp, ready["qk"], count(b, 8, 8))
                            sp.dma_start(xT[:], T["xT"][b + 1].rearrange("(k p) n -> p k n", p=P)).then_inc(xT_in, 16)
                        if g == 1 and s == 0:
                            if not first:
                                wait_apart(sp, wo_seq, count(b, WO_OPS * 4, 0))
                                wait_apart(sp, x1_out, count(b, 16, 0))
                                wait_apart(sp, route_out, count(b, 32, 0))
                            sp.dma_start(xb[:], T["x"][b].rearrange("(t p) d -> p t d", p=P)).then_inc(x_in, 16)

            for it in HEAD:
                if it[0] == "qk":
                    qk_io(0, it)
            flush()
            m_rows(0, 0, 0, 0)
            body(0, True, False)
            with sp.Fori(1, NB - 1) as b:
                body(b, False, False)
            body(NB - 1, False, True)
            stores(NB - 1, "xt0", 0)
            stores(NB - 1, "pf", 0)
            wait_apart(sp, x1_out, 16 * NB)
            wait_apart(sp, route_out, 32 * NB)
            wait_apart(sp, scat, 16 * 16 * NB)
            wait_apart(sp, zero_out, 16 * N_ZERO)

        @block.tensor
        def _(pe):
            last_item = [None]

            def mm(out, a, bb, start, stop):
                return pe.matmul(out, a, bb, start=start, stop=stop, skip_group_check=True)

            def item(b, it):
                kind, const = it[0], it[1]
                if last_item[0] is not None:
                    k0, c0 = last_item[0]
                    read, per, nth = taken[k0]
                    pe.wait_ge(read, count(b, per * PER_SEQ[k0], per * c0 + nth))
                last_item[0] = (kind, const)
                if kind == "qk":
                    _, _, db, g2, j = it
                    t, n = j % 2, j // 2
                    if j == 0:
                        pe.wait_ge(xT_in, count(b, 16, 16 * (db + 1)))
                    w = (wq, wk)[t]
                    for k in range(KC):
                        m = mm(misc[:], w[:, k, g2 * P:(g2 + 1) * P], xT[:, k, n * HALF:(n + 1) * HALF], k == 0, k == KC - 1)
                elif kind == "v":
                    j = it[2]
                    for u in range(2):
                        t = 2 * j + u
                        for k in range(KC):
                            m = mm(misc[:, u * D:(u + 1) * D], xT[:, k, t * P:(t + 1) * P], wv[:, k, :], k == 0, k == KC - 1)
                elif kind == "g":
                    pe.wait_ge(raw_ready, count(b, 8, const + 1))
                    for q in range(4):
                        m = pe.transpose(misc[:, q * P:(q + 1) * P], ctx_raw[:, q * P:(q + 1) * P], identF)
                elif kind == "m":
                    pe.wait_ge(mcol_seq, count(b, 2 * 4, 2 * (const + 1)))
                    m = pe.transpose(misc[:, 0:P], mcol[:], identF)
                elif kind == "ct":
                    j = it[2]
                    pe.wait_ge(g_seq, count(b, 8 * G_OPS, 8 * G_OPS * ((const - j) // 4 + 1)))
                    for q in range(4):
                        m = pe.transpose(misc[:, q * P:(q + 1) * P], ctxn[:, 4 * (j // 2) + q, (j % 2) * P:(j % 2 + 1) * P], identF)
                elif kind == "wo":
                    j = it[2]
                    pe.wait_ge(act_took["ct"], count(b, 4, const - j + 2 * (j // 2) + 2))
                    for u in range(2):
                        t = 2 * j + u
                        for k in range(KC):
                            m = mm(misc[:, u * D:(u + 1) * D], actT[:, k, t * P:(t + 1) * P], wo[:, k, :], k == 0, k == KC - 1)
                elif kind == "xt":
                    j = it[2]
                    pe.wait_ge(x1_ready, count(b, 1, (const - j) // 4 + 1))
                    for q in range(4):
                        m = pe.transpose(misc[:, q * P:(q + 1) * P], x1[:, 4 * (j // 2) + q, (j % 2) * P:(j % 2 + 1) * P], identF)
                elif kind == "lg":
                    pe.wait_ge(act_took["xt"], count(b, 4, 4 * const + 4))
                    for t in range(NT):
                        for k in range(KC):
                            m = mm(misc[:, t * NE:(t + 1) * NE], actT[:, k, t * P:(t + 1) * P], wg[:, k, :], k == 0, k == KC - 1)
                elif kind == "pf":
                    pe.wait_ge(lg_seq, count(b, LG_OPS, LG_OPS * (const + 1)))
                    mm(misc[:, 0:64], before, ohb[:].rearrange("p t e -> p (t e)"), True, True)
                    m = mm(misc[:, 64:128], onesB, ohb[:].rearrange("p t e -> p (t e)"), True, True)
                m.then_inc(ready[kind], 1)

            def tiles(b, db, g2, grp, lo, hi):
                for k in range(lo, hi):
                    h, (t, k0, w, col) = GROUP_TILES[k]
                    i = grp * GH + h
                    idx = 192 * db + 96 * g2 + 48 * grp + k
                    if k == 0 and grp == 0:
                        pe.wait_ge(stack_in, count(b, 2 * 16 * STACK_DMAS, 16 * STACK_DMAS * (2 * db + g2 + 1)))
                    if idx >= 2 or not isinstance(b, int) or b > 0:
                        pe.wait_ge(mx_done, count(b, 192, idx - 1))
                    bank = mx[:, idx % 2, 0:w]
                    q, kk = qk_stack[g2]
                    mm(bank, q[0:NSTACK, i, t * P:(t + 1) * P], kk[0:NSTACK, i, k0:k0 + w], True, False) \
                        if k0 + w == (t + 1) * P else \
                        mm(bank, q[0:NSTACK, i, t * P:(t + 1) * P], kk[0:NSTACK, i, k0:k0 + w], True, True).then_inc(mx_ready, 1)
                    if k0 + w == (t + 1) * P:
                        mm(mx[:, idx % 2, w - P:w], identB, maskK, False, True).then_inc(mx_ready, 1)

            def scores(b, g, s, p, n0):
                grp, c, kb, off, _ = step_block(s)
                if p == 0 and s % 12 == 0:
                    pe.wait_ge(mrow_in, count(b, 16 * 4, 16 * (2 * g + grp + 1)))
                if n0 >= 0:
                    pe.wait_ge(probs_ready, count(b, 96, 2 * (24 * g + s - 1) + p + 1))
                q, kk = qk_stack[g]
                for h in range(2):
                    i = grp * GH + 2 * p + h
                    diag = kb >= 4 * c
                    m = mm(st[:, 2 * p + h, off:HALF], kk[0:NROWS, i, kb * P:(kb + 1) * P],
                           q[0:NROWS, i, c * HALF + off:(c + 1) * HALF], True, not diag)
                    if diag:
                        m = mm(st[:, 2 * p + h, off:off + P], identB, maskQ, False, True)
                m.then_inc(st_ready, 1)

            def values(b, g, s, rel):
                grp, c, kb, off, is_last = step_block(s)
                if kb == 0:
                    done = 4 * g + 2 * grp + c + (8 * (rel // 48))
                    if not (isinstance(b, int) and b == 0 and done == 0):
                        pe.wait_ge(raw_ready, count(b, 8, done))
                pe.wait_ge(probs_ready, count(b, 96, 2 * rel + 2))
                for h in range(GH):
                    head = g * UH + grp * GH + h
                    m = pe.matmul(pv[32 * h:32 * h + 32, off:HALF], v_now[:, kb, head * VS:head * VS + 32],
                                  probs[rel % 2][:, h, off:HALF], start=kb == 0, stop=is_last, skip_group_check=True)
                m.then_inc(pv_done, 1)

            def body(b, first, last):
                if last_item[0] is not None:
                    k0, c0 = last_item[0]
                    last_item[0] = (k0, c0 - PER_SEQ[k0])
                for g in range(2):
                    items = items_of(g, first, last)
                    for s in range(STEPS):
                        n = 24 * g + s
                        ms = []
                        if s in TILES_THIS:
                            ms = [(0, g, 1, k) for k in range(*TILES_THIS[s])]
                        if s in TILES_NEXT and not (last and g == 1):
                            ms = [(0 if g == 0 else 1, 1 - g, 0, k) for k in range(*TILES_NEXT[s])]
                        cut = [len(ms) * q // 3 for q in range(4)]
                        scores(b, g, s, 0, -1 if first and n == 0 else 0)
                        for m in ms[cut[0]:cut[1]]:
                            tiles(b, m[0], m[1], m[2], m[3], m[3] + 1)
                        scores(b, g, s, 1, -1 if first and n == 0 else 0)
                        for it in items.get((s, 0), []):
                            item(b, it)
                        for m in ms[cut[1]:cut[2]]:
                            tiles(b, m[0], m[1], m[2], m[3], m[3] + 1)
                        if n == 1:
                            pe.wait_ge(v_switched, count(b, 1, 1))
                        if n > 0:
                            values(b, (n - 1) // 24, (n - 1) % 24, n - 1)
                        elif not first:
                            values(b, 1, 23, -1)
                        for it in items.get((s, 1), []):
                            item(b, it)
                        for m in ms[cut[2]:cut[3]]:
                            tiles(b, m[0], m[1], m[2], m[3], m[3] + 1)

            pe.wait_ge(consts_in, 16 * 9)
            pe.wait_ge(consts_ready, 1)
            for it in HEAD:
                item(0, it)
            pe.wait_ge(ones_ready, 2)
            tiles(0, 0, 0, 0, 0, 48)
            item(0, ("m", 0, 0, 0, 0))
            last_item[0] = ("m", 0 + PER_SEQ["m"])
            body(0, True, False)
            with pe.Fori(1, NB - 1) as b:
                body(b, False, False)
            body(NB - 1, False, True)
            values(NB - 1, 1, 23, 47)
            for it in TAIL:
                item(NB - 1, it)

        @block.scalar
        def _(act):
            act.wait_ge(consts_in, 16 * 9)
            nc.scalar.activation(bqk[:, 0, :], bqk_in[:, 0, :], ACT.Copy, scale=0.25).then_inc(biases_ready, 1)
            nc.scalar.activation(bqk[:, 1, :], bqk_in[:, 1, :], ACT.Copy).then_inc(biases_ready, 1)
            act.wait_ge(biases_ready, 2)

            def exps(b, g, s, p):
                grp, c, kb, off, _ = step_block(s)
                n = 24 * g + s
                act.wait_ge(st_ready, count(b, 96, 2 * n + p + 1))
                if not (isinstance(b, int) and b == 0 and n < 2):
                    act.wait_ge(pv_done, count(b, 48, n - 1))
                nc.scalar.activation(probs[n % 2][:, 2 * p:2 * p + 2, off:HALF], st[:, 2 * p:2 * p + 2, off:HALF],
                                     ACT.Exp).then_inc(probs_ready, 1)

            def item(b, it):
                kind, const = it[0], it[1]
                if kind == "qk":
                    _, _, db, g2, j = it
                    t = j % 2
                    act.wait_ge(ready["qk"], count(b, 8, const + 1))
                    if not (isinstance(b, int) and b == 0 and const < 2):
                        act.wait_ge(split_seq, count(b, 3 * 8, 3 * (const - 1)))
                        act.wait_ge(parts_out[const % 2], count(b, 16 * 4, 16 * (const // 2)))
                    kw = dict(bias=bqk[:, t, g2:g2 + 1], scale=(0.25, 1.0)[t])
                    nc.scalar.activation(qf[const % 2][:], misc[:], ACT.Identity, **kw).then_inc(qf_ready, 1)
                    nc.scalar.activation(parts[const % 2][:, 0, :], misc[:], ACT.Identity, **kw).then_inc(act_took["qk"], 1)
                if kind in ("ct", "xt"):
                    j = it[2]
                    act.wait_ge(ready[kind], count(b, 4, const + 1))
                    nc.scalar.activation(actT[:, j % 2, (j // 2) * HALF:(j // 2 + 1) * HALF], misc[:], ACT.Copy)\
                        .then_inc(act_took[kind], 1)

            def raw(b, rel, const):
                act.wait_ge(pv_done, count(b, 48, rel + 1))
                nc.scalar.activation(ctx_raw[:], pv[:], ACT.Copy).then_inc(raw_ready, 1)

            def router_exp(b, const):
                act.wait_ge(lg_seq, count(b, LG_OPS, LG_OPS * (const + 1)))
                nc.scalar.activation(expd[:], dlt[:], ACT.Exp).then_inc(expd_ready, 1)

            def body(b, first, last):
                for g in range(2):
                    items = items_of(g, first, last)
                    for s in range(STEPS):
                        n = 24 * g + s
                        exps(b, g, s, 0)
                        for it in items.get((s, 0), []):
                            item(b, it)
                        exps(b, g, s, 1)
                        if s in (4, 12, 16):
                            raw(b, n - 1, 4 * g + {4: 0, 12: 1, 16: 2}[s])
                        if s == 0 and not (first and g == 0):
                            raw(b, n - 1, 4 * g - 1)
                        for it in items.get((s, 1), []):
                            item(b, it)
                        if g == 0 and s == 16 and not first:
                            router_exp(b, -1)

            for it in HEAD:
                item(0, it)
            body(0, True, False)
            with act.Fori(1, NB - 1) as b:
                body(b, False, False)
            body(NB - 1, False, True)
            raw(NB - 1, 47, 7)
            for it in TAIL:
                item(NB - 1, it)
                if it[0] == "lg":
                    router_exp(NB - 1, 0)

        @block.gpsimd
        def _(pool):
            for s in range(2):
                nc.gpsimd.memset(qk_stack[s][1][NSTACK:NROWS, :, :], 1.0).then_inc(ones_ready, 1)
                pool.wait_ge(ones_ready, s + 1)
            pool.wait_ge(zero_ready, 1)
            flat = T["buf"].rearrange("(p r) d -> p (r d)", p=P)
            for z in range(15):
                pool.dma_start(flat[:, z * 2304:(z + 1) * 2304], zeros[:]).then_inc(zero_out, 16)
            pool.dma_start(T["y"][NE * SLOTS:NE * SLOTS + 1, :], zeros[0:1, 0:D]).then_inc(zero_out, 16)

            def residual(b):
                pool.wait_ge(x_in, count(b, 16, 16))
                for t in range(NT):
                    ins = nc.gpsimd.tensor_tensor(xb[:, t, :], xb[:, t, :], bo[:], ALU.add)
                ins.then_inc(xb_ready, 1)

            def root(b, const):
                pool.wait_ge(ve_ready, b + const + 1)
                nc.gpsimd.tensor_tensor(rstd[:], vare[:], mhalf[:], ALU.pow).then_inc(rstd_ready, 1)

            def scatter(b, const):
                wait_apart(pool, pf_seq, count(b, PF_OPS, PF_OPS * (const + 1)))
                for t in range(NT):
                    for k in range(TOPK):
                        pool.indirect_dma_start(
                            T["buf"], bass.IndirectOffsetOnAxis(ap=idx_s[:, t, k:k + 1].bitcast(U32), axis=0),
                            x1[:, t, :], None, bounds_check=NE * SLOTS - 1, oob_is_err=False).then_inc(scat, 16)

            pool.wait_ge(ones_ready, 2)
            pool.wait_ge(consts_in, 16 * 9)
            pool.wait_ge(zero_out, 16 * N_ZERO)
            residual(0)
            with pool.Fori(1, NB) as b:
                root(b, -1)
                scatter(b, -1)
                wait_apart(pool, scat, count(b, 256, 0))
                residual(b)
            root(NB - 1, 0)
            scatter(NB - 1, 0)

        @block.vector
        def _(dve):
            V = nc.vector

            class Chain:

                def __init__(self, sem_, per_item):
                    self.sem, self.per = sem_, per_item

                def begin(self, b, kind_per, const):
                    self.b, self.kp, self.c, self.n = b, kind_per, const, 0

                def link(self, ins):
                    self.n += 1
                    ins.then_inc(self.sem, 1)
                    wait_apart(dve, self.sem, count(self.b, self.kp * self.per, self.per * self.c + self.n))

                def end(self, ins):
                    self.n += 1
                    ins.then_inc(self.sem, 1)
                    assert self.n == self.per, (self.n, self.per)

            split = Chain(split_seq, 3)
            msplit = Chain(m_seq, M_OPS)
            gch = Chain(g_seq, G_OPS)
            woch = Chain(wo_seq, WO_OPS)
            lgch = Chain(lg_seq, LG_OPS)
            pfch = Chain(pf_seq, PF_OPS)

            def item(b, it):
                kind, const = it[0], it[1]
                if kind == "qk":
                    i = const % 2
                    dve.wait_ge(qf_ready, count(b, 8, const + 1))
                    dve.wait_ge(act_took["qk"], count(b, 8, const + 1))
                    split.begin(b, 8, const)
                    split.link(V.tensor_tensor(rest[i][:], qf[i][:], parts[i][:, 0, :], ALU.subtract))
                    split.link(V.tensor_copy(parts[i][:, 1, :], rest[i][:]))
                    split.end(V.tensor_tensor(parts[i][:, 2, :], rest[i][:], parts[i][:, 1, :], ALU.subtract))
                elif kind == "v":
                    j = it[2]
                    dve.wait_ge(ready["v"], count(b, 4, const + 1))
                    for u in range(2):
                        t = 2 * j + u
                        ins = V.tensor_tensor(
                            v_next[:, t, 0:NH * VS].rearrange("p (h c) -> p h c", c=VS)[:, :, 0:HD],
                            misc[:, u * D:(u + 1) * D].rearrange("p (h c) -> p h c", c=HD),
                            bv[:].rearrange("p (h c) -> p h c", c=HD), ALU.add)
                    ins.then_inc(v_taken, 1)
                elif kind == "g":
                    _, _, g, grp, c = it
                    dve.wait_ge(ready["g"], count(b, 8, const + 1))
                    if g == 0 and grp == 0 and c == 0 and not (isinstance(b, int) and b == 0):
                        dve.wait_ge(ready["ct"], count(b, 4, 0))
                    gch.begin(b, 8, const)
                    v4 = misc[:].rearrange("p (q h c) -> p q h c", q=4, h=GH)
                    gch.link(V.reciprocal(rden[:], v4[:, :, :, HD]))
                    col = (2 * g + grp) * GH * HD
                    ins = V.tensor_tensor(
                        ctxn[:, 4 * c:4 * c + 4, col:col + GH * HD].rearrange("p q (h c) -> p q h c", h=GH),
                        v4[:, :, :, 0:HD], rden[:].unsqueeze(3).to_broadcast([P, 4, GH, HD]), ALU.mult)
                    gch.end(ins)
                elif kind == "m":
                    _, _, db, g2, grp = it
                    dve.wait_ge(ready["m"], count(b, 4, const + 1))
                    if not (isinstance(b, int) and b == 0 and const == 0):
                        dve.wait_ge(mrow_out, count(b, 64, 16 * const))
                    msplit.begin(b, 4, const)
                    msplit.link(V.tensor_scalar(nmax[:], misc[0:32, 0:P], -1.0, None, ALU.mult))
                    msplit.link(V.tensor_copy(nparts[:, 0, :], nmax[:]))
                    msplit.link(V.tensor_tensor(nrest[:], nmax[:], nparts[:, 0, :], ALU.subtract))
                    msplit.link(V.tensor_copy(nparts[:, 1, :], nrest[:]))
                    msplit.end(V.tensor_tensor(nparts[:, 2, :], nrest[:], nparts[:, 1, :], ALU.subtract))
                elif kind == "wo":
                    j = it[2]
                    dve.wait_ge(ready["wo"], count(b, 4, const + 1))
                    dve.wait_ge(xb_ready, count(b, 1, (const - j) // 4 + 1))
                    woch.begin(b, 4, const)
                    woch.link(V.tensor_tensor(x1[:, 2 * j:2 * j + 2, :], misc[:].rearrange("p (t d) -> p t d", t=2),
                                              xb[:, 2 * j:2 * j + 2, :], ALU.add))
                    for t in (2 * j, 2 * j + 1):
                        woch.link(V.bn_stats(stats[:, t, :], x1[:, t, :]))
                    woch.link(V.bn_aggr(mv[:, 2 * j, :], stats[:, 2 * j, :]))
                    woch.end(V.bn_aggr(mv[:, 2 * j + 1, :], stats[:, 2 * j + 1, :]))
                elif kind == "lg":
                    L = lgch
                    shp = [P, NT, NE]
                    dve.wait_ge(ready["lg"], b + const + 1)
                    lgch.begin(b, 1, const)
                    d3 = desc.rearrange("p (t e) -> p t e", t=NT)
                    L.link(V.tensor_copy(lg[:], misc[:, 0:64].rearrange("p (t e) -> p t e", t=NT)))
                    for k, src in ((0, lg), (1, lg2)):
                        if k:
                            L.link(V.scalar_tensor_tensor(out=lg2[:], in0=oh[0][:], scalar=-3.0e38, in1=lg[:],
                                                          op0=ALU.mult, op1=ALU.add))
                        L.link(V.tensor_reduce(top[:, :, k:k + 1], src[:], AX_X, ALU.max))
                        L.link(V.tensor_tensor(sel[:], src[:], top[:, :, k:k + 1].to_broadcast(shp), ALU.is_equal))
                        L.link(V.tensor_tensor(sel[:], sel[:], d3, ALU.mult))
                        L.link(V.tensor_reduce(pick[:, :, k:k + 1], sel[:], AX_X, ALU.max))
                        L.link(V.tensor_tensor(oh[k][:], d3, pick[:, :, k:k + 1].to_broadcast(shp), ALU.is_equal))
                    L.link(V.tensor_tensor(dlt[:], top[:, :, 1], top[:, :, 0], ALU.subtract))
                    L.end(V.tensor_tensor(ohb[:], oh[0][:], oh[1][:], ALU.add))
                elif kind == "pf":
                    Q = pfch
                    dve.wait_ge(ready["pf"], b + const + 1)
                    dve.wait_ge(expd_ready, b + const + 1)
                    pfch.begin(b, 1, const)
                    Q.link(V.tensor_copy(tot[:], misc[:, 64:128].rearrange("p (t e) -> p t e", t=NT)))
                    Q.link(V.tensor_copy(base[:, 0, :], base[:, NT, :]))
                    for t in range(NT):
                        Q.link(V.tensor_tensor(base[:, t + 1, :], base[:, t, :], tot[:, t, :], ALU.add))
                    Q.link(V.tensor_tensor(pos[:], misc[:, 0:64].rearrange("p (t e) -> p t e", t=NT), base[:, 0:NT, :], ALU.add))
                    for k in range(2):
                        Q.link(V.tensor_tensor(sel[:], oh[k][:], pos[:], ALU.mult))
                        Q.link(V.tensor_reduce(posk[:, :, k:k + 1], sel[:], AX_X, ALU.add))
                    Q.link(V.tensor_scalar(keep[:], posk[:], float(CAP), None, ALU.is_lt))
                    Q.link(V.tensor_scalar(drop[:], keep[:], -1.0, 1.0, ALU.mult, ALU.add))
                    Q.link(V.scalar_tensor_tensor(out=dest[:], in0=pick[:], scalar=-float(SLOTS), in1=posk[:],
                                                  op0=ALU.mult, op1=ALU.add))
                    Q.link(V.tensor_scalar(dest[:], dest[:], float(NE * SLOTS), None, ALU.add))
                    Q.link(V.scalar_tensor_tensor(out=dst_s[:], in0=drop[:], scalar=float(NE * SLOTS), in1=dest[:],
                                                  op0=ALU.mult, op1=ALU.add))
                    Q.link(V.tensor_copy(idx_s[:], dst_s[:]))
                    Q.link(V.tensor_tensor(dest[:], dest[:], keep[:], ALU.mult))
                    Q.link(V.scalar_tensor_tensor(out=dst_g[:], in0=drop[:], scalar=float(NE * SLOTS), in1=dest[:],
                                                  op0=ALU.mult, op1=ALU.add))
                    Q.link(V.tensor_copy(idx_g[:], dst_g[:]))
                    Q.link(V.tensor_scalar(den[:], expd[:], 1.0, None, ALU.add))
                    Q.link(V.reciprocal(gates[:, :, 0], den[:]))
                    Q.link(V.tensor_tensor(gates[:, :, 1], gates[:, :, 0], expd[:], ALU.mult))
                    Q.end(V.tensor_tensor(gates[:], gates[:], keep[:], ALU.mult))

            def tiles(b, db, g2, grp, k):
                h, (t, k0, w, col) = GROUP_TILES[k]
                idx = 192 * db + 96 * g2 + 48 * grp + k
                dve.wait_ge(mx_ready, count(b, 192, idx + 1))
                V.tensor_reduce(pmax[:, grp, h, col:col + 1], mx[:, idx % 2, 0:w], AX_X, ALU.max).then_inc(mx_done, 1)

            def gather_max(b, db, g2, grp):
                const = 4 * db + 2 * g2 + grp
                dve.wait_ge(mx_done, count(b, 192, 192 * db + 96 * g2 + 48 * grp + 48))
                if not (isinstance(b, int) and b == 0 and const == 0):
                    dve.wait_ge(ready["m"], count(b, 4, const))
                m3 = mcol[:, 0:32].rearrange("p (h t) -> p h t", h=GH)
                V.tensor_copy(m3[:, :, 0:4], pmax[:, grp, :, 0:4]).then_inc(mcol_seq, 1)
                V.tensor_tensor(m3[:, :, 4:8], pmax[:, grp, :, 4:8], pmax[:, grp, :, 8:12], ALU.max).then_inc(mcol_seq, 1)

            def norm(b, const):
                dve.wait_ge(wo_seq, count(b, 4 * WO_OPS, 4 * WO_OPS * (const + 1)))
                V.tensor_scalar(vare[:], mv[:, :, 1], EPS, None, ALU.add).then_inc(ve_ready, 1)
                dve.wait_ge(rstd_ready, b + const + 1)
                for t in range(NT):
                    ins = V.tensor_scalar(x1[:, t, :], x1[:, t, :], mv[:, t, 0:1], rstd[:, t:t + 1],
                                          ALU.subtract, ALU.mult)
                ins.then_inc(x1_ready, 1)

            def v_switch(b):
                if not (isinstance(b, int) and b == 0):
                    dve.wait_ge(pv_done, count(b, 48, 0))
                dve.wait_ge(v_taken, count(b, 4, 4))
                V.tensor_copy(v_now[:], v_next[:]).then_inc(v_switched, 1)

            def body(b, first, last):
                for g in range(2):
                    items = items_of(g, first, last)
                    for s in range(STEPS):
                        ms = []
                        if s in TILES_THIS:
                            ms = [(0, g, 1, k) for k in range(*TILES_THIS[s])]
                        if s in TILES_NEXT and not (last and g == 1):
                            ms = [(0 if g == 0 else 1, 1 - g, 0, k) for k in range(*TILES_NEXT[s])]
                        cut = [len(ms) * q // 3 for q in range(4)]
                        for m in ms[cut[0]:cut[1]]:
                            tiles(b, *m)
                        for it in items.get((s, 0), []):
                            item(b, it)
                        for m in ms[cut[1]:cut[2]]:
                            tiles(b, *m)
                        if g == 0 and s == 0:
                            v_switch(b)
                        for it in items.get((s, 1), []):
                            item(b, it)
                        for m in ms[cut[2]:cut[3]]:
                            tiles(b, *m)
                        if s == 6:
                            gather_max(b, 0, g, 1)
                        if s == 18 and not (last and g == 1):
                            gather_max(b, 0 if g == 0 else 1, 1 - g, 0)
                        if g == 0 and s == 8 and not first:
                            norm(b, -1)

            V.memset(zeros[:], 0.0).then_inc(zero_ready, 1)
            V.memset(mcol[:], 0.0).then_inc(cleared, 1)
            V.memset(base[:], 0.0).then_inc(cleared, 1)
            V.memset(v_next[:], 1.0).then_inc(cleared, 1)
            V.memset(mhalf[:], -0.5).then_inc(cleared, 1)
            dve.wait_ge(cleared, 4)
            dve.wait_ge(consts_in, 16 * 9)
            V.tensor_copy(cb[:, 0:4 * P], cf[:, 0:4 * P])
            V.memset(onesB, 1.0).then_inc(consts_ready, 1)
            dve.wait_ge(consts_ready, 1)
            for it in HEAD:
                item(0, it)
            for k in range(48):
                tiles(0, 0, 0, 0, k)
            gather_max(0, 0, 0, 0)
            item(0, ("m", 0, 0, 0, 0))
            body(0, True, False)
            with dve.Fori(1, NB - 1) as b:
                body(b, False, False)
            body(NB - 1, False, True)
            for it in TAIL:
                item(NB - 1, it)
                if it[0] == "wo" and it[2] == 3:
                    norm(NB - 1, 0)




HID = 1024
MH = HID // P
CH = 432
NCH = SLOTS // CH
SUB = CH // 4


def phase_experts(nc, T):
    with ExitStack() as ctx:
        def sb(name, shape, dt=F32):
            return ctx.enter_context(nc.sbuf_tensor("b_" + name, shape, dt))

        def sem(name):
            return ctx.enter_context(nc.semaphore("b_" + name))

        def psum(name, shape):
            return ctx.enter_context(nc.psum_tensor("b_" + name, shape, F32))

        identF = sb("ident", [P, P])
        raw1 = sb("raw1", [P, KC, HID])
        raw2 = sb("raw2", [P, MH, D])
        w1 = [[sb(f"w1_{s}{p}", [P, KC, HID], F32R) for p in range(2)] for s in range(2)]
        w2 = [[sb(f"w2_{s}{p}", [P, MH, D], F32R) for p in range(2)] for s in range(2)]
        b1 = [sb(f"b1_{s}", [P, MH]) for s in range(2)]
        b2 = [sb(f"b2_{s}", [P, KC]) for s in range(2)]
        xin = [sb(f"xin{i}", [SUB, 4, D]) for i in range(2)]
        xp = [[sb(f"xp{i}{p}", [P, KC, CH], F32R) for p in range(2)] for i in range(2)]
        hf = [sb(f"hf{i}", [P, CH]) for i in range(2)]
        hp = [[sb(f"hp{i}{p}", [P, MH, CH], F32R) for p in range(2)] for i in range(2)]
        yT = [sb(f"yT{i}", [P, KC, CH]) for i in range(2)]
        yo = [sb(f"yo{i}", [SUB, 4, D]) for i in range(2)]
        p_x = psum("p_x", [P, KC, 512])
        p_h = psum("p_h", [P, 2, 512])
        p_y = psum("p_y", [P, KC, 512])
        p_t = psum("p_t", [P, 2, 512])

        ident_in = sem("ident_in")
        raw_in = sem("raw_in")
        bias_in = [sem(f"bias_in{i}") for i in range(2)]
        w_seq = sem("w_seq")
        xin_in = [sem(f"xin_in{i}") for i in range(2)]
        xt_ready = sem("xt_ready")
        xh_ready = sem("xh_ready")
        xl_ready = sem("xl_ready")
        h_ready = sem("h_ready")
        hf_ready = sem("hf_ready")
        hh_ready = sem("hh_ready")
        hl_ready = sem("hl_ready")
        y_ready = sem("y_ready")
        yT_ready = sem("yT_ready")
        yt_ready = sem("yt_ready")
        yo_ready = sem("yo_ready")
        y_out = [sem(f"y_out{i}") for i in range(2)]
        N2 = 2 * NCH
        NALL = NE * NCH

        def rows(i, c):
            return (i * 2 + c // NCH) * SLOTS + (c % NCH) * CH

        block = ctx.enter_context(nc.Block())

        @block.sync
        def _(sp):
            def weights(e, slot, first=False):
                if not first:
                    pass
                sp.dma_start(raw1[:], T["w1"][e].rearrange("(k p) n -> p k n", p=P)).then_inc(raw_in, 16)
                sp.dma_start(raw2[:], T["w2"][e].rearrange("(k p) n -> p k n", p=P)).then_inc(raw_in, 16)
                sp.dma_start(b1[slot][:], T["b1"][e]).then_inc(bias_in[slot], 16)
                sp.dma_start(b2[slot][:], T["b2"][e]).then_inc(bias_in[slot], 16)

            def load(i, c):
                sp.dma_start(xin[c % 2][:], T["buf"][bass.ds(rows(i, c), CH), :].rearrange("(q p) d -> p q d", p=SUB))\
                    .then_inc(xin_in[c % 2], 16)

            def store(i, c):
                wait_apart(sp, yo_ready, count(i, N2, c + 1))
                sp.dma_start(T["y"][bass.ds(rows(i, c) if c >= 0 else rows(i, c + N2) - 2 * SLOTS, CH), :]
                             .rearrange("(q p) d -> p q d", p=SUB), yo[c % 2][:]).then_inc(y_out[c % 2], 16)

            def body(i, first, last):
                for c in range(N2):
                    if not (last and c == N2 - 1):
                        if not (first and c == 0):
                            wait_apart(sp, xt_ready, count(i, N2, c))
                        if c < N2 - 1:
                            load(i, c + 1)
                        else:
                            load(i + 1, 0)
                    if c % NCH == 1 and not (last and c >= NCH):
                        half = c // NCH
                        wait_apart(sp, w_seq, count(i, 16, 8 * (half + 1)))
                        if not (first and half == 0):
                            wait_apart(sp, yT_ready, count(i, 2 * N2, 2 * (half * NCH)))
                        weights(2 * i + half + 1, 1 - half)
                    if c >= 2 or not first:
                        store(i, c - 2)

            sp.dma_start(identF[:], T["consts"][:, 0:P]).then_inc(ident_in, 16)
            weights(0, 0, True)
            load(0, 0)
            body(0, True, False)
            with sp.Fori(1, NE // 2 - 1) as i:
                body(i, False, False)
            body(NE // 2 - 1, False, True)
            store(NE // 2 - 1, N2 - 2)
            store(NE // 2 - 1, N2 - 1)
            wait_apart(sp, y_out[0], 16 * NALL // 2)
            wait_apart(sp, y_out[1], 16 * NALL // 2)

        @block.tensor
        def _(pe):
            def mm(out, a, bb, start, stop):
                return pe.matmul(out, a, bb, start=start, stop=stop)

            def turn_in(i, c):
                pe.wait_ge(xin_in[c % 2], count(i, 16 * NCH, 16 * (c // 2 + 1)))
                if not (isinstance(i, int) and i == 0 and c == 0):
                    pe.wait_ge(xl_ready, count(i, N2, c))
                for k in range(KC):
                    for q in range(4):
                        m = pe.transpose(p_x[:, k, q * SUB:(q + 1) * SUB], xin[c % 2][:, q, k * P:(k + 1) * P],
                                         identF[0:SUB, 0:SUB])
                m.then_inc(xt_ready, 1)

            def turn_out(i, c):
                pe.wait_ge(yT_ready, count(i, 2 * N2, 2 * (c + 1)))
                if not (isinstance(i, int) and i == 0 and c == 0):
                    pe.wait_ge(yo_ready, count(i, N2, c))
                for q in range(4):
                    for k in range(KC):
                        m = pe.transpose(p_t[0:SUB, q // 2, (q % 2) * D + k * P:(q % 2) * D + (k + 1) * P],
                                         yT[c % 2][:, k, q * SUB:(q + 1) * SUB], identF[:])
                m.then_inc(yt_ready, 1)

            def hidden(i, c, m):
                slot = c // NCH
                if m == 0:
                    pe.wait_ge(xl_ready, count(i, N2, c + 1))
                    if c % NCH == 0:
                        pe.wait_ge(w_seq, count(i, 16, 8 * (slot + 1)))
                n = MH * c + m
                if not (isinstance(i, int) and i == 0 and n < 2):
                    pe.wait_ge(hh_ready, count(i, MH * N2, n - 1))
                x = xp[c % 2]
                o = p_h[:, m % 2, 0:CH]
                terms = [(wp, xq, k) for wp, xq in ((0, 0), (0, 1), (1, 0)) for k in range(KC)]
                for t, (wp, xq, k) in enumerate(terms):
                    r = mm(o, w1[slot][wp][:, k, m * P:(m + 1) * P], x[xq][:, k, :], t == 0, t == len(terms) - 1)
                r.then_inc(h_ready, 1)

            def output(i, c, part):
                slot = (c // NCH) % 2
                k, first = part // 4, (part % 4) * 2
                if part % 4 == 0 and not (isinstance(i, int) and i == 0 and c == 0):
                    pe.wait_ge(yT_ready, count(i, 2 * N2, 2 * c + k - 1 + 0) if k else count(i, 2 * N2, 2 * c - 1))
                if part % 4 == 0 and k == 1 and False:
                    pass
                for j in (first, first + 1):
                    if k == 0:
                        pe.wait_ge(hl_ready, count(i, MH * N2, MH * c + j + 1))
                    for t, (wp, hq) in enumerate(((0, 0), (0, 1), (1, 0))):
                        r = mm(p_y[:, k, 0:CH], w2[slot][wp][:, j, k * P:(k + 1) * P], hp[c % 2][hq][:, j, :],
                               j == 0 and t == 0, j == MH - 1 and t == 2)
                if part % 4 == 3:
                    r.then_inc(y_ready, 1)

            def body(i, first, last):
                for c in range(N2):
                    for m in range(MH):
                        hidden(i, c, m)
                        if m == 3 and not (last and c == N2 - 1):
                            turn_in(i, c + 1)
                        if c > 0 or not first:
                            output(i, c - 1, m)
                        if m == 1 and (c > 1 or not first):
                            turn_out(i, c - 2)

            pe.wait_ge(ident_in, 16)
            turn_in(0, 0)
            body(0, True, False)
            with pe.Fori(1, NE // 2 - 1) as i:
                body(i, False, False)
            body(NE // 2 - 1, False, True)
            for part in range(MH):
                if part == 1:
                    turn_out(NE // 2 - 1, N2 - 2)
                output(NE // 2 - 1, N2 - 1, part)
            turn_out(NE // 2 - 1, N2 - 1)

        @block.scalar
        def _(act):
            A = nc.scalar

            def high(i, c):
                act.wait_ge(xt_ready, count(i, N2, c + 1))
                A.activation(xp[c % 2][0][:], p_x[:, :, 0:CH], ACT.Copy).then_inc(xh_ready, 1)

            def gelu(i, c, m):
                n = MH * c + m
                act.wait_ge(h_ready, count(i, MH * N2, n + 1))
                if not (isinstance(i, int) and i == 0 and n < 2):
                    act.wait_ge(hl_ready, count(i, MH * N2, n - 1))
                bias = b1[c // NCH][:, m:m + 1]
                A.activation(hf[m % 2][:], p_h[:, m % 2, 0:CH], ACT.Gelu_apprx_tanh, bias=bias).then_inc(hf_ready, 1)
                A.activation(hp[c % 2][0][:, m, :], p_h[:, m % 2, 0:CH], ACT.Gelu_apprx_tanh, bias=bias).then_inc(hh_ready, 1)

            def out(i, c, k):
                act.wait_ge(y_ready, count(i, 2 * N2, 2 * c + k + 1))
                slot = (c // NCH) % 2
                A.activation(yT[c % 2][:, k, :], p_y[:, k, 0:CH], ACT.Identity, bias=b2[slot][:, k:k + 1]).then_inc(yT_ready, 1)

            def body(i, first, last):
                for c in range(N2):
                    for m in range(MH):
                        if m == 0 and c % NCH == 0:
                            act.wait_ge(bias_in[c // NCH], count(i, 32, 32))
                        if m == 0 and (c > 0 or not first) :
                            pass
                        gelu(i, c, m)
                        if m == 3 and not (last and c == N2 - 1):
                            high(i, c + 1)
                        if m == 3 and (c > 0 or not first):
                            out(i, c - 1, 0)
                    if c > 0 or not first:
                        out(i, c - 1, 1)

            high(0, 0)
            body(0, True, False)
            with act.Fori(1, NE // 2 - 1) as i:
                body(i, False, False)
            body(NE // 2 - 1, False, True)
            out(NE // 2 - 1, N2 - 1, 0)
            out(NE // 2 - 1, N2 - 1, 1)

        @block.vector
        def _(dve):
            V = nc.vector

            def low(i, c):
                dve.wait_ge(xh_ready, count(i, N2, c + 1))
                V.tensor_tensor(xp[c % 2][1][:], p_x[:, :, 0:CH], xp[c % 2][0][:].bitcast(F32), ALU.subtract)\
                    .then_inc(xl_ready, 1)

            def hlow(i, c, m):
                dve.wait_ge(hf_ready, count(i, MH * N2, MH * c + m + 1))
                dve.wait_ge(hh_ready, count(i, MH * N2, MH * c + m + 1))
                V.tensor_tensor(hp[c % 2][1][:, m, :], hf[m % 2][:], hp[c % 2][0][:, m, :].bitcast(F32), ALU.subtract)\
                    .then_inc(hl_ready, 1)

            def rows_out(i, c):
                dve.wait_ge(yt_ready, count(i, N2, c + 1))
                if not (isinstance(i, int) and i == 0 and c < 2):
                    dve.wait_ge(y_out[c % 2], count(i, 16 * NCH, 16 * (c // 2)))
                V.tensor_copy(yo[c % 2][:].rearrange("p (a q) d -> p a (q d)", a=2), p_t[0:SUB, :, :]).then_inc(yo_ready, 1)

            def weights(i, slot, piece):
                if piece == 0:
                    dve.wait_ge(raw_in, count(i, 64, 32 * (slot + 1)))
                w, raw, h = (w1, raw1, slice(piece, piece + 1)) if piece < 2 else (w2, raw2, slice(4 * (piece - 2), 4 * (piece - 1)))
                s = slot % 2
                V.tensor_copy(w[s][0][:, h, :], raw[:, h, :]).then_inc(w_seq, 1)
                dve.wait_ge(w_seq, count(i, 16, 8 * slot + 2 * piece + 1))
                V.tensor_tensor(w[s][1][:, h, :], raw[:, h, :], w[s][0][:, h, :].bitcast(F32), ALU.subtract).then_inc(w_seq, 1)

            def body(i, first, last):
                for c in range(N2):
                    for m in range(MH):
                        hlow(i, c, m)
                        if m == 3 and not (last and c == N2 - 1):
                            low(i, c + 1)
                        if m == 2 and (c > 1 or not first):
                            rows_out(i, c - 2)
                        if m == 5 and c % NCH >= 1 and not (last and c >= NCH):
                            if c % NCH == 1:
                                if not (first and c < NCH):
                                    dve.wait_ge(y_ready, count(i, 2 * N2, 2 * (c - 1)))
                            weights(i, c // NCH + 1, c % NCH - 1)

            for piece in range(4):
                weights(0, 0, piece)
            low(0, 0)
            body(0, True, False)
            with dve.Fori(1, NE // 2 - 1) as i:
                body(i, False, False)
            body(NE // 2 - 1, False, True)
            rows_out(NE // 2 - 1, N2 - 2)
            rows_out(NE // 2 - 1, N2 - 1)


FH = 768
FM = FH // P
N_FF = 2 * FM
SCALE = 1.0 / 127.0
TINY = 1.1754943508222875e-38

C_SEQ = {"xt": 4, "v": 4, "q": 4, "g": 4, "rt": 4, "zt": 4, "wo": 4, "d1": 4, "ff": N_FF, "dn": 4}
RING = {"xt": "turn", "d1": "turn", "rt": "turn", "zt": "turn", "v": "prod", "q": "prod", "g": "prod",
        "wo": "prod", "dn": "prod", "ff": "pair"}
LATE = ("d1", "ff", "dn")


def order(head, tail, combine):
    items = []

    def put(kind, *js):
        for j in js:
            if kind in LATE and head or kind in C_SEQ and kind not in LATE and tail:
                continue
            items.append((kind, j))

    put("xt", 0, 1, 2, 3)
    put("v", 0, 1, 2, 3)
    put("q", 0, 1, 2, 3)
    put("d1", 0, 1, 2, 3)
    put("g", 0, 1, 2, 3)
    put("ff", 0, 1, 2)
    put("rt", 0, 1, 2, 3)
    if not tail:
        items.append(("rt_norm", 0))
    for f in range(3, N_FF):
        put("ff", f)
        if combine and not head and f - 3 < NT:
            items.append(("sum", f - 3))
        if f == 6:
            put("zt", 0, 1, 2, 3)
    if combine and not head:
        items.append(("sum_norm", 0))
    put("dn", 0, 1, 2, 3)
    if not head:
        items.append(("dn_norm", 0))
    put("wo", 0, 1, 2, 3)
    if not tail:
        items.append(("wo_norm", 0))
    if head:
        items += [("sum", t) for t in range(NT)] + [("sum_norm", 0)]
    return items


SUM_OPS, RT_OPS, ADD_OPS = 4, 4, 5
PREP = 16


def run_steps(eng, step):
    step(0, True, False, True, True)
    with eng.Fori(1, NB - 2) as b:
        step(b, False, False, True, True)
    step(NB - 2, False, False, True, False)
    step(NB - 1, False, False, False, False)
    step(NB, False, True, False, False)


def phase_layer1(nc, T):
    with ExitStack() as ctx:
        def sb(name, shape, dt=F32):
            return ctx.enter_context(nc.sbuf_tensor("c_" + name, shape, dt))

        def sem(name):
            return ctx.enter_context(nc.semaphore("c_" + name))

        identF = sb("ident", [P, P])
        wp = {k: [sb(f"w{k}{p}", [P, KC, D], F32R) for p in range(2)] for k in ("q", "v", "g")}
        wo = sb("wo", [P, KC, D])
        wgt = [sb(f"wgt{p}", [P, KC, FH], F32R) for p in range(2)]
        wup = [sb(f"wup{p}", [P, KC, FH], F32R) for p in range(2)]
        wdn = sb("wdn", [P, FM, D])
        gb = sb("gb", [P, 2, KC])
        bexp = sb("bexp", [P, KC])
        lam = sb("lam", [P, KC])
        x1t = sb("x1t", [P, NT, D])
        yg = [sb(f"yg{k}", [P, NT, D]) for k in range(TOPK)]
        gates = sb("gates", [P, NT, TOPK])
        idx = sb("idx", [P, NT, TOPK], I32)
        xn = sb("xn", [P, NT, D])
        x2 = sb("x2", [P, NT, D])
        x3 = sb("x3", [P, NT, D])
        o = sb("o", [P, NT, D])
        xp = [sb(f"xp{p}", [P, KC, S], F32R) for p in range(2)]
        x3p = [sb(f"x3p{p}", [P, KC, S], F32R) for p in range(2)]
        ret = sb("ret", [P, KC, S])
        gT = sb("gT", [P, KC, S])
        rt = sb("rt", [P, NT, D])
        zT = sb("zT", [P, KC, S])
        h = sb("h", [P, FM, S])
        sg = [sb(f"sg{i}", [P, HALF]) for i in range(2)]
        LNS = ("sum", "rt", "wo", "dn")
        stats = {k: sb("stats_" + k, [P, NT, 6]) for k in LNS}
        mv = {k: sb("mv_" + k, [P, NT, 2]) for k in LNS}
        vare = {k: sb("vare_" + k, [P, NT]) for k in LNS}
        rstd = {k: sb("rstd_" + k, [P, NT]) for k in LNS}
        mhalf = sb("mhalf", [P, NT])
        stage = h[:].rearrange("p m n -> p (m n)")

        p_turn = ctx.enter_context(nc.psum_tensor("c_turn", [P, 2, HALF], F32))
        p_prod = ctx.enter_context(nc.psum_tensor("c_prod", [P, 2, HALF], F32))
        p_pair = ctx.enter_context(nc.psum_tensor("c_pair", [P, 2, 2, HALF], F32))

        const_in = sem("const_in")
        stage_in = sem("stage_in")
        stage_seq = sem("stage_seq")
        prep = sem("prep")
        prep_pool = sem("prep_pool")
        lam_exp = sem("lam_exp")
        ready = {k: sem(k + "_ready") for k in C_SEQ}
        act_took = {k: sem(k + "_copied") for k in ("xt", "g", "rt", "zt", "d1")}
        silu_ready = sem("silu_ready")
        xl_ready = sem("xl_ready")
        x3l_ready = sem("x3l_ready")
        scanned = sem("scanned")
        ret_ready = sem("ret_ready")
        h_ready = sem("h_ready")
        z_ready = sem("z_ready")
        seq = {k: sem(k + "_seq") for k in LNS}
        ve_ready = {k: sem(k + "_ve") for k in LNS}
        rstd_ready = {k: sem(k + "_rstd") for k in LNS}
        normed = {k: sem(k + "_normed") for k in LNS}
        gathered = sem("gathered")
        idx_in = sem("idx_in")
        x1_in = sem("x1_in")
        x2_ready = sem("x2_ready")
        o_free = sem("o_free")

        taken = {"xt": (xl_ready, 1, 1), "d1": (x3l_ready, 1, 1), "rt": (act_took["rt"], 1, 1),
                 "zt": (act_took["zt"], 1, 1), "v": (scanned, 1, 1), "q": (ret_ready, 1, 1), "g": (act_took["g"], 1, 1),
                 "wo": (seq["wo"], ADD_OPS, 1), "dn": (seq["dn"], ADD_OPS, 1), "ff": (h_ready, 1, 1)}

        def const_of(kind, j):
            return j - C_SEQ[kind] if kind in LATE else j

        N_STAGE = 9
        block = ctx.enter_context(nc.Block())

        def staged():
            for k in ("q", "v", "g"):
                yield T["w1" + k].rearrange("(k p) n -> p k n", p=P), KC * D, wp[k], False
            for src, dst in ((T["wgt"], wgt), (T["wup"], wup)):
                yield src.rearrange("(k p) n -> p k n", p=P), KC * FH, dst, True
            yield T["wdn"].rearrange("(k p) n -> p k n", p=P), FM * D, wdn, True

        STAGED = list(staged())
        offs, at = [], 0
        for src, cols, dst, integer in STAGED:
            offs.append(at)
            at += cols
        assert at <= FM * S

        @block.sync
        def _(sp):
            def load_idx(b, db):
                sp.dma_start(idx[:], T["dest"][b + db]).then_inc(idx_in, 16)

            def load_x1(b, db):
                sp.dma_start(x1t[:], T["x1"][b + db].rearrange("(t p) d -> p t d", p=P)).then_inc(x1_in, 16)
                sp.dma_start(gates[:], T["gates"][b + db]).then_inc(x1_in, 16)

            load_idx(0, 0)
            for (src, cols, dst, integer), off in zip(STAGED, offs):
                v = stage[:, off:off + cols].rearrange("p (k n) -> p k n", k=src.shape[1])
                sp.dma_start(v.bitcast(I32) if integer else v, src).then_inc(stage_in, 16)
            load_x1(0, 0)
            sp.dma_start(identF[:], T["consts"][:, 0:P]).then_inc(const_in, 16)
            sp.dma_start(gb[:], T["gb"]).then_inc(const_in, 16)
            sp.dma_start(bexp[:], T["bexp"]).then_inc(const_in, 16)
            sp.dma_start(wo[:], T["w1o"].rearrange("(k p) n -> p k n", p=P)).then_inc(const_in, 16)
            wait_apart(sp, gathered, 256)
            load_idx(0, 1)
            wait_apart(sp, normed["sum"], 1)
            load_x1(0, 1)

            def step(b, head, tail, combine, gather):
                if gather:
                    wait_apart(sp, gathered, count(b, 256, 512))
                    load_idx(b, 2)
                    wait_apart(sp, normed["sum"], count(b, 1, 2))
                    load_x1(b, 2)
                if not head:
                    wait_apart(sp, normed["dn"], count(b, 1, 0))
                    sp.dma_start(T["out"][b - 1].rearrange("(t p) d -> p t d", p=P), o[:]).then_inc(o_free, 16)

            run_steps(sp, step)
            wait_apart(sp, o_free, 16 * (NB + 1))

        @block.tensor
        def _(pe):
            hist = {"turn": [], "prod": [], "pair": []}

            def mm(out, a, bb, start, stop):
                return pe.matmul(out, a, bb, start=start, stop=stop, skip_group_check=True)

            def split_product(out, w, x, cols, n, more=False):
                terms = [(a, c, k) for a, c in ((0, 0), (0, 1), (1, 0)) for k in range(KC)]
                for t, (a, c, k) in enumerate(terms):
                    r = mm(out, w[a][:, k, cols], x[c][:, k, n * HALF:(n + 1) * HALF], t == 0, t == len(terms) - 1)
                return r

            def turn(bank, src, j):
                for q in range(4):
                    r = pe.transpose(bank[:, q * P:(q + 1) * P], src[:, 4 * (j // 2) + q, (j % 2) * P:(j % 2 + 1) * P], identF[:])
                return r

            def item(b, kind, j):
                const = const_of(kind, j)
                ring = RING[kind]
                past = hist[ring]
                slot = j % 2
                if len(past) >= 2 and past[-2] is not None:
                    k0, c0 = past[-2]
                    read, per, nth = taken[k0]
                    if not (kind == "ff" and j < 2):
                        pe.wait_ge(read, count(b, per * C_SEQ[k0], per * c0 + nth))
                past.append((kind, const))
                n, m = j // 2, j % 2
                if kind == "xt":
                    if j == 0:
                        pe.wait_ge(normed["sum"], count(b, 1, 1))
                    r = turn(p_turn[:, slot, :], xn, j)
                elif kind == "d1":
                    if j == 0:
                        pe.wait_ge(normed["wo"], count(b, 1, 0))
                    r = turn(p_turn[:, slot, :], x3, j)
                elif kind in ("v", "q", "g"):
                    pe.wait_ge(xl_ready, count(b, 4, 2 * n + 2))
                    r = split_product(p_prod[:, slot, :], wp[kind], xp, slice(m * P, (m + 1) * P), n)
                elif kind == "rt":
                    pe.wait_ge(ret_ready, count(b, 4, 2 * (j // 2) + 2))
                    bank = p_turn[:, slot, :].rearrange("p (t d) -> p t d", t=2)
                    for u in range(2):
                        t = 2 * j + u
                        for k in range(KC):
                            r = pe.transpose(bank[:, u, k * P:(k + 1) * P], ret[:, k, t * P:(t + 1) * P], identF[:])
                elif kind == "zt":
                    if j == 0:
                        pe.wait_ge(normed["rt"], count(b, 1, 1))
                    r = turn(p_turn[:, slot, :], rt, j)
                elif kind == "wo":
                    pe.wait_ge(z_ready, count(b, 4, 2 * (j // 2) + 2))
                    for u in range(2):
                        t = 2 * j + u
                        for k in range(KC):
                            r = mm(p_prod[:, slot, u * D:(u + 1) * D], zT[:, k, t * P:(t + 1) * P], wo[:, k, :], k == 0, k == KC - 1)
                elif kind == "ff":
                    n, m = divmod(j, FM)
                    if m == 0:
                        pe.wait_ge(x3l_ready, count(b, 4, 2 * n + 2 - 4))
                    split_product(p_pair[:, slot, 0, :], wgt, x3p, slice(m * P, (m + 1) * P), n)
                    r = split_product(p_pair[:, slot, 1, :], wup, x3p, slice(m * P, (m + 1) * P), n)
                elif kind == "dn":
                    pe.wait_ge(h_ready, count(b, N_FF, FM * (j // 2 + 1) - N_FF))
                    for u in range(2):
                        t = 2 * j + u
                        for k in range(FM):
                            r = mm(p_prod[:, slot, u * D:(u + 1) * D], h[:, k, t * P:(t + 1) * P], wdn[:, k, :], k == 0, k == FM - 1)
                r.then_inc(ready[kind], 1)

            def step(b, head, tail, combine, gather):
                for ring in hist:
                    hist[ring] = [(k, c - C_SEQ[k]) for k, c in hist[ring][-2:]]
                for kind, j in order(head, tail, combine):
                    if kind in C_SEQ:
                        item(b, kind, j)

            pe.wait_ge(const_in, 64)
            pe.wait_ge(prep, PREP)
            run_steps(pe, step)

        @block.scalar
        def _(act):
            A = nc.scalar
            act.wait_ge(const_in, 64)
            A.activation(lam[:], bexp[:], ACT.Exp, scale=-0.6931471805599453).then_inc(lam_exp, 1)

            def item(b, kind, j):
                const = const_of(kind, j)
                hist_slot = j % 2
                n, m = j // 2, j % 2
                cols = slice(n * HALF, (n + 1) * HALF)
                if kind in ("xt", "d1"):
                    act.wait_ge(ready[kind], count(b, 4, const + 1))
                    A.activation((xp if kind == "xt" else x3p)[0][:, m, cols], p_turn[:, hist_slot, :], ACT.Copy)\
                        .then_inc(act_took[kind], 1)
                elif kind == "g":
                    act.wait_ge(ready[kind], count(b, 4, const + 1))
                    A.activation(gT[:, m, cols], p_prod[:, hist_slot, :], ACT.Silu).then_inc(act_took["g"], 1)
                elif kind == "rt":
                    act.wait_ge(ready[kind], count(b, 4, const + 1))
                    A.activation(rt[:, 2 * j:2 * j + 2, :], p_turn[:, hist_slot, :].rearrange("p (t d) -> p t d", t=2), ACT.Copy)\
                        .then_inc(act_took["rt"], 1)
                elif kind == "zt":
                    act.wait_ge(ready[kind], count(b, 4, const + 1))
                    A.activation(zT[:, m, cols], p_turn[:, hist_slot, :], ACT.Identity,
                                 scale=gb[:, 0, m:m + 1], bias=gb[:, 1, m:m + 1]).then_inc(act_took["zt"], 1)
                elif kind == "ff":
                    act.wait_ge(ready[kind], count(b, N_FF, const + 1))
                    A.activation(sg[j % 2][:], p_pair[:, hist_slot, 0, :], ACT.Silu).then_inc(silu_ready, 1)

            def step(b, head, tail, combine, gather):
                for kind, j in order(head, tail, combine):
                    if kind in C_SEQ:
                        item(b, kind, j)

            run_steps(act, step)

        @block.gpsimd
        def _(pool):
            def gather(b, db):
                wait_apart(pool, idx_in, count(b, 16, 16 * (db + 1)))
                for t in range(NT):
                    for k in range(TOPK):
                        pool.indirect_dma_start(yg[k][:, t, :], None, T["y"],
                                                bass.IndirectOffsetOnAxis(ap=idx[:, t, k:k + 1].bitcast(U32), axis=0))\
                            .then_inc(gathered, 16)

            def root(b, kind, const):
                pool.wait_ge(ve_ready[kind], count(b, 1, const + 1))
                nc.gpsimd.tensor_tensor(rstd[kind][:], vare[kind][:], mhalf[:], ALU.pow).then_inc(rstd_ready[kind], 1)

            def gate(b, j):
                n, m = j // 2, j % 2
                pool.wait_ge(act_took["zt"], count(b, 4, j + 1))
                pool.wait_ge(act_took["g"], count(b, 4, j + 1))
                v = zT[:, m, n * HALF:(n + 1) * HALF]
                nc.gpsimd.tensor_tensor(v, v, gT[:, m, n * HALF:(n + 1) * HALF], ALU.mult).then_inc(z_ready, 1)

            def step(b, head, tail, combine, gather_):
                for kind, j in order(head, tail, combine):
                    if kind == "rt_norm":
                        root(b, "rt", 0)
                    elif kind == "zt" and j == 3:
                        for i in range(4):
                            gate(b, i)
                    elif kind == "sum_norm":
                        root(b, "sum", 1)
                        if gather_:
                            gather(b, 2)
                    elif kind == "dn_norm":
                        root(b, "dn", -1)
                    elif kind == "wo_norm":
                        root(b, "wo", 0)

            nc.gpsimd.memset(mhalf[:], -0.5).then_inc(prep_pool, 1)
            pool.wait_ge(prep_pool, 1)
            gather(0, 0)
            root(0, "sum", 0)
            gather(0, 1)
            run_steps(pool, step)

        @block.vector
        def _(dve):
            V = nc.vector

            def chain(kind, b, per_seq, per, const):
                n = [0]

                def link(ins, last=False):
                    n[0] += 1
                    ins.then_inc(seq[kind], 1)
                    if not last:
                        wait_apart(dve, seq[kind], count(b, per_seq * per, per * const + n[0]))
                    else:
                        assert n[0] == per
                return link

            def stats_of(link, kind, src, tiles):
                for t in tiles:
                    link(V.bn_stats(stats[kind][:, t, :], src[:, t, :]))
                for t in tiles:
                    link(V.bn_aggr(mv[kind][:, t, :], stats[kind][:, t, :]), last=t == tiles[-1])

            def norm(b, kind, const, per, src, dst):
                per_seq = NT if kind == "sum" else 4
                dve.wait_ge(seq[kind], count(b, per_seq * per, per_seq * per * (const + 1)))
                V.tensor_scalar(vare[kind][:], mv[kind][:, :, 1], EPS, None, ALU.add).then_inc(ve_ready[kind], 1)
                dve.wait_ge(rstd_ready[kind], count(b, 1, const + 1))
                for t in range(NT):
                    ins = V.tensor_scalar(dst[:, t, :], src[:, t, :], mv[kind][:, t, 0:1], rstd[kind][:, t:t + 1],
                                          ALU.subtract, ALU.mult)
                ins.then_inc(normed[kind], 1)

            def combine_tile(b, db, t):
                if t == 0:
                    dve.wait_ge(gathered, count(b, 256, 256 * (db + 1)))
                    dve.wait_ge(x1_in, count(b, 32, 32 * (db + 1)))
                link = chain("sum", b, NT, SUM_OPS, NT * db + t)
                for k in range(TOPK):
                    link(V.scalar_tensor_tensor(out=x1t[:, t, :], in0=yg[k][:, t, :], scalar=gates[:, t, k:k + 1],
                                                in1=x1t[:, t, :], op0=ALU.mult, op1=ALU.add))
                stats_of(link, "sum", x1t, [t])

            def item(b, kind, j):
                const = const_of(kind, j)
                slot = j % 2
                n, m = j // 2, j % 2
                cols = slice(n * HALF, (n + 1) * HALF)
                if kind in ("xt", "d1"):
                    hi, lo = xp if kind == "xt" else x3p
                    dve.wait_ge(act_took[kind], count(b, 4, const + 1))
                    V.tensor_tensor(lo[:, m, cols], p_turn[:, slot, :], hi[:, m, cols].bitcast(F32), ALU.subtract)\
                        .then_inc(xl_ready if kind == "xt" else x3l_ready, 1)
                elif kind == "v":
                    dve.wait_ge(ready["v"], count(b, 4, const + 1))
                    if n:
                        dve.wait_ge(scanned, count(b, 4, j - 1))
                    V.tensor_tensor_scan(ret[:, m, cols], lam[:, m:m + 1].to_broadcast([P, HALF]), p_prod[:, slot, :],
                                         ret[:, m, n * HALF - 1:n * HALF] if n else 0.0, ALU.mult, ALU.add)\
                        .then_inc(scanned, 1)
                elif kind == "q":
                    dve.wait_ge(ready["q"], count(b, 4, const + 1))
                    if j == 0:
                        dve.wait_ge(scanned, count(b, 4, 4))
                    V.tensor_tensor(ret[:, m, cols], p_prod[:, slot, :], ret[:, m, cols], ALU.mult).then_inc(ret_ready, 1)
                elif kind == "rt":
                    dve.wait_ge(act_took["rt"], count(b, 4, const + 1))
                    link = chain("rt", b, 4, RT_OPS, const)
                    stats_of(link, "rt", rt, [2 * j, 2 * j + 1])
                elif kind == "ff":
                    n, m = divmod(j, FM)
                    dve.wait_ge(silu_ready, count(b, N_FF, const + 1))
                    V.tensor_tensor(h[:, m, n * HALF:(n + 1) * HALF], p_pair[:, slot, 1, :], sg[j % 2][:], ALU.mult)\
                        .then_inc(h_ready, 1)
                elif kind in ("wo", "dn"):
                    dst, base = (x3, x2) if kind == "wo" else (o, x3)
                    dve.wait_ge(ready[kind], count(b, 4, const + 1))
                    if kind == "dn" and j == 0:
                        dve.wait_ge(o_free, count(b, 16, 0))
                    link = chain(kind, b, 4, ADD_OPS, const)
                    link(V.tensor_tensor(dst[:, 2 * j:2 * j + 2, :], p_prod[:, slot, :].rearrange("p (t d) -> p t d", t=2),
                                         base[:, 2 * j:2 * j + 2, :], ALU.add))
                    stats_of(link, kind, dst, [2 * j, 2 * j + 1])

            def step(b, head, tail, combine, gather):
                if not tail:
                    dve.wait_ge(normed["sum"], count(b, 1, 1))
                    V.tensor_copy(x2[:], xn[:]).then_inc(x2_ready, 1)
                    dve.wait_ge(x2_ready, count(b, 1, 1))
                for kind, j in order(head, tail, combine):
                    if kind in C_SEQ:
                        item(b, kind, j)
                    elif kind == "sum":
                        combine_tile(b, 1, j)
                    elif kind == "sum_norm":
                        norm(b, "sum", 1, SUM_OPS, x1t, xn)
                    elif kind == "rt_norm":
                        norm(b, "rt", 0, RT_OPS, rt, rt)
                    elif kind == "wo_norm":
                        norm(b, "wo", 0, ADD_OPS, x3, x3)
                    elif kind == "dn_norm":
                        norm(b, "dn", -1, ADD_OPS, o, o)

            k = [0]

            def link(ins):
                k[0] += 1
                ins.then_inc(prep, 1)
                dve.wait_ge(prep, k[0])

            dve.wait_ge(lam_exp, 1)
            link(V.tensor_scalar(lam[:], lam[:], -1.0, 1.0, ALU.mult, ALU.add))
            link(V.tensor_scalar(lam[:], lam[:], TINY, 1.0 - 1e-9, ALU.max, ALU.min))
            dve.wait_ge(stage_in, 16 * len(STAGED))
            for (src, cols, dst, integer), off in zip(STAGED, offs):
                raw = stage[:, off:off + cols]
                if integer:
                    link(V.tensor_scalar(raw, raw.bitcast(I32), SCALE, None, ALU.mult))
                if dst is wdn:
                    link(V.tensor_copy(wdn[:].rearrange("p k n -> p (k n)"), raw))
                    continue
                hi, lo = (d[:].rearrange("p k n -> p (k n)") for d in dst)
                link(V.tensor_copy(hi, raw))
                link(V.tensor_tensor(lo, raw, hi.bitcast(F32), ALU.subtract))
            assert k[0] == PREP
            V.memset(o[0:1, 0, 0:1], 0.0).then_inc(o_free, 16)
            for t in range(NT):
                combine_tile(0, 0, t)
            norm(0, "sum", 0, SUM_OPS, x1t, xn)
            run_steps(dve, step)


def build(nc, T):
    def scratch(name, shape, dt=F32):
        return nc.dram_tensor(name, shape, dt, kind="Internal").ap()

    T["qk_scr"] = scratch("qk_scr", (2, 4, 3, P, HALF), BF16)
    T["m_scr"] = scratch("m_scr", (2, 2, 3, GH * S), BF16)
    T["x1"] = scratch("x1", (NB, S, D))
    T["gates"] = scratch("gates", (NB, P, NT, TOPK))
    T["dest"] = scratch("dest", (NB, P, NT, TOPK), I32)
    T["buf"] = scratch("buf", (NE * SLOTS, D))
    T["y"] = scratch("y", (NE * SLOTS + 1, D))
    phase_attention(nc, T)
    phase_experts(nc, T)
    phase_layer1(nc, T)


def constants():
    i = np.arange(P)
    parts = [np.eye(P), np.where(i[None, :] > i[:, None], -HUGE, 0.0), np.where(i[None, :] < i[:, None], -HUGE, 0.0),
             i[:, None] < i[None, :], np.tile(NE - np.arange(NE), (P, NT))]
    return np.concatenate([p.astype(np.float32) for p in parts], axis=1)


def kernel(**inputs):
    import concourse.bacc as bacc
    from concourse.bass_utils import run_bass_kernel_spmd

    g = {k: np.asarray(v) for k, v in inputs.items()}

    def columns(*vectors):
        return np.stack(vectors).reshape(len(vectors), KC, P).transpose(2, 0, 1)

    x = g["L0_attn_x"]
    arrays = {
        "consts": constants(),
        "x": x,
        "xT": x.transpose(0, 2, 1),
        "wq": g["L0_attn_Wq"], "wk": g["L0_attn_Wk"], "wv": g["L0_attn_Wv"], "wo": g["L0_attn_Wo"],
        "bqk": columns(g["L0_attn_bq"], g["L0_attn_bk"]),
        "bv": np.tile(g["L0_attn_bv"], (P, 1)),
        "bo": np.tile(g["L0_attn_bo"], (P, 1)),
        "wg": g["L0_ffn_Wg"], "w1": g["L0_ffn_W1"], "w2": g["L0_ffn_W2"],
        "b1": g["L0_ffn_b1"].reshape(NE, HID // P, P).transpose(0, 2, 1),
        "b2": g["L0_ffn_b2"].reshape(NE, KC, P).transpose(0, 2, 1),
        "w1q": g["L1_attn_Wq"].T, "w1v": g["L1_attn_Wv"].T, "w1o": g["L1_attn_Wo"].T, "w1g": g["L1_attn_Wg"].T,
        "bexp": np.repeat(g["L1_attn_beta"], HD).reshape(KC, P).T,
        "gb": columns(g["L1_attn_ln_gamma"], g["L1_attn_ln_beta"]),
        "wgt": g["L1_ffn_w_gate"].T, "wup": g["L1_ffn_w_up"].T, "wdn": g["L1_ffn_w_down"].T,
    }
    arrays = {"in_" + k: np.ascontiguousarray(v) for k, v in arrays.items()}
    nc = bacc.Bacc("TRN2", target_bir_lowering=False, num_devices=1)
    T = {k[3:]: nc.dram_tensor(k, a.shape, mybir.dt.from_np(a.dtype), kind="ExternalInput").ap()
         for k, a in arrays.items()}
    T["out"] = nc.dram_tensor("out", (NB, S, D), F32, kind="ExternalOutput").ap()
    build(nc, T)
    return run_bass_kernel_spmd(nc, [arrays], core_ids=[0]).results[0]["out"]
```

```python
from contextlib import ExitStack

import numpy as np

import concourse.bass as bass
from concourse import mybir

F32 = mybir.dt.float32
F32R = mybir.dt.float32r
BF16 = mybir.dt.bfloat16
I32 = mybir.dt.int32
U32 = mybir.dt.uint32
ALU = mybir.AluOpType
ACT = mybir.ActivationFunctionType
AX_X = mybir.AxisListType.X

P = 128
NB, S, D = 8, 1024, 256
NH, HD = 16, 16
KC = D // P
NT = S // P
HALF = 512
UH = NH // 2
GH = 4
VS = HD + 1
VW = (NH - 1) * VS + 32
NE, TOPK = 8, 2
CAP = 2151
SLOTS = 2160
EPS = 1e-5
HUGE = 1.0e30

Q_PARTS = (0, 0, 1, 0, 2, 1)
K_PARTS = (0, 1, 0, 2, 0, 1)
NSTACK = len(Q_PARTS) * HD
NROWS = NSTACK + 3

STEPS = 24


def step_block(s):
    grp, r = divmod(s, 12)
    c = 0 if r < 4 else 1
    kb = r if r < 4 else r - 4
    return grp, c, kb, max(0, kb - 4 * c) * P, kb == 4 * c + 3


def max_tiles():
    tiles = [(t, 0, (t + 1) * P, t) for t in range(4)]
    tiles += [(t, 0, HALF, t) for t in range(4, 8)]
    tiles += [(t, HALF, (t - 3) * P, t + 4) for t in range(4, 8)]
    return tiles


MAX_TILES = max_tiles()
GROUP_TILES = [(h, tile) for h in range(GH) for tile in MAX_TILES]

PER_SEQ = {"qk": 8, "v": 4, "g": 8, "m": 4, "ct": 4, "wo": 4, "xt": 4, "lg": 1, "pf": 1}


G_OPS, M_OPS, LG_OPS, PF_OPS, STAT_OPS = 2, 5, 14, 29, 4

CHUNKS = {"qk": (858, 858), "v": (853, 853), "wo": (853, 853), "g": (428,), "ct": (428,), "xt": (428,), "m": (107,),
          "lg": (800,) * 4, "pf": (110,)}
TILE_NS, DVE_SHARE = 215, 0.5


def items_of(g, first, last):
    it = {}

    def put(step, place, kind, const, *what):
        it.setdefault((step, place), []).append((kind, const) + what)

    nxt = not (last and g == 1)
    db, g2 = (0, 1) if g == 0 else (1, 0)
    if nxt:
        for j, (s, pl) in enumerate(((0, 1), (1, 1), (2, 1), (3, 1))):
            put(s, pl, "qk", 8 * db + 4 * g2 + j, db, g2, j)
    if not (first and g == 0):
        put(1, 0, "g", 4 * g - 1, 1 - g, 1, 1)
    put(5, 0, "g", 4 * g, g, 0, 0)
    put(13, 0, "g", 4 * g + 1, g, 0, 1)
    put(17, 0, "g", 4 * g + 2, g, 1, 0)
    put(8, 0, "m", 2 * g + 1, 0, g, 1)
    if nxt:
        put(20, 0, "m", 4 * db + 2 * g2, db, g2, 0)
    if g == 1 and not last:
        for j, s in enumerate((7, 8, 10, 11)):
            put(s, 0, "v", 4 + j, j)
    if g == 0 and not first:
        for j, (s, pl) in enumerate(((2, 0), (3, 0), (4, 0), (4, 1))):
            put(s, pl, "ct", j - 4, j)
        for j, (s, pl) in enumerate(((5, 1), (6, 0), (7, 0), (8, 1))):
            put(s, pl, "wo", j - 4, j)
        for j, (s, pl) in enumerate(((13, 1), (14, 0), (14, 1), (15, 0))):
            put(s, pl, "xt", j - 4, j)
        put(16, 0, "lg", -1)
        put(19, 0, "pf", -1)
    return it


def jobs_of(g, first, last):
    jobs = {}

    def put(step, ns, kind, const, part):
        jobs.setdefault(step, []).append((ns, (kind, const, part)))

    nxt = not (last and g == 1)
    if nxt:
        for j, s in enumerate((1, 2, 3, 4)):
            for n in range(3):
                put(s, 600, "split", 4 * (g + 1) + j, n)
    if g == 0:
        for part, s in ((1, 1), (2, 1), (3, 2)):
            put(s, 350, "v_switch", 0, part)
        if not first:
            for j, s in enumerate((6, 7, 8, 9)):
                for u in range(2):
                    put(s, 540, "stat", j - 4, (j, u))
            put(10, 100, "vare", -1, 0)
            for q, s in enumerate((11, 11, 12, 12)):
                put(s, 650, "norm", -1, q)
            for part, s in ((1, 17), (2, 17)):
                put(s, 900, "lg", -1, part)
            for part, s in enumerate((20, 20, 21, 22, 22)):
                put(s, 900, "pf", -1, part + 1)
    return jobs


def chunks_of(g, s, first, last):
    def share(step):
        return (HALF - step_block(step)[3]) / HALF

    items = items_of(g, first, last)
    diag = 106 if step_block(s)[2] >= 4 * step_block(s)[1] else 0
    half_step = 432 * share(s) + diag
    before = 458 * share((s - 1) % STEPS)
    out = [(half_step, ("scores", 0)), (half_step, ("scores", 1))]
    for place in (0, 1):
        for it in items.get((s, place), []):
            out += [(ns, ("item", it, i)) for i, ns in enumerate(CHUNKS[it[0]])]
        if place == 0 and not (first and g == 0 and s == 0):
            out += [(before, ("values", 0)), (before, ("values", 1))]
    return out


def tile_steps(u):
    def weights(v, steps):
        return [(v, s, max(400.0, sum(ns for ns, _ in chunks_of(v, s, False, False))
                           - DVE_SHARE * sum(ns for ns, _ in jobs_of(v, False, False).get(s, [])))) for s in steps]

    def cut(places):
        total, at, out = sum(w for *_, w in places), 0.0, {}
        for v, s, w in places:
            lo, hi = round(48 * at / total), round(48 * (at + w) / total)
            out[v, s] = (lo, hi)
            at += w
        return out

    return (cut(weights(1 - u, range(20, 24)) + weights(u, range(0, 8))), cut(weights(1 - u, range(8, 20))))


TILE_STEPS = [tile_steps(u) for u in range(2)]
EARLY = TILE_STEPS[0][0][1, 23][1]


def tiles_of(g, s, last):
    db, g2 = (0, 1) if g == 0 else (1, 0)
    if s < 8:
        return [(0, g, 1, k) for k in range(*TILE_STEPS[g][0][g, s])]
    if last and g == 1:
        return []
    grp = 1 if s > 19 else 0
    return [(db, g2, grp, k) for k in range(*TILE_STEPS[g2][1 - grp][g, s])]


def plan_of(g, s, first, last):
    chunks = chunks_of(g, s, first, last)
    total = sum(ns for ns, _ in chunks)
    tiles = tiles_of(g, s, last)
    jobs = [job for _, job in jobs_of(g, first, last).get(s, [])]
    extra = [((k + 0.5) / len(tiles), ("tile", t)) for k, t in enumerate(tiles)]
    extra += [((k + 0.8) / len(jobs), ("job", j)) for k, j in enumerate(jobs)]
    extra.sort(key=lambda e: e[0])
    out, at = [], 0.0
    for ns, what in chunks:
        out.append(what)
        at += ns
        while extra and extra[0][0] * total <= at:
            out.append(extra.pop(0)[1])
    out += [e for _, e in extra]
    if g == 0 and s == 0:
        out.append(("job", ("v_switch", 0, 0)))
    db, g2 = (0, 1) if g == 0 else (1, 0)
    if s == 7:
        out.append(("job", ("gather", 2 * g + 1, (0, g, 1))))
    if s == 19 and not (last and g == 1):
        out.append(("job", ("gather", 4 * db + 2 * g2, (db, g2, 0))))
    return out


def in_order(work):
    out = []
    for w in work:
        out += [("item", w[1], i) for i in range(len(CHUNKS[w[1][0]]))] if w[0] == "item" else [w]
    return out


HEAD = in_order([w for j in range(4) for w in ([("item", ("qk", j, 0, 0, j))] + ([("job", ("split", j - 1, n)) for n in range(3)] if j else []))]
                + [("item", ("v", 0, 0))] + [("job", ("split", 3, n)) for n in range(3)]
                + [("item", ("v", j, j)) for j in range(1, 4)])
TAIL = in_order([("item", ("g", 7, 1, 1, 1))] + [("item", ("ct", j, j)) for j in range(4)]
                + [("item", ("wo", j, j)) for j in range(4)]
                + [("job", ("stat", j, (j, u))) for j in range(4) for u in range(2)] + [("job", ("vare", 0, 0))]
                + [("job", ("norm", 0, q)) for q in range(4)]
                + [("item", ("xt", j, j)) for j in range(4)] + [("item", ("lg", 0))]
                + [("job", ("lg", 0, p)) for p in (1, 2)] + [("item", ("pf", 0))]
                + [("job", ("pf", 0, p)) for p in range(1, 6)])


def count(b, per_seq, const):
    return b * per_seq + const


def wait_apart(eng, semaphore, value):
    if not isinstance(value, int):
        value = eng.to_reg(value)
        eng.wait_ge(semaphore, 1)
    eng.wait_ge(semaphore, value)


def phase_attention(nc, T):
    with ExitStack() as ctx:
        def sb(name, shape, dt=F32):
            return ctx.enter_context(nc.sbuf_tensor("a_" + name, shape, dt))

        def sem(name):
            return ctx.enter_context(nc.semaphore("a_" + name))

        cf = sb("cf", [P, 4 * P + 64])
        identF = cf[:, 0:P]
        cb = sb("cb", [P, 5 * P], BF16)
        identB, maskK, maskQ, before, onesB = (cb[:, i * P:(i + 1) * P] for i in range(5))
        desc = cf[:, 4 * P:4 * P + 64]
        wq, wk, wv, wo = (sb(n, [P, KC, D]) for n in ("wq", "wk", "wv", "wo"))
        wg = sb("wg", [P, KC, NE])
        bqk = sb("bqk", [P, 2, KC])
        bqk_in = sb("bqk_in", [P, 2, KC])
        bv = sb("bv", [P, D])
        bo = sb("bo", [P, D])
        xT = sb("xT", [P, KC, S])
        qk_stack = [[sb(f"stack{s}{t}", [NROWS, UH, S], BF16) for t in range(2)] for s in range(2)]
        v_now = sb("v_now", [P, NT, VW])
        v_next = sb("v_next", [P, NT, VW])
        probs = [sb(f"probs{i}", [P, GH, HALF]) for i in range(2)]
        qf = [sb(f"qf{i}", [P, HALF]) for i in range(2)]
        parts = [sb(f"parts{i}", [P, 3, HALF], BF16) for i in range(2)]
        rest = [sb(f"rest{i}", [P, HALF]) for i in range(2)]
        pmax = sb("pmax", [P, 2, GH, 12])
        mcol = sb("mcol", [P, P])
        nmax = sb("nmax", [32, P])
        nrest = sb("nrest", [32, P])
        nparts = sb("nparts", [32, 3, P], BF16)
        ctx_raw = sb("ctx_raw", [P, HALF])
        rden = sb("rden", [P, 4, GH])
        ctxn = sb("ctxn", [P, NT, D])
        actT = sb("actT", [P, KC, S])
        xb = sb("xb", [P, NT, D])
        x1 = sb("x1", [P, NT, D])
        stats = sb("stats", [P, NT, 6])
        mv = sb("mv", [P, NT, 2])
        vare = sb("vare", [P, NT])
        mhalf = sb("mhalf", [P, NT])
        rstd = sb("rstd", [P, NT])
        zeros = sb("zeros", [P, 2304])
        lg = sb("lg", [P, NT, NE])
        lg2 = sb("lg2", [P, NT, NE])
        sel = sb("sel", [P, NT, NE])
        oh = [sb(f"oh{k}", [P, NT, NE]) for k in range(2)]
        ohb = sb("ohb", [P, NT, NE], BF16)
        top = sb("top", [P, NT, 2])
        pick = sb("pick", [P, NT, 2])
        dlt = sb("dlt", [P, NT])
        expd = sb("expd", [P, NT])
        den = sb("den", [P, NT])
        gates = sb("gates", [P, NT, 2])
        tot = sb("tot", [P, NT, NE])
        base = sb("base", [P, NT + 1, NE])
        pos = sb("pos", [P, NT, NE])
        posk = sb("posk", [P, NT, 2])
        keep = sb("keep", [P, NT, 2])
        drop = sb("drop", [P, NT, 2])
        dest = sb("dest", [P, NT, 2])
        dst_s = sb("dst_s", [P, NT, 2])
        dst_g = sb("dst_g", [P, NT, 2])
        idx_s = sb("idx_s", [P, NT, 2], I32)
        idx_g = sb("idx_g", [P, NT, 2], I32)

        st = ctx.enter_context(nc.psum_tensor("a_st", [P, 4, HALF], F32))
        pv = ctx.enter_context(nc.psum_tensor("a_pv", [P, HALF], F32))
        mx = ctx.enter_context(nc.psum_tensor("a_mx", [P, 2, HALF], F32))
        misc = ctx.enter_context(nc.psum_tensor("a_misc", [P, HALF], F32))

        consts_in = sem("consts_in")
        consts_ready = sem("consts_ready")
        biases_ready = sem("biases_ready")
        ones_ready = sem("ones_ready")
        xT_in = sem("xT_in")
        x_in = sem("x_in")
        xb_ready = sem("xb_ready")
        ready = {k: sem(k + "_ready") for k in PER_SEQ}
        act_took = {k: sem(k + "_copied") for k in ("qk", "ct", "xt")}
        v_taken = sem("v_taken")
        qf_ready = sem("qf_ready")
        split_seq = sem("split_seq")
        parts_out = [sem(f"parts_out{i}") for i in range(2)]
        stack_in = sem("stack_in")
        v_switched = sem("v_switched")
        st_ready = sem("st_ready")
        probs_ready = sem("probs_ready")
        pv_done = sem("pv_done")
        mx_ready = sem("mx_ready")
        mx_done = sem("mx_done")
        mcol_seq = sem("mcol_seq")
        m_seq = sem("m_seq")
        mrow_out = sem("mrow_out")
        mrow_in = sem("mrow_in")
        raw_ready = sem("raw_ready")
        g_seq = sem("g_seq")
        wo_seq = sem("wo_seq")
        stat_seq = sem("stat_seq")
        ve_ready = sem("ve_ready")
        rstd_ready = sem("rstd_ready")
        x1_ready = sem("x1_ready")
        x1_out = sem("x1_out")
        lg_seq = sem("lg_seq")
        pf_seq = sem("pf_seq")
        expd_ready = sem("expd_ready")
        scat = sem("scat")
        route_out = sem("route_out")
        zero_ready = sem("zero_ready")
        cleared = sem("cleared")
        zero_out = sem("zero_out")

        N_CONST = 10
        N_ZERO = 15 + 1
        STACK_DMAS = 4 * 6
        taken = {"qk": (act_took["qk"], 1, 1), "ct": (act_took["ct"], 1, 1), "xt": (act_took["xt"], 1, 1),
                 "v": (v_taken, 1, 1), "g": (g_seq, G_OPS, G_OPS), "m": (m_seq, M_OPS, 1),
                 "wo": (wo_seq, 1, 1), "lg": (lg_seq, LG_OPS, 1), "pf": (pf_seq, PF_OPS, 2)}

        block = ctx.enter_context(nc.Block())

        @block.sync
        def _(sp):
            sp.dma_start(xT[:], T["xT"][0].rearrange("(k p) n -> p k n", p=P)).then_inc(xT_in, 16)
            for dst, src in ((cf[:], T["consts"]), (bqk_in[:], T["bqk"]), (bv[:], T["bv"]), (bo[:], T["bo"]),
                             (wq[:], T["wq"].rearrange("(k p) n -> p k n", p=P)),
                             (wk[:], T["wk"].rearrange("(k p) n -> p k n", p=P)),
                             (wv[:], T["wv"].rearrange("(k p) n -> p k n", p=P)),
                             (wo[:], T["wo"].rearrange("(k p) n -> p k n", p=P)),
                             (wg[:], T["wg"].rearrange("(k p) n -> p k n", p=P))):
                sp.dma_start(dst, src).then_inc(consts_in, 16)

            def parts_write(b, const, j, g2):
                t, n = j % 2, j // 2
                wait_apart(sp, split_seq, count(b, 3 * 8, 3 * (const + 1)))
                sp.dma_start(T["qk_scr"][g2, j].rearrange("r p n -> p r n"), parts[const % 2][:]).then_inc(parts_out[const % 2], 16)

            def stack_read(b, const, j, g2):
                t, n = j % 2, j // 2
                wait_apart(sp, parts_out[const % 2], count(b, 16 * 4, 16 * (const // 2 + 1)))
                for r, part in enumerate((Q_PARTS, K_PARTS)[t]):
                    sp.dma_start(qk_stack[g2][t][r * HD:(r + 1) * HD, :, n * HALF:(n + 1) * HALF],
                                 T["qk_scr"][g2, j, part].rearrange("(i d) n -> d i n", d=HD)).then_inc(stack_in, 16)

            def m_rows(b, const, g2, grp):
                wait_apart(sp, m_seq, count(b, M_OPS * 4, M_OPS * (const + 1)))
                sp.dma_start(T["m_scr"][g2, grp].rearrange("r (a n) -> a r n", a=32), nparts[:]).then_inc(mrow_out, 16)
                wait_apart(sp, mrow_out, count(b, 16 * 4, 16 * (const + 1)))
                sp.dma_start(qk_stack[g2][0][NSTACK:NROWS, grp * GH:(grp + 1) * GH, :],
                             T["m_scr"][g2, grp].rearrange("r (h n) -> r h n", h=GH)).then_inc(mrow_in, 16)

            def stores(b, kind, const):
                if kind == "xt0":
                    wait_apart(sp, x1_ready, b + const + 1)
                    sp.dma_start(T["x1"][b + const].rearrange("(t p) d -> p t d", p=P), x1[:]).then_inc(x1_out, 16)
                if kind == "pf":
                    wait_apart(sp, pf_seq, count(b, PF_OPS, PF_OPS * (const + 1)))
                    sp.dma_start(T["gates"][b + const], gates[:]).then_inc(route_out, 16)
                    sp.dma_start(T["dest"][b + const], idx_g[:]).then_inc(route_out, 16)

            pend = []

            def qk_io(b, item):
                _, const, _, g2, j = item
                parts_write(b, const, j, g2)
                if pend:
                    stack_read(*pend.pop())
                pend.append((b, const, j, g2))

            def flush():
                if pend:
                    stack_read(*pend.pop())

            def run(b, what):
                if what[0] == "job":
                    kind, const, part = what[1]
                    if kind == "split" and part == 2:
                        j, g2 = const % 4, (const // 4) % 2
                        qk_io(b, ("qk", const, 0, g2, j))
                        if j == 3:
                            flush()
                    if kind == "norm" and part == 3:
                        stores(b, "xt0", const)
                    if kind == "pf" and part == 5:
                        stores(b, "pf", const)
                elif what[0] == "item" and what[1][0] == "m":
                    m_rows(b, what[1][1], what[1][3], what[1][4])

            def body(b, first, last):
                for g in range(2):
                    for s in range(STEPS):
                        if s == 0 and not (first and g == 0):
                            wait_apart(sp, pv_done, count(b, 48, 24 * g))
                        for what in plan_of(g, s, first, last):
                            run(b, what)
                        if g == 0 and s == 4 and not last:
                            wait_apart(sp, ready["qk"], count(b, 8, 8))
                            sp.dma_start(xT[:], T["xT"][b + 1].rearrange("(k p) n -> p k n", p=P)).then_inc(xT_in, 16)
                        if g == 1 and s == 0:
                            if not first:
                                wait_apart(sp, wo_seq, count(b, 4, 0))
                                wait_apart(sp, x1_out, count(b, 16, 0))
                                wait_apart(sp, route_out, count(b, 32, 0))
                            sp.dma_start(xb[:], T["x"][b].rearrange("(t p) d -> p t d", p=P)).then_inc(x_in, 16)

            for what in HEAD:
                run(0, what)
            m_rows(0, 0, 0, 0)
            body(0, True, False)
            with sp.Fori(1, NB - 1) as b:
                body(b, False, False)
            body(NB - 1, False, True)
            for what in TAIL:
                run(NB - 1, what)
            wait_apart(sp, x1_out, 16 * NB)
            wait_apart(sp, route_out, 32 * NB)
            wait_apart(sp, scat, 16 * 16 * NB)
            wait_apart(sp, zero_out, 16 * N_ZERO)

        @block.tensor
        def _(pe):
            last_item = [None]

            def mm(out, a, bb, start, stop):
                return pe.matmul(out, a, bb, start=start, stop=stop, skip_group_check=True)

            def chunk(b, it, i):
                kind, const = it[0], it[1]
                if i == 0:
                    if last_item[0] is not None:
                        k0, c0 = last_item[0]
                        read, per, nth = taken[k0]
                        pe.wait_ge(read, count(b, per * PER_SEQ[k0], per * c0 + nth))
                    last_item[0] = (kind, const)
                if kind == "qk":
                    _, _, db, g2, j = it
                    t, n = j % 2, j // 2
                    if j == 0 and i == 0:
                        pe.wait_ge(xT_in, count(b, 16, 16 * (db + 1)))
                    m = mm(misc[:], (wq, wk)[t][:, i, g2 * P:(g2 + 1) * P], xT[:, i, n * HALF:(n + 1) * HALF], i == 0, i == KC - 1)
                elif kind == "v":
                    t = 2 * it[2] + i
                    for k in range(KC):
                        m = mm(misc[:, i * D:(i + 1) * D], xT[:, k, t * P:(t + 1) * P], wv[:, k, :], k == 0, k == KC - 1)
                elif kind == "g":
                    pe.wait_ge(raw_ready, count(b, 8, const + 1))
                    for q in range(4):
                        m = pe.transpose(misc[:, q * P:(q + 1) * P], ctx_raw[:, q * P:(q + 1) * P], identF)
                elif kind == "m":
                    pe.wait_ge(mcol_seq, count(b, 2 * 4, 2 * (const + 1)))
                    m = pe.transpose(misc[:, 0:P], mcol[:], identF)
                elif kind == "ct":
                    j = it[2]
                    pe.wait_ge(g_seq, count(b, 8 * G_OPS, 8 * G_OPS * ((const - j) // 4 + 1)))
                    for q in range(4):
                        m = pe.transpose(misc[:, q * P:(q + 1) * P], ctxn[:, 4 * (j // 2) + q, (j % 2) * P:(j % 2 + 1) * P], identF)
                elif kind == "wo":
                    j = it[2]
                    if i == 0:
                        pe.wait_ge(act_took["ct"], count(b, 4, const - j + 2 * (j // 2) + 2))
                    t = 2 * j + i
                    for k in range(KC):
                        m = mm(misc[:, i * D:(i + 1) * D], actT[:, k, t * P:(t + 1) * P], wo[:, k, :], k == 0, k == KC - 1)
                elif kind == "xt":
                    j = it[2]
                    pe.wait_ge(x1_ready, count(b, 1, (const - j) // 4 + 1))
                    for q in range(4):
                        m = pe.transpose(misc[:, q * P:(q + 1) * P], x1[:, 4 * (j // 2) + q, (j % 2) * P:(j % 2 + 1) * P], identF)
                elif kind == "lg":
                    if i == 0:
                        pe.wait_ge(act_took["xt"], count(b, 4, 4 * const + 4))
                    for t in (2 * i, 2 * i + 1):
                        for k in range(KC):
                            m = mm(misc[:, t * NE:(t + 1) * NE], actT[:, k, t * P:(t + 1) * P], wg[:, k, :], k == 0, k == KC - 1)
                elif kind == "pf":
                    pe.wait_ge(lg_seq, count(b, LG_OPS, LG_OPS * (const + 1)))
                    mm(misc[:, 0:64], before, ohb[:].rearrange("p t e -> p (t e)"), True, True)
                    m = mm(misc[:, 64:128], onesB, ohb[:].rearrange("p t e -> p (t e)"), True, True)
                if i == len(CHUNKS[kind]) - 1:
                    m.then_inc(ready[kind], 1)

            def tiles(b, db, g2, grp, lo, hi):
                for k in range(lo, hi):
                    h, (t, k0, w, col) = GROUP_TILES[k]
                    i = grp * GH + h
                    idx = 192 * db + 96 * g2 + 48 * grp + k
                    if k == 0 and grp == 0:
                        pe.wait_ge(stack_in, count(b, 2 * 16 * STACK_DMAS, 16 * STACK_DMAS * (2 * db + g2 + 1)))
                    if idx >= 2 or not isinstance(b, int) or b > 0:
                        pe.wait_ge(mx_done, count(b, 192, idx - 1))
                    bank = mx[:, idx % 2, 0:w]
                    q, kk = qk_stack[g2]
                    mm(bank, q[0:NSTACK, i, t * P:(t + 1) * P], kk[0:NSTACK, i, k0:k0 + w], True, False) \
                        if k0 + w == (t + 1) * P else \
                        mm(bank, q[0:NSTACK, i, t * P:(t + 1) * P], kk[0:NSTACK, i, k0:k0 + w], True, True).then_inc(mx_ready, 1)
                    if k0 + w == (t + 1) * P:
                        mm(mx[:, idx % 2, w - P:w], identB, maskK, False, True).then_inc(mx_ready, 1)

            def scores(b, g, s, p, n0):
                grp, c, kb, off, _ = step_block(s)
                if p == 0 and s % 12 == 0:
                    pe.wait_ge(mrow_in, count(b, 16 * 4, 16 * (2 * g + grp + 1)))
                if n0 >= 0:
                    pe.wait_ge(probs_ready, count(b, 96, 2 * (24 * g + s - 1) + p + 1))
                q, kk = qk_stack[g]
                for h in range(2):
                    i = grp * GH + 2 * p + h
                    diag = kb >= 4 * c
                    m = mm(st[:, 2 * p + h, off:HALF], kk[0:NROWS, i, kb * P:(kb + 1) * P],
                           q[0:NROWS, i, c * HALF + off:(c + 1) * HALF], True, not diag)
                    if diag:
                        m = mm(st[:, 2 * p + h, off:off + P], identB, maskQ, False, True)
                m.then_inc(st_ready, 1)

            def values(b, g, s, rel, half):
                grp, c, kb, off, is_last = step_block(s)
                if half == 0:
                    if kb == 0:
                        done = 4 * g + 2 * grp + c + (8 * (rel // 48))
                        if not (isinstance(b, int) and b == 0 and done == 0):
                            pe.wait_ge(raw_ready, count(b, 8, done))
                    if g == 0 and grp == 0 and kb % 2 == 0:
                        pe.wait_ge(v_switched, count(b, 4, kb // 2 + 1))
                    pe.wait_ge(probs_ready, count(b, 96, 2 * rel + 2))
                for h in (2 * half, 2 * half + 1):
                    head = g * UH + grp * GH + h
                    m = pe.matmul(pv[32 * h:32 * h + 32, off:HALF], v_now[:, kb, head * VS:head * VS + 32],
                                  probs[rel % 2][:, h, off:HALF], start=kb == 0, stop=is_last, skip_group_check=True)
                if half == 1:
                    m.then_inc(pv_done, 1)

            def body(b, first, last):
                if last_item[0] is not None:
                    k0, c0 = last_item[0]
                    last_item[0] = (k0, c0 - PER_SEQ[k0])
                for g in range(2):
                    for s in range(STEPS):
                        n = 24 * g + s
                        for what in plan_of(g, s, first, last):
                            if what[0] == "scores":
                                scores(b, g, s, what[1], -1 if first and n == 0 else 0)
                            elif what[0] == "item":
                                chunk(b, what[1], what[2])
                            elif what[0] == "tile":
                                db, g2, grp, k = what[1]
                                tiles(b, db, g2, grp, k, k + 1)
                            elif what[0] == "values":
                                values(b, (n - 1) // 24 % 2, (n - 1) % 24, n - 1, what[1])

            pe.wait_ge(consts_in, 16 * 9)
            pe.wait_ge(consts_ready, 1)
            for what in HEAD:
                if what[0] == "item":
                    chunk(0, what[1], what[2])
            pe.wait_ge(ones_ready, 2)
            tiles(0, 0, 0, 0, 0, 48)
            chunk(0, ("m", 0, 0, 0, 0), 0)
            tiles(0, 0, 0, 1, 0, EARLY)
            last_item[0] = ("m", 0 + PER_SEQ["m"])
            body(0, True, False)
            with pe.Fori(1, NB - 1) as b:
                body(b, False, False)
            body(NB - 1, False, True)
            for half in range(2):
                values(NB - 1, 1, 23, 47, half)
            for what in TAIL:
                if what[0] == "item":
                    chunk(NB - 1, what[1], what[2])

        @block.scalar
        def _(act):
            act.wait_ge(consts_in, 16 * 9)
            nc.scalar.activation(bqk[:, 0, :], bqk_in[:, 0, :], ACT.Copy, scale=0.25).then_inc(biases_ready, 1)
            nc.scalar.activation(bqk[:, 1, :], bqk_in[:, 1, :], ACT.Copy).then_inc(biases_ready, 1)
            act.wait_ge(biases_ready, 2)

            def exps(b, g, s, p):
                grp, c, kb, off, _ = step_block(s)
                n = 24 * g + s
                act.wait_ge(st_ready, count(b, 96, 2 * n + p + 1))
                if not (isinstance(b, int) and b == 0 and n < 2):
                    act.wait_ge(pv_done, count(b, 48, n - 1))
                nc.scalar.activation(probs[n % 2][:, 2 * p:2 * p + 2, off:HALF], st[:, 2 * p:2 * p + 2, off:HALF],
                                     ACT.Exp).then_inc(probs_ready, 1)

            def item(b, it):
                kind, const = it[0], it[1]
                if kind == "qk":
                    _, _, db, g2, j = it
                    t = j % 2
                    act.wait_ge(ready["qk"], count(b, 8, const + 1))
                    if not (isinstance(b, int) and b == 0 and const < 2):
                        act.wait_ge(split_seq, count(b, 3 * 8, 3 * (const - 1)))
                        act.wait_ge(parts_out[const % 2], count(b, 16 * 4, 16 * (const // 2)))
                    kw = dict(bias=bqk[:, t, g2:g2 + 1], scale=(0.25, 1.0)[t])
                    nc.scalar.activation(qf[const % 2][:], misc[:], ACT.Identity, **kw).then_inc(qf_ready, 1)
                    nc.scalar.activation(parts[const % 2][:, 0, :], misc[:], ACT.Identity, **kw).then_inc(act_took["qk"], 1)
                if kind in ("ct", "xt"):
                    j = it[2]
                    act.wait_ge(ready[kind], count(b, 4, const + 1))
                    nc.scalar.activation(actT[:, j % 2, (j // 2) * HALF:(j // 2 + 1) * HALF], misc[:], ACT.Copy)\
                        .then_inc(act_took[kind], 1)

            def raw(b, rel, const):
                act.wait_ge(pv_done, count(b, 48, rel + 1))
                nc.scalar.activation(ctx_raw[:], pv[:], ACT.Copy).then_inc(raw_ready, 1)

            def router_exp(b, const):
                act.wait_ge(lg_seq, count(b, LG_OPS, LG_OPS * (const + 1)))
                nc.scalar.activation(expd[:], dlt[:], ACT.Exp).then_inc(expd_ready, 1)

            def run(b, what):
                if what[0] == "item" and what[2] == len(CHUNKS[what[1][0]]) - 1:
                    item(b, what[1])
                if what[0] == "job" and what[1][0] == "lg" and what[1][2] == 2:
                    router_exp(b, what[1][1])

            def body(b, first, last):
                for g in range(2):
                    for s in range(STEPS):
                        n = 24 * g + s
                        for what in plan_of(g, s, first, last):
                            if what[0] == "scores":
                                exps(b, g, s, what[1])
                            elif what == ("values", 1):
                                if s in (4, 12, 16):
                                    raw(b, n - 1, 4 * g + {4: 0, 12: 1, 16: 2}[s])
                                if s == 0 and not (first and g == 0):
                                    raw(b, n - 1, 4 * g - 1)
                            else:
                                run(b, what)

            for what in HEAD:
                run(0, what)
            body(0, True, False)
            with act.Fori(1, NB - 1) as b:
                body(b, False, False)
            body(NB - 1, False, True)
            raw(NB - 1, 47, 7)
            for what in TAIL:
                run(NB - 1, what)

        @block.gpsimd
        def _(pool):
            for s in range(2):
                nc.gpsimd.memset(qk_stack[s][1][NSTACK:NROWS, :, :], 1.0).then_inc(ones_ready, 1)
                pool.wait_ge(ones_ready, s + 1)

            def clear_rows():
                pool.wait_ge(zero_ready, 1)
                flat = T["buf"].rearrange("(p r) d -> p (r d)", p=P)
                for z in range(15):
                    if z % 3 == 0:
                        pool.wait_ge(mrow_in, 16 * (z // 3 + 1))
                    pool.dma_start(flat[:, z * 2304:(z + 1) * 2304], zeros[:]).then_inc(zero_out, 16)
                pool.dma_start(T["y"][NE * SLOTS:NE * SLOTS + 1, :], zeros[0:1, 0:D]).then_inc(zero_out, 16)

            def residual(b):
                pool.wait_ge(x_in, count(b, 16, 16))
                for t in range(NT):
                    ins = nc.gpsimd.tensor_tensor(xb[:, t, :], xb[:, t, :], bo[:], ALU.add)
                ins.then_inc(xb_ready, 1)

            def root(b, const):
                pool.wait_ge(ve_ready, b + const + 1)
                nc.gpsimd.tensor_tensor(rstd[:], vare[:], mhalf[:], ALU.pow).then_inc(rstd_ready, 1)

            def scatter(b, const):
                wait_apart(pool, pf_seq, count(b, PF_OPS, PF_OPS * (const + 1)))
                for t in range(NT):
                    for k in range(TOPK):
                        pool.indirect_dma_start(
                            T["buf"], bass.IndirectOffsetOnAxis(ap=idx_s[:, t, k:k + 1].bitcast(U32), axis=0),
                            x1[:, t, :], None, bounds_check=NE * SLOTS - 1, oob_is_err=False).then_inc(scat, 16)

            pool.wait_ge(ones_ready, 2)
            pool.wait_ge(consts_in, 16 * 9)
            clear_rows()
            residual(0)
            pool.wait_ge(zero_out, 16 * N_ZERO)
            with pool.Fori(1, NB) as b:
                root(b, -1)
                scatter(b, -1)
                wait_apart(pool, scat, count(b, 256, 0))
                residual(b)
            root(NB - 1, 0)
            scatter(NB - 1, 0)

        @block.vector
        def _(dve):
            V = nc.vector

            class Chain:

                def __init__(self, sem_, per_item):
                    self.sem, self.per = sem_, per_item

                def begin(self, b, kind_per, const, done=0):
                    self.b, self.kp, self.c, self.n = b, kind_per, const, done

                def link(self, ins):
                    self.n += 1
                    ins.then_inc(self.sem, 1)
                    wait_apart(dve, self.sem, count(self.b, self.kp * self.per, self.per * self.c + self.n))

                def end(self, ins):
                    self.n += 1
                    ins.then_inc(self.sem, 1)
                    assert self.n == self.per, (self.n, self.per)

            split = Chain(split_seq, 3)
            msplit = Chain(m_seq, M_OPS)
            gch = Chain(g_seq, G_OPS)
            stats_ch = Chain(stat_seq, STAT_OPS)
            lgch = Chain(lg_seq, LG_OPS)
            pfch = Chain(pf_seq, PF_OPS)

            def item(b, it):
                kind, const = it[0], it[1]
                if kind == "v":
                    j = it[2]
                    dve.wait_ge(ready["v"], count(b, 4, const + 1))
                    for u in range(2):
                        t = 2 * j + u
                        ins = V.tensor_tensor(
                            v_next[:, t, 0:NH * VS].rearrange("p (h c) -> p h c", c=VS)[:, :, 0:HD],
                            misc[:, u * D:(u + 1) * D].rearrange("p (h c) -> p h c", c=HD),
                            bv[:].rearrange("p (h c) -> p h c", c=HD), ALU.add)
                    ins.then_inc(v_taken, 1)
                elif kind == "g":
                    _, _, g, grp, c = it
                    dve.wait_ge(ready["g"], count(b, 8, const + 1))
                    if g == 0 and grp == 0 and c == 0 and not (isinstance(b, int) and b == 0):
                        dve.wait_ge(ready["ct"], count(b, 4, 0))
                    gch.begin(b, 8, const)
                    v4 = misc[:].rearrange("p (q h c) -> p q h c", q=4, h=GH)
                    gch.link(V.reciprocal(rden[:], v4[:, :, :, HD]))
                    col = (2 * g + grp) * GH * HD
                    ins = V.tensor_tensor(
                        ctxn[:, 4 * c:4 * c + 4, col:col + GH * HD].rearrange("p q (h c) -> p q h c", h=GH),
                        v4[:, :, :, 0:HD], rden[:].unsqueeze(3).to_broadcast([P, 4, GH, HD]), ALU.mult)
                    gch.end(ins)
                elif kind == "m":
                    _, _, db, g2, grp = it
                    dve.wait_ge(ready["m"], count(b, 4, const + 1))
                    if not (isinstance(b, int) and b == 0 and const == 0):
                        dve.wait_ge(mrow_out, count(b, 64, 16 * const))
                    msplit.begin(b, 4, const)
                    msplit.link(V.tensor_scalar(nmax[:], misc[0:32, 0:P], -1.0, None, ALU.mult))
                    msplit.link(V.tensor_copy(nparts[:, 0, :], nmax[:]))
                    msplit.link(V.tensor_tensor(nrest[:], nmax[:], nparts[:, 0, :], ALU.subtract))
                    msplit.link(V.tensor_copy(nparts[:, 1, :], nrest[:]))
                    msplit.end(V.tensor_tensor(nparts[:, 2, :], nrest[:], nparts[:, 1, :], ALU.subtract))
                elif kind == "wo":
                    j = it[2]
                    dve.wait_ge(ready["wo"], count(b, 4, const + 1))
                    dve.wait_ge(xb_ready, count(b, 1, (const - j) // 4 + 1))
                    V.tensor_tensor(x1[:, 2 * j:2 * j + 2, :], misc[:].rearrange("p (t d) -> p t d", t=2),
                                    xb[:, 2 * j:2 * j + 2, :], ALU.add).then_inc(wo_seq, 1)
                elif kind == "lg":
                    dve.wait_ge(ready["lg"], b + const + 1)
                    lgch.begin(b, 1, const)
                    lgch.link(V.tensor_copy(lg[:], misc[:, 0:64].rearrange("p (t e) -> p t e", t=NT)))
                elif kind == "pf":
                    dve.wait_ge(ready["pf"], b + const + 1)
                    pfch.begin(b, 1, const)
                    pfch.link(V.tensor_copy(tot[:], misc[:, 64:128].rearrange("p (t e) -> p t e", t=NT)))
                    pfch.link(V.tensor_copy(pos[:], misc[:, 0:64].rearrange("p (t e) -> p t e", t=NT)))

            def split_job(b, const, n):
                i = const % 2
                split.begin(b, 8, const, n)
                if n == 0:
                    dve.wait_ge(qf_ready, count(b, 8, const + 1))
                    dve.wait_ge(act_took["qk"], count(b, 8, const + 1))
                    split.link(V.tensor_tensor(rest[i][:], qf[i][:], parts[i][:, 0, :], ALU.subtract))
                elif n == 1:
                    split.link(V.tensor_copy(parts[i][:, 1, :], rest[i][:]))
                else:
                    split.end(V.tensor_tensor(parts[i][:, 2, :], rest[i][:], parts[i][:, 1, :], ALU.subtract))

            def stat_job(b, const, j, u):
                t = 2 * j + u
                dve.wait_ge(wo_seq, count(b, 4, const + 1))
                stats_ch.begin(b, 4, const, 2 * u)
                stats_ch.link(V.bn_stats(stats[:, t, :], x1[:, t, :]))
                last_ = V.bn_aggr(mv[:, t, :], stats[:, t, :])
                stats_ch.end(last_) if u else stats_ch.link(last_)

            def norm_job(b, const, q):
                if q == 0:
                    dve.wait_ge(rstd_ready, b + const + 1)
                for t in (2 * q, 2 * q + 1):
                    ins = V.tensor_scalar(x1[:, t, :], x1[:, t, :], mv[:, t, 0:1], rstd[:, t:t + 1],
                                          ALU.subtract, ALU.mult)
                if q == 3:
                    ins.then_inc(x1_ready, 1)

            def switch_job(b, part):
                if part == 0:
                    if not (isinstance(b, int) and b == 0):
                        dve.wait_ge(pv_done, count(b, 48, 0))
                    dve.wait_ge(v_taken, count(b, 4, 4))
                rows = slice(2 * part, 2 * part + 2)
                V.tensor_copy(v_now[:, rows, :], v_next[:, rows, :]).then_inc(v_switched, 1)

            def lg_job(b, const, part):
                L, shp = lgch, [P, NT, NE]
                d3 = desc.rearrange("p (t e) -> p t e", t=NT)
                k, src = ((0, lg), (1, lg2))[part - 1]
                L.begin(b, 1, const, (1, 6)[k])
                if k:
                    L.link(V.scalar_tensor_tensor(out=lg2[:], in0=oh[0][:], scalar=-3.0e38, in1=lg[:],
                                                  op0=ALU.mult, op1=ALU.add))
                L.link(V.tensor_reduce(top[:, :, k:k + 1], src[:], AX_X, ALU.max))
                L.link(V.tensor_tensor(sel[:], src[:], top[:, :, k:k + 1].to_broadcast(shp), ALU.is_equal))
                L.link(V.tensor_tensor(sel[:], sel[:], d3, ALU.mult))
                L.link(V.tensor_reduce(pick[:, :, k:k + 1], sel[:], AX_X, ALU.max))
                L.link(V.tensor_tensor(oh[k][:], d3, pick[:, :, k:k + 1].to_broadcast(shp), ALU.is_equal))
                if k:
                    L.link(V.tensor_tensor(dlt[:], top[:, :, 1], top[:, :, 0], ALU.subtract))
                    L.end(V.tensor_tensor(ohb[:], oh[0][:], oh[1][:], ALU.add))

            def pf_job(b, const, part):
                Q = pfch
                Q.begin(b, 1, const, (2, 7, 12, 18, 25)[part - 1])
                if part == 1:
                    Q.link(V.tensor_copy(base[:, 0, :], base[:, NT, :]))
                if part in (1, 2):
                    for t in range(4 * (part - 1), 4 * part):
                        Q.link(V.tensor_tensor(base[:, t + 1, :], base[:, t, :], tot[:, t, :], ALU.add))
                if part == 2:
                    Q.link(V.tensor_tensor(pos[:], pos[:], base[:, 0:NT, :], ALU.add))
                if part == 3:
                    for k in range(2):
                        Q.link(V.tensor_tensor(sel[:], oh[k][:], pos[:], ALU.mult))
                        Q.link(V.tensor_reduce(posk[:, :, k:k + 1], sel[:], AX_X, ALU.add))
                    Q.link(V.tensor_scalar(keep[:], posk[:], float(CAP), None, ALU.is_lt))
                    Q.link(V.tensor_scalar(drop[:], keep[:], -1.0, 1.0, ALU.mult, ALU.add))
                if part == 4:
                    Q.link(V.scalar_tensor_tensor(out=dest[:], in0=pick[:], scalar=-float(SLOTS), in1=posk[:],
                                                  op0=ALU.mult, op1=ALU.add))
                    Q.link(V.tensor_scalar(dest[:], dest[:], float(NE * SLOTS), None, ALU.add))
                    Q.link(V.scalar_tensor_tensor(out=dst_s[:], in0=drop[:], scalar=float(NE * SLOTS), in1=dest[:],
                                                  op0=ALU.mult, op1=ALU.add))
                    Q.link(V.tensor_copy(idx_s[:], dst_s[:]))
                    Q.link(V.tensor_tensor(dest[:], dest[:], keep[:], ALU.mult))
                    Q.link(V.scalar_tensor_tensor(out=dst_g[:], in0=drop[:], scalar=float(NE * SLOTS), in1=dest[:],
                                                  op0=ALU.mult, op1=ALU.add))
                    Q.link(V.tensor_copy(idx_g[:], dst_g[:]))
                if part == 5:
                    dve.wait_ge(expd_ready, b + const + 1)
                    Q.link(V.tensor_scalar(den[:], expd[:], 1.0, None, ALU.add))
                    Q.link(V.reciprocal(gates[:, :, 0], den[:]))
                    Q.link(V.tensor_tensor(gates[:, :, 1], gates[:, :, 0], expd[:], ALU.mult))
                    Q.end(V.tensor_tensor(gates[:], gates[:], keep[:], ALU.mult))

            def tiles(b, db, g2, grp, k):
                h, (t, k0, w, col) = GROUP_TILES[k]
                idx = 192 * db + 96 * g2 + 48 * grp + k
                dve.wait_ge(mx_ready, count(b, 192, idx + 1))
                V.tensor_reduce(pmax[:, grp, h, col:col + 1], mx[:, idx % 2, 0:w], AX_X, ALU.max).then_inc(mx_done, 1)

            def gather_max(b, db, g2, grp):
                const = 4 * db + 2 * g2 + grp
                dve.wait_ge(mx_done, count(b, 192, 192 * db + 96 * g2 + 48 * grp + 48))
                if not (isinstance(b, int) and b == 0 and const == 0):
                    dve.wait_ge(ready["m"], count(b, 4, const))
                m3 = mcol[:, 0:32].rearrange("p (h t) -> p h t", h=GH)
                V.tensor_copy(m3[:, :, 0:4], pmax[:, grp, :, 0:4]).then_inc(mcol_seq, 1)
                V.tensor_tensor(m3[:, :, 4:8], pmax[:, grp, :, 4:8], pmax[:, grp, :, 8:12], ALU.max).then_inc(mcol_seq, 1)

            def job(b, kind, const, part):
                if kind == "split":
                    split_job(b, const, part)
                elif kind == "stat":
                    stat_job(b, const, *part)
                elif kind == "vare":
                    dve.wait_ge(stat_seq, count(b, 4 * STAT_OPS, 4 * STAT_OPS * (const + 1)))
                    V.tensor_scalar(vare[:], mv[:, :, 1], EPS, None, ALU.add).then_inc(ve_ready, 1)
                elif kind == "norm":
                    norm_job(b, const, part)
                elif kind == "v_switch":
                    switch_job(b, part)
                elif kind == "lg":
                    lg_job(b, const, part)
                elif kind == "pf":
                    pf_job(b, const, part)
                elif kind == "gather":
                    gather_max(b, *part)

            def run(b, what):
                if what[0] == "item" and what[2] == len(CHUNKS[what[1][0]]) - 1:
                    item(b, what[1])
                elif what[0] == "job":
                    job(b, *what[1])
                elif what[0] == "tile":
                    tiles(b, *what[1])

            def body(b, first, last):
                for g in range(2):
                    for s in range(STEPS):
                        for what in plan_of(g, s, first, last):
                            run(b, what)

            V.memset(zeros[:], 0.0).then_inc(zero_ready, 1)
            V.memset(mcol[:], 0.0).then_inc(cleared, 1)
            V.memset(base[:], 0.0).then_inc(cleared, 1)
            V.memset(v_next[:], 1.0).then_inc(cleared, 1)
            V.memset(mhalf[:], -0.5).then_inc(cleared, 1)
            dve.wait_ge(cleared, 4)
            dve.wait_ge(consts_in, 16 * 9)
            V.tensor_copy(cb[:, 0:4 * P], cf[:, 0:4 * P])
            V.memset(onesB, 1.0).then_inc(consts_ready, 1)
            dve.wait_ge(consts_ready, 1)
            for what in HEAD:
                run(0, what)
            for k in range(48):
                tiles(0, 0, 0, 0, k)
            gather_max(0, 0, 0, 0)
            item(0, ("m", 0, 0, 0, 0))
            for k in range(EARLY):
                tiles(0, 0, 0, 1, k)
            body(0, True, False)
            with dve.Fori(1, NB - 1) as b:
                body(b, False, False)
            body(NB - 1, False, True)
            for what in TAIL:
                run(NB - 1, what)


HID = 1024
MH = HID // P
CH = 432
NCH = SLOTS // CH
SUB = CH // 4


def phase_experts(nc, T):
    with ExitStack() as ctx:
        def sb(name, shape, dt=F32):
            return ctx.enter_context(nc.sbuf_tensor("b_" + name, shape, dt))

        def sem(name):
            return ctx.enter_context(nc.semaphore("b_" + name))

        def psum(name, shape):
            return ctx.enter_context(nc.psum_tensor("b_" + name, shape, F32))

        identF = sb("ident", [P, P])
        raw1 = sb("raw1", [P, KC, HID])
        raw2 = sb("raw2", [P, MH, D])
        w1 = [[sb(f"w1_{s}{p}", [P, KC, HID], F32R) for p in range(2)] for s in range(2)]
        w2 = [[sb(f"w2_{s}{p}", [P, MH, D], F32R) for p in range(2)] for s in range(2)]
        b1 = [sb(f"b1_{s}", [P, MH]) for s in range(2)]
        b2 = [sb(f"b2_{s}", [P, KC]) for s in range(2)]
        xin = [sb(f"xin{i}", [SUB, 4, D]) for i in range(2)]
        xp = [[sb(f"xp{i}{p}", [P, KC, CH], F32R) for p in range(2)] for i in range(2)]
        hf = [sb(f"hf{i}", [P, CH]) for i in range(2)]
        hp = [[sb(f"hp{i}{p}", [P, MH, CH], F32R) for p in range(2)] for i in range(2)]
        yT = [sb(f"yT{i}", [P, KC, CH]) for i in range(2)]
        yo = [sb(f"yo{i}", [SUB, 4, D]) for i in range(2)]
        p_x = psum("p_x", [P, KC, 512])
        p_h = psum("p_h", [P, 2, 512])
        p_y = psum("p_y", [P, KC, 512])
        p_t = psum("p_t", [P, 2, 512])

        ident_in = sem("ident_in")
        raw_in = sem("raw_in")
        bias_in = [sem(f"bias_in{i}") for i in range(2)]
        w_seq = sem("w_seq")
        xin_in = [sem(f"xin_in{i}") for i in range(2)]
        xt_ready = sem("xt_ready")
        xh_ready = sem("xh_ready")
        xl_ready = sem("xl_ready")
        h_ready = sem("h_ready")
        hf_ready = sem("hf_ready")
        hh_ready = sem("hh_ready")
        hl_ready = sem("hl_ready")
        y_ready = sem("y_ready")
        yT_ready = sem("yT_ready")
        yt_ready = sem("yt_ready")
        yo_ready = sem("yo_ready")
        y_out = [sem(f"y_out{i}") for i in range(2)]
        N2 = 2 * NCH
        NALL = NE * NCH

        def rows(i, c):
            return (i * 2 + c // NCH) * SLOTS + (c % NCH) * CH

        block = ctx.enter_context(nc.Block())

        @block.sync
        def _(sp):
            def weights(e, slot, first=False):
                if not first:
                    pass
                sp.dma_start(raw1[:], T["w1"][e].rearrange("(k p) n -> p k n", p=P)).then_inc(raw_in, 16)
                sp.dma_start(raw2[:], T["w2"][e].rearrange("(k p) n -> p k n", p=P)).then_inc(raw_in, 16)
                sp.dma_start(b1[slot][:], T["b1"][e]).then_inc(bias_in[slot], 16)
                sp.dma_start(b2[slot][:], T["b2"][e]).then_inc(bias_in[slot], 16)

            def load(i, c):
                sp.dma_start(xin[c % 2][:], T["buf"][bass.ds(rows(i, c), CH), :].rearrange("(q p) d -> p q d", p=SUB))\
                    .then_inc(xin_in[c % 2], 16)

            def store(i, c):
                wait_apart(sp, yo_ready, count(i, N2, c + 1))
                sp.dma_start(T["y"][bass.ds(rows(i, c) if c >= 0 else rows(i, c + N2) - 2 * SLOTS, CH), :]
                             .rearrange("(q p) d -> p q d", p=SUB), yo[c % 2][:]).then_inc(y_out[c % 2], 16)

            def body(i, first, last):
                for c in range(N2):
                    if not (last and c == N2 - 1):
                        if not (first and c == 0):
                            wait_apart(sp, xt_ready, count(i, N2, c))
                        if c < N2 - 1:
                            load(i, c + 1)
                        else:
                            load(i + 1, 0)
                    if c % NCH == 1 and not (last and c >= NCH):
                        half = c // NCH
                        wait_apart(sp, w_seq, count(i, 16, 8 * (half + 1)))
                        if not (first and half == 0):
                            wait_apart(sp, yT_ready, count(i, 2 * N2, 2 * (half * NCH)))
                        weights(2 * i + half + 1, 1 - half)
                    if c >= 2 or not first:
                        store(i, c - 2)

            sp.dma_start(identF[:], T["consts"][:, 0:P]).then_inc(ident_in, 16)
            weights(0, 0, True)
            load(0, 0)
            body(0, True, False)
            with sp.Fori(1, NE // 2 - 1) as i:
                body(i, False, False)
            body(NE // 2 - 1, False, True)
            store(NE // 2 - 1, N2 - 2)
            store(NE // 2 - 1, N2 - 1)
            wait_apart(sp, y_out[0], 16 * NALL // 2)
            wait_apart(sp, y_out[1], 16 * NALL // 2)

        @block.tensor
        def _(pe):
            def mm(out, a, bb, start, stop):
                return pe.matmul(out, a, bb, start=start, stop=stop)

            def turn_in(i, c):
                pe.wait_ge(xin_in[c % 2], count(i, 16 * NCH, 16 * (c // 2 + 1)))
                if not (isinstance(i, int) and i == 0 and c == 0):
                    pe.wait_ge(xl_ready, count(i, N2, c))
                for k in range(KC):
                    for q in range(4):
                        m = pe.transpose(p_x[:, k, q * SUB:(q + 1) * SUB], xin[c % 2][:, q, k * P:(k + 1) * P],
                                         identF[0:SUB, 0:SUB])
                m.then_inc(xt_ready, 1)

            def turn_out(i, c):
                pe.wait_ge(yT_ready, count(i, 2 * N2, 2 * (c + 1)))
                if not (isinstance(i, int) and i == 0 and c == 0):
                    pe.wait_ge(yo_ready, count(i, N2, c))
                for q in range(4):
                    for k in range(KC):
                        m = pe.transpose(p_t[0:SUB, q // 2, (q % 2) * D + k * P:(q % 2) * D + (k + 1) * P],
                                         yT[c % 2][:, k, q * SUB:(q + 1) * SUB], identF[:])
                m.then_inc(yt_ready, 1)

            def hidden(i, c, m):
                slot = c // NCH
                if m == 0:
                    pe.wait_ge(xl_ready, count(i, N2, c + 1))
                    if c % NCH == 0:
                        pe.wait_ge(w_seq, count(i, 16, 8 * (slot + 1)))
                n = MH * c + m
                if not (isinstance(i, int) and i == 0 and n < 2):
                    pe.wait_ge(hh_ready, count(i, MH * N2, n - 1))
                x = xp[c % 2]
                o = p_h[:, m % 2, 0:CH]
                terms = [(wp, xq, k) for wp, xq in ((0, 0), (0, 1), (1, 0)) for k in range(KC)]
                for t, (wp, xq, k) in enumerate(terms):
                    r = mm(o, w1[slot][wp][:, k, m * P:(m + 1) * P], x[xq][:, k, :], t == 0, t == len(terms) - 1)
                r.then_inc(h_ready, 1)

            def output(i, c, part):
                slot = (c // NCH) % 2
                k, first = part // 4, (part % 4) * 2
                if part % 4 == 0 and not (isinstance(i, int) and i == 0 and c == 0):
                    pe.wait_ge(yT_ready, count(i, 2 * N2, 2 * c + k - 1 + 0) if k else count(i, 2 * N2, 2 * c - 1))
                if part % 4 == 0 and k == 1 and False:
                    pass
                for j in (first, first + 1):
                    if k == 0:
                        pe.wait_ge(hl_ready, count(i, MH * N2, MH * c + j + 1))
                    for t, (wp, hq) in enumerate(((0, 0), (0, 1), (1, 0))):
                        r = mm(p_y[:, k, 0:CH], w2[slot][wp][:, j, k * P:(k + 1) * P], hp[c % 2][hq][:, j, :],
                               j == 0 and t == 0, j == MH - 1 and t == 2)
                if part % 4 == 3:
                    r.then_inc(y_ready, 1)

            def body(i, first, last):
                for c in range(N2):
                    for m in range(MH):
                        hidden(i, c, m)
                        if m == 3 and not (last and c == N2 - 1):
                            turn_in(i, c + 1)
                        if c > 0 or not first:
                            output(i, c - 1, m)
                        if m == 1 and (c > 1 or not first):
                            turn_out(i, c - 2)

            pe.wait_ge(ident_in, 16)
            turn_in(0, 0)
            body(0, True, False)
            with pe.Fori(1, NE // 2 - 1) as i:
                body(i, False, False)
            body(NE // 2 - 1, False, True)
            for part in range(MH):
                if part == 1:
                    turn_out(NE // 2 - 1, N2 - 2)
                output(NE // 2 - 1, N2 - 1, part)
            turn_out(NE // 2 - 1, N2 - 1)

        @block.scalar
        def _(act):
            A = nc.scalar

            def high(i, c):
                act.wait_ge(xt_ready, count(i, N2, c + 1))
                A.activation(xp[c % 2][0][:], p_x[:, :, 0:CH], ACT.Copy).then_inc(xh_ready, 1)

            def gelu(i, c, m):
                n = MH * c + m
                act.wait_ge(h_ready, count(i, MH * N2, n + 1))
                if not (isinstance(i, int) and i == 0 and n < 2):
                    act.wait_ge(hl_ready, count(i, MH * N2, n - 1))
                bias = b1[c // NCH][:, m:m + 1]
                A.activation(hf[m % 2][:], p_h[:, m % 2, 0:CH], ACT.Gelu_apprx_tanh, bias=bias).then_inc(hf_ready, 1)
                A.activation(hp[c % 2][0][:, m, :], p_h[:, m % 2, 0:CH], ACT.Gelu_apprx_tanh, bias=bias).then_inc(hh_ready, 1)

            def out(i, c, k):
                act.wait_ge(y_ready, count(i, 2 * N2, 2 * c + k + 1))
                slot = (c // NCH) % 2
                A.activation(yT[c % 2][:, k, :], p_y[:, k, 0:CH], ACT.Identity, bias=b2[slot][:, k:k + 1]).then_inc(yT_ready, 1)

            def body(i, first, last):
                for c in range(N2):
                    for m in range(MH):
                        if m == 0 and c % NCH == 0:
                            act.wait_ge(bias_in[c // NCH], count(i, 32, 32))
                        if m == 0 and (c > 0 or not first) :
                            pass
                        gelu(i, c, m)
                        if m == 3 and not (last and c == N2 - 1):
                            high(i, c + 1)
                        if m == 3 and (c > 0 or not first):
                            out(i, c - 1, 0)
                    if c > 0 or not first:
                        out(i, c - 1, 1)

            high(0, 0)
            body(0, True, False)
            with act.Fori(1, NE // 2 - 1) as i:
                body(i, False, False)
            body(NE // 2 - 1, False, True)
            out(NE // 2 - 1, N2 - 1, 0)
            out(NE // 2 - 1, N2 - 1, 1)

        @block.vector
        def _(dve):
            V = nc.vector

            def low(i, c):
                dve.wait_ge(xh_ready, count(i, N2, c + 1))
                V.tensor_tensor(xp[c % 2][1][:], p_x[:, :, 0:CH], xp[c % 2][0][:].bitcast(F32), ALU.subtract)\
                    .then_inc(xl_ready, 1)

            def hlow(i, c, m):
                dve.wait_ge(hf_ready, count(i, MH * N2, MH * c + m + 1))
                dve.wait_ge(hh_ready, count(i, MH * N2, MH * c + m + 1))
                V.tensor_tensor(hp[c % 2][1][:, m, :], hf[m % 2][:], hp[c % 2][0][:, m, :].bitcast(F32), ALU.subtract)\
                    .then_inc(hl_ready, 1)

            def rows_out(i, c):
                dve.wait_ge(yt_ready, count(i, N2, c + 1))
                if not (isinstance(i, int) and i == 0 and c < 2):
                    dve.wait_ge(y_out[c % 2], count(i, 16 * NCH, 16 * (c // 2)))
                V.tensor_copy(yo[c % 2][:].rearrange("p (a q) d -> p a (q d)", a=2), p_t[0:SUB, :, :]).then_inc(yo_ready, 1)

            def weights(i, slot, piece):
                if piece == 0:
                    dve.wait_ge(raw_in, count(i, 64, 32 * (slot + 1)))
                w, raw, h = (w1, raw1, slice(piece, piece + 1)) if piece < 2 else (w2, raw2, slice(4 * (piece - 2), 4 * (piece - 1)))
                s = slot % 2
                V.tensor_copy(w[s][0][:, h, :], raw[:, h, :]).then_inc(w_seq, 1)
                dve.wait_ge(w_seq, count(i, 16, 8 * slot + 2 * piece + 1))
                V.tensor_tensor(w[s][1][:, h, :], raw[:, h, :], w[s][0][:, h, :].bitcast(F32), ALU.subtract).then_inc(w_seq, 1)

            def body(i, first, last):
                for c in range(N2):
                    for m in range(MH):
                        hlow(i, c, m)
                        if m == 3 and not (last and c == N2 - 1):
                            low(i, c + 1)
                        if m == 2 and (c > 1 or not first):
                            rows_out(i, c - 2)
                        if m == 5 and c % NCH >= 1 and not (last and c >= NCH):
                            if c % NCH == 1:
                                if not (first and c < NCH):
                                    dve.wait_ge(y_ready, count(i, 2 * N2, 2 * (c - 1)))
                            weights(i, c // NCH + 1, c % NCH - 1)

            for piece in range(4):
                weights(0, 0, piece)
            low(0, 0)
            body(0, True, False)
            with dve.Fori(1, NE // 2 - 1) as i:
                body(i, False, False)
            body(NE // 2 - 1, False, True)
            rows_out(NE // 2 - 1, N2 - 2)
            rows_out(NE // 2 - 1, N2 - 1)


FH = 768
FM = FH // P
N_FF = 2 * FM
SCALE = 1.0 / 127.0
TINY = 1.1754943508222875e-38

C_SEQ = {"xt": 4, "v": 4, "q": 4, "g": 4, "rt": 4, "zt": 4, "wo": 4, "d1": 4, "ff": N_FF, "dn": 4}
RING = {"xt": "turn", "d1": "turn", "rt": "turn", "zt": "turn", "v": "prod", "q": "prod", "g": "prod",
        "wo": "prod", "dn": "prod", "ff": "pair"}
LATE = ("d1", "ff", "dn")


def order(head, tail, combine):
    items = []

    def put(kind, *js):
        for j in js:
            if kind in LATE and head or kind in C_SEQ and kind not in LATE and tail:
                continue
            items.append((kind, j))

    put("xt", 0, 1, 2, 3)
    put("v", 0, 1, 2, 3)
    put("q", 0, 1, 2, 3)
    put("d1", 0, 1, 2, 3)
    put("g", 0, 1, 2, 3)
    put("ff", 0, 1, 2)
    put("rt", 0, 1, 2, 3)
    if not tail:
        items.append(("rt_norm", 0))
    for f in range(3, N_FF):
        put("ff", f)
        if combine and not head and f - 3 < NT:
            items.append(("sum", f - 3))
        if f == 6:
            put("zt", 0, 1, 2, 3)
    if combine and not head:
        items.append(("sum_norm", 0))
    put("dn", 0, 1, 2, 3)
    if not head:
        items.append(("dn_norm", 0))
    put("wo", 0, 1, 2, 3)
    if not tail:
        items.append(("wo_norm", 0))
    if head:
        items += [("sum", t) for t in range(NT)] + [("sum_norm", 0)]
    return items


SUM_OPS, RT_OPS, ADD_OPS = 4, 4, 5
PREP = 16


def run_steps(eng, step):
    step(0, True, False, True, True)
    with eng.Fori(1, NB - 2) as b:
        step(b, False, False, True, True)
    step(NB - 2, False, False, True, False)
    step(NB - 1, False, False, False, False)
    step(NB, False, True, False, False)


def phase_layer1(nc, T):
    with ExitStack() as ctx:
        def sb(name, shape, dt=F32):
            return ctx.enter_context(nc.sbuf_tensor("c_" + name, shape, dt))

        def sem(name):
            return ctx.enter_context(nc.semaphore("c_" + name))

        identF = sb("ident", [P, P])
        wp = {k: [sb(f"w{k}{p}", [P, KC, D], F32R) for p in range(2)] for k in ("q", "v", "g")}
        wo = sb("wo", [P, KC, D])
        wgt = [sb(f"wgt{p}", [P, KC, FH], F32R) for p in range(2)]
        wup = [sb(f"wup{p}", [P, KC, FH], F32R) for p in range(2)]
        wdn = sb("wdn", [P, FM, D])
        gb = sb("gb", [P, 2, KC])
        bexp = sb("bexp", [P, KC])
        lam = sb("lam", [P, KC])
        x1t = sb("x1t", [P, NT, D])
        yg = [sb(f"yg{k}", [P, NT, D]) for k in range(TOPK)]
        gates = sb("gates", [P, NT, TOPK])
        idx = sb("idx", [P, NT, TOPK], I32)
        xn = sb("xn", [P, NT, D])
        x2 = sb("x2", [P, NT, D])
        x3 = sb("x3", [P, NT, D])
        o = sb("o", [P, NT, D])
        xp = [sb(f"xp{p}", [P, KC, S], F32R) for p in range(2)]
        x3p = [sb(f"x3p{p}", [P, KC, S], F32R) for p in range(2)]
        ret = sb("ret", [P, KC, S])
        gT = sb("gT", [P, KC, S])
        rt = sb("rt", [P, NT, D])
        zT = sb("zT", [P, KC, S])
        h = sb("h", [P, FM, S])
        sg = [sb(f"sg{i}", [P, HALF]) for i in range(2)]
        LNS = ("sum", "rt", "wo", "dn")
        stats = {k: sb("stats_" + k, [P, NT, 6]) for k in LNS}
        mv = {k: sb("mv_" + k, [P, NT, 2]) for k in LNS}
        vare = {k: sb("vare_" + k, [P, NT]) for k in LNS}
        rstd = {k: sb("rstd_" + k, [P, NT]) for k in LNS}
        mhalf = sb("mhalf", [P, NT])
        stage = h[:].rearrange("p m n -> p (m n)")

        p_turn = ctx.enter_context(nc.psum_tensor("c_turn", [P, 2, HALF], F32))
        p_prod = ctx.enter_context(nc.psum_tensor("c_prod", [P, 2, HALF], F32))
        p_pair = ctx.enter_context(nc.psum_tensor("c_pair", [P, 2, 2, HALF], F32))

        const_in = sem("const_in")
        stage_in = sem("stage_in")
        stage_seq = sem("stage_seq")
        prep = sem("prep")
        prep_pool = sem("prep_pool")
        lam_exp = sem("lam_exp")
        ready = {k: sem(k + "_ready") for k in C_SEQ}
        act_took = {k: sem(k + "_copied") for k in ("xt", "g", "rt", "zt", "d1")}
        silu_ready = sem("silu_ready")
        xl_ready = sem("xl_ready")
        x3l_ready = sem("x3l_ready")
        scanned = sem("scanned")
        ret_ready = sem("ret_ready")
        h_ready = sem("h_ready")
        z_ready = sem("z_ready")
        seq = {k: sem(k + "_seq") for k in LNS}
        ve_ready = {k: sem(k + "_ve") for k in LNS}
        rstd_ready = {k: sem(k + "_rstd") for k in LNS}
        normed = {k: sem(k + "_normed") for k in LNS}
        gathered = sem("gathered")
        idx_in = sem("idx_in")
        x1_in = sem("x1_in")
        x2_ready = sem("x2_ready")
        o_free = sem("o_free")

        taken = {"xt": (xl_ready, 1, 1), "d1": (x3l_ready, 1, 1), "rt": (act_took["rt"], 1, 1),
                 "zt": (act_took["zt"], 1, 1), "v": (scanned, 1, 1), "q": (ret_ready, 1, 1), "g": (act_took["g"], 1, 1),
                 "wo": (seq["wo"], ADD_OPS, 1), "dn": (seq["dn"], ADD_OPS, 1), "ff": (h_ready, 1, 1)}

        def const_of(kind, j):
            return j - C_SEQ[kind] if kind in LATE else j

        N_STAGE = 9
        block = ctx.enter_context(nc.Block())

        def staged():
            for k in ("q", "v", "g"):
                yield T["w1" + k].rearrange("(k p) n -> p k n", p=P), KC * D, wp[k], False
            for src, dst in ((T["wgt"], wgt), (T["wup"], wup)):
                yield src.rearrange("(k p) n -> p k n", p=P), KC * FH, dst, True
            yield T["wdn"].rearrange("(k p) n -> p k n", p=P), FM * D, wdn, True

        STAGED = list(staged())
        offs, at = [], 0
        for src, cols, dst, integer in STAGED:
            offs.append(at)
            at += cols
        assert at <= FM * S

        @block.sync
        def _(sp):
            def load_idx(b, db):
                sp.dma_start(idx[:], T["dest"][b + db]).then_inc(idx_in, 16)

            def load_x1(b, db):
                sp.dma_start(x1t[:], T["x1"][b + db].rearrange("(t p) d -> p t d", p=P)).then_inc(x1_in, 16)
                sp.dma_start(gates[:], T["gates"][b + db]).then_inc(x1_in, 16)

            load_idx(0, 0)
            for (src, cols, dst, integer), off in zip(STAGED, offs):
                v = stage[:, off:off + cols].rearrange("p (k n) -> p k n", k=src.shape[1])
                sp.dma_start(v.bitcast(I32) if integer else v, src).then_inc(stage_in, 16)
            load_x1(0, 0)
            sp.dma_start(identF[:], T["consts"][:, 0:P]).then_inc(const_in, 16)
            sp.dma_start(gb[:], T["gb"]).then_inc(const_in, 16)
            sp.dma_start(bexp[:], T["bexp"]).then_inc(const_in, 16)
            sp.dma_start(wo[:], T["w1o"].rearrange("(k p) n -> p k n", p=P)).then_inc(const_in, 16)
            wait_apart(sp, gathered, 256)
            load_idx(0, 1)
            wait_apart(sp, normed["sum"], 1)
            load_x1(0, 1)

            def step(b, head, tail, combine, gather):
                if gather:
                    wait_apart(sp, gathered, count(b, 256, 512))
                    load_idx(b, 2)
                    wait_apart(sp, normed["sum"], count(b, 1, 2))
                    load_x1(b, 2)
                if not head:
                    wait_apart(sp, normed["dn"], count(b, 1, 0))
                    sp.dma_start(T["out"][b - 1].rearrange("(t p) d -> p t d", p=P), o[:]).then_inc(o_free, 16)

            run_steps(sp, step)
            wait_apart(sp, o_free, 16 * (NB + 1))

        @block.tensor
        def _(pe):
            hist = {"turn": [], "prod": [], "pair": []}

            def mm(out, a, bb, start, stop):
                return pe.matmul(out, a, bb, start=start, stop=stop, skip_group_check=True)

            def split_product(out, w, x, cols, n, more=False):
                terms = [(a, c, k) for a, c in ((0, 0), (0, 1), (1, 0)) for k in range(KC)]
                for t, (a, c, k) in enumerate(terms):
                    r = mm(out, w[a][:, k, cols], x[c][:, k, n * HALF:(n + 1) * HALF], t == 0, t == len(terms) - 1)
                return r

            def turn(bank, src, j):
                for q in range(4):
                    r = pe.transpose(bank[:, q * P:(q + 1) * P], src[:, 4 * (j // 2) + q, (j % 2) * P:(j % 2 + 1) * P], identF[:])
                return r

            def item(b, kind, j):
                const = const_of(kind, j)
                ring = RING[kind]
                past = hist[ring]
                slot = j % 2
                if len(past) >= 2 and past[-2] is not None:
                    k0, c0 = past[-2]
                    read, per, nth = taken[k0]
                    if not (kind == "ff" and j < 2):
                        pe.wait_ge(read, count(b, per * C_SEQ[k0], per * c0 + nth))
                past.append((kind, const))
                n, m = j // 2, j % 2
                if kind == "xt":
                    if j == 0:
                        pe.wait_ge(normed["sum"], count(b, 1, 1))
                    r = turn(p_turn[:, slot, :], xn, j)
                elif kind == "d1":
                    if j == 0:
                        pe.wait_ge(normed["wo"], count(b, 1, 0))
                    r = turn(p_turn[:, slot, :], x3, j)
                elif kind in ("v", "q", "g"):
                    pe.wait_ge(xl_ready, count(b, 4, 2 * n + 2))
                    r = split_product(p_prod[:, slot, :], wp[kind], xp, slice(m * P, (m + 1) * P), n)
                elif kind == "rt":
                    pe.wait_ge(ret_ready, count(b, 4, 2 * (j // 2) + 2))
                    bank = p_turn[:, slot, :].rearrange("p (t d) -> p t d", t=2)
                    for u in range(2):
                        t = 2 * j + u
                        for k in range(KC):
                            r = pe.transpose(bank[:, u, k * P:(k + 1) * P], ret[:, k, t * P:(t + 1) * P], identF[:])
                elif kind == "zt":
                    if j == 0:
                        pe.wait_ge(normed["rt"], count(b, 1, 1))
                    r = turn(p_turn[:, slot, :], rt, j)
                elif kind == "wo":
                    pe.wait_ge(z_ready, count(b, 4, 2 * (j // 2) + 2))
                    for u in range(2):
                        t = 2 * j + u
                        for k in range(KC):
                            r = mm(p_prod[:, slot, u * D:(u + 1) * D], zT[:, k, t * P:(t + 1) * P], wo[:, k, :], k == 0, k == KC - 1)
                elif kind == "ff":
                    n, m = divmod(j, FM)
                    if m == 0:
                        pe.wait_ge(x3l_ready, count(b, 4, 2 * n + 2 - 4))
                    split_product(p_pair[:, slot, 0, :], wgt, x3p, slice(m * P, (m + 1) * P), n)
                    r = split_product(p_pair[:, slot, 1, :], wup, x3p, slice(m * P, (m + 1) * P), n)
                elif kind == "dn":
                    pe.wait_ge(h_ready, count(b, N_FF, FM * (j // 2 + 1) - N_FF))
                    for u in range(2):
                        t = 2 * j + u
                        for k in range(FM):
                            r = mm(p_prod[:, slot, u * D:(u + 1) * D], h[:, k, t * P:(t + 1) * P], wdn[:, k, :], k == 0, k == FM - 1)
                r.then_inc(ready[kind], 1)

            def step(b, head, tail, combine, gather):
                for ring in hist:
                    hist[ring] = [(k, c - C_SEQ[k]) for k, c in hist[ring][-2:]]
                for kind, j in order(head, tail, combine):
                    if kind in C_SEQ:
                        item(b, kind, j)

            pe.wait_ge(const_in, 64)
            pe.wait_ge(prep, PREP)
            run_steps(pe, step)

        @block.scalar
        def _(act):
            A = nc.scalar
            act.wait_ge(const_in, 64)
            A.activation(lam[:], bexp[:], ACT.Exp, scale=-0.6931471805599453).then_inc(lam_exp, 1)

            def item(b, kind, j):
                const = const_of(kind, j)
                hist_slot = j % 2
                n, m = j // 2, j % 2
                cols = slice(n * HALF, (n + 1) * HALF)
                if kind in ("xt", "d1"):
                    act.wait_ge(ready[kind], count(b, 4, const + 1))
                    A.activation((xp if kind == "xt" else x3p)[0][:, m, cols], p_turn[:, hist_slot, :], ACT.Copy)\
                        .then_inc(act_took[kind], 1)
                elif kind == "g":
                    act.wait_ge(ready[kind], count(b, 4, const + 1))
                    A.activation(gT[:, m, cols], p_prod[:, hist_slot, :], ACT.Silu).then_inc(act_took["g"], 1)
                elif kind == "rt":
                    act.wait_ge(ready[kind], count(b, 4, const + 1))
                    A.activation(rt[:, 2 * j:2 * j + 2, :], p_turn[:, hist_slot, :].rearrange("p (t d) -> p t d", t=2), ACT.Copy)\
                        .then_inc(act_took["rt"], 1)
                elif kind == "zt":
                    act.wait_ge(ready[kind], count(b, 4, const + 1))
                    A.activation(zT[:, m, cols], p_turn[:, hist_slot, :], ACT.Identity,
                                 scale=gb[:, 0, m:m + 1], bias=gb[:, 1, m:m + 1]).then_inc(act_took["zt"], 1)
                elif kind == "ff":
                    act.wait_ge(ready[kind], count(b, N_FF, const + 1))
                    A.activation(sg[j % 2][:], p_pair[:, hist_slot, 0, :], ACT.Silu).then_inc(silu_ready, 1)

            def step(b, head, tail, combine, gather):
                for kind, j in order(head, tail, combine):
                    if kind in C_SEQ:
                        item(b, kind, j)

            run_steps(act, step)

        @block.gpsimd
        def _(pool):
            def gather(b, db):
                wait_apart(pool, idx_in, count(b, 16, 16 * (db + 1)))
                for t in range(NT):
                    for k in range(TOPK):
                        pool.indirect_dma_start(yg[k][:, t, :], None, T["y"],
                                                bass.IndirectOffsetOnAxis(ap=idx[:, t, k:k + 1].bitcast(U32), axis=0))\
                            .then_inc(gathered, 16)

            def root(b, kind, const):
                pool.wait_ge(ve_ready[kind], count(b, 1, const + 1))
                nc.gpsimd.tensor_tensor(rstd[kind][:], vare[kind][:], mhalf[:], ALU.pow).then_inc(rstd_ready[kind], 1)

            def gate(b, j):
                n, m = j // 2, j % 2
                pool.wait_ge(act_took["zt"], count(b, 4, j + 1))
                pool.wait_ge(act_took["g"], count(b, 4, j + 1))
                v = zT[:, m, n * HALF:(n + 1) * HALF]
                nc.gpsimd.tensor_tensor(v, v, gT[:, m, n * HALF:(n + 1) * HALF], ALU.mult).then_inc(z_ready, 1)

            def step(b, head, tail, combine, gather_):
                for kind, j in order(head, tail, combine):
                    if kind == "rt_norm":
                        root(b, "rt", 0)
                    elif kind == "zt" and j == 3:
                        for i in range(4):
                            gate(b, i)
                    elif kind == "sum_norm":
                        root(b, "sum", 1)
                        if gather_:
                            gather(b, 2)
                    elif kind == "dn_norm":
                        root(b, "dn", -1)
                    elif kind == "wo_norm":
                        root(b, "wo", 0)

            nc.gpsimd.memset(mhalf[:], -0.5).then_inc(prep_pool, 1)
            pool.wait_ge(prep_pool, 1)
            gather(0, 0)
            root(0, "sum", 0)
            gather(0, 1)
            run_steps(pool, step)

        @block.vector
        def _(dve):
            V = nc.vector

            def chain(kind, b, per_seq, per, const):
                n = [0]

                def link(ins, last=False):
                    n[0] += 1
                    ins.then_inc(seq[kind], 1)
                    if not last:
                        wait_apart(dve, seq[kind], count(b, per_seq * per, per * const + n[0]))
                    else:
                        assert n[0] == per
                return link

            def stats_of(link, kind, src, tiles):
                for t in tiles:
                    link(V.bn_stats(stats[kind][:, t, :], src[:, t, :]))
                for t in tiles:
                    link(V.bn_aggr(mv[kind][:, t, :], stats[kind][:, t, :]), last=t == tiles[-1])

            def norm(b, kind, const, per, src, dst):
                per_seq = NT if kind == "sum" else 4
                dve.wait_ge(seq[kind], count(b, per_seq * per, per_seq * per * (const + 1)))
                V.tensor_scalar(vare[kind][:], mv[kind][:, :, 1], EPS, None, ALU.add).then_inc(ve_ready[kind], 1)
                dve.wait_ge(rstd_ready[kind], count(b, 1, const + 1))
                for t in range(NT):
                    ins = V.tensor_scalar(dst[:, t, :], src[:, t, :], mv[kind][:, t, 0:1], rstd[kind][:, t:t + 1],
                                          ALU.subtract, ALU.mult)
                ins.then_inc(normed[kind], 1)

            def combine_tile(b, db, t):
                if t == 0:
                    dve.wait_ge(gathered, count(b, 256, 256 * (db + 1)))
                    dve.wait_ge(x1_in, count(b, 32, 32 * (db + 1)))
                link = chain("sum", b, NT, SUM_OPS, NT * db + t)
                for k in range(TOPK):
                    link(V.scalar_tensor_tensor(out=x1t[:, t, :], in0=yg[k][:, t, :], scalar=gates[:, t, k:k + 1],
                                                in1=x1t[:, t, :], op0=ALU.mult, op1=ALU.add))
                stats_of(link, "sum", x1t, [t])

            def item(b, kind, j):
                const = const_of(kind, j)
                slot = j % 2
                n, m = j // 2, j % 2
                cols = slice(n * HALF, (n + 1) * HALF)
                if kind in ("xt", "d1"):
                    hi, lo = xp if kind == "xt" else x3p
                    dve.wait_ge(act_took[kind], count(b, 4, const + 1))
                    V.tensor_tensor(lo[:, m, cols], p_turn[:, slot, :], hi[:, m, cols].bitcast(F32), ALU.subtract)\
                        .then_inc(xl_ready if kind == "xt" else x3l_ready, 1)
                elif kind == "v":
                    dve.wait_ge(ready["v"], count(b, 4, const + 1))
                    if n:
                        dve.wait_ge(scanned, count(b, 4, j - 1))
                    V.tensor_tensor_scan(ret[:, m, cols], lam[:, m:m + 1].to_broadcast([P, HALF]), p_prod[:, slot, :],
                                         ret[:, m, n * HALF - 1:n * HALF] if n else 0.0, ALU.mult, ALU.add)\
                        .then_inc(scanned, 1)
                elif kind == "q":
                    dve.wait_ge(ready["q"], count(b, 4, const + 1))
                    if j == 0:
                        dve.wait_ge(scanned, count(b, 4, 4))
                    V.tensor_tensor(ret[:, m, cols], p_prod[:, slot, :], ret[:, m, cols], ALU.mult).then_inc(ret_ready, 1)
                elif kind == "rt":
                    dve.wait_ge(act_took["rt"], count(b, 4, const + 1))
                    link = chain("rt", b, 4, RT_OPS, const)
                    stats_of(link, "rt", rt, [2 * j, 2 * j + 1])
                elif kind == "ff":
                    n, m = divmod(j, FM)
                    dve.wait_ge(silu_ready, count(b, N_FF, const + 1))
                    V.tensor_tensor(h[:, m, n * HALF:(n + 1) * HALF], p_pair[:, slot, 1, :], sg[j % 2][:], ALU.mult)\
                        .then_inc(h_ready, 1)
                elif kind in ("wo", "dn"):
                    dst, base = (x3, x2) if kind == "wo" else (o, x3)
                    dve.wait_ge(ready[kind], count(b, 4, const + 1))
                    if kind == "dn" and j == 0:
                        dve.wait_ge(o_free, count(b, 16, 0))
                    link = chain(kind, b, 4, ADD_OPS, const)
                    link(V.tensor_tensor(dst[:, 2 * j:2 * j + 2, :], p_prod[:, slot, :].rearrange("p (t d) -> p t d", t=2),
                                         base[:, 2 * j:2 * j + 2, :], ALU.add))
                    stats_of(link, kind, dst, [2 * j, 2 * j + 1])

            def step(b, head, tail, combine, gather):
                if not tail:
                    dve.wait_ge(normed["sum"], count(b, 1, 1))
                    V.tensor_copy(x2[:], xn[:]).then_inc(x2_ready, 1)
                    dve.wait_ge(x2_ready, count(b, 1, 1))
                for kind, j in order(head, tail, combine):
                    if kind in C_SEQ:
                        item(b, kind, j)
                    elif kind == "sum":
                        combine_tile(b, 1, j)
                    elif kind == "sum_norm":
                        norm(b, "sum", 1, SUM_OPS, x1t, xn)
                    elif kind == "rt_norm":
                        norm(b, "rt", 0, RT_OPS, rt, rt)
                    elif kind == "wo_norm":
                        norm(b, "wo", 0, ADD_OPS, x3, x3)
                    elif kind == "dn_norm":
                        norm(b, "dn", -1, ADD_OPS, o, o)

            k = [0]

            def link(ins):
                k[0] += 1
                ins.then_inc(prep, 1)
                dve.wait_ge(prep, k[0])

            dve.wait_ge(lam_exp, 1)
            link(V.tensor_scalar(lam[:], lam[:], -1.0, 1.0, ALU.mult, ALU.add))
            link(V.tensor_scalar(lam[:], lam[:], TINY, 1.0 - 1e-9, ALU.max, ALU.min))
            dve.wait_ge(stage_in, 16 * len(STAGED))
            for (src, cols, dst, integer), off in zip(STAGED, offs):
                raw = stage[:, off:off + cols]
                if integer:
                    link(V.tensor_scalar(raw, raw.bitcast(I32), SCALE, None, ALU.mult))
                if dst is wdn:
                    link(V.tensor_copy(wdn[:].rearrange("p k n -> p (k n)"), raw))
                    continue
                hi, lo = (d[:].rearrange("p k n -> p (k n)") for d in dst)
                link(V.tensor_copy(hi, raw))
                link(V.tensor_tensor(lo, raw, hi.bitcast(F32), ALU.subtract))
            assert k[0] == PREP
            V.memset(o[0:1, 0, 0:1], 0.0).then_inc(o_free, 16)
            for t in range(NT):
                combine_tile(0, 0, t)
            norm(0, "sum", 0, SUM_OPS, x1t, xn)
            run_steps(dve, step)


def build(nc, T):
    def scratch(name, shape, dt=F32):
        return nc.dram_tensor(name, shape, dt, kind="Internal").ap()

    T["qk_scr"] = scratch("qk_scr", (2, 4, 3, P, HALF), BF16)
    T["m_scr"] = scratch("m_scr", (2, 2, 3, GH * S), BF16)
    T["x1"] = scratch("x1", (NB, S, D))
    T["gates"] = scratch("gates", (NB, P, NT, TOPK))
    T["dest"] = scratch("dest", (NB, P, NT, TOPK), I32)
    T["buf"] = scratch("buf", (NE * SLOTS, D))
    T["y"] = scratch("y", (NE * SLOTS + 1, D))
    phase_attention(nc, T)
    phase_experts(nc, T)
    phase_layer1(nc, T)


def constants():
    i = np.arange(P)
    parts = [np.eye(P), np.where(i[None, :] > i[:, None], -HUGE, 0.0), np.where(i[None, :] < i[:, None], -HUGE, 0.0),
             i[:, None] < i[None, :], np.tile(NE - np.arange(NE), (P, NT))]
    return np.concatenate([p.astype(np.float32) for p in parts], axis=1)


def kernel(**inputs):
    import concourse.bacc as bacc
    from concourse.bass_utils import run_bass_kernel_spmd

    g = {k: np.asarray(v) for k, v in inputs.items()}

    def columns(*vectors):
        return np.stack(vectors).reshape(len(vectors), KC, P).transpose(2, 0, 1)

    x = g["L0_attn_x"]
    arrays = {
        "consts": constants(),
        "x": x,
        "xT": x.transpose(0, 2, 1),
        "wq": g["L0_attn_Wq"], "wk": g["L0_attn_Wk"], "wv": g["L0_attn_Wv"], "wo": g["L0_attn_Wo"],
        "bqk": columns(g["L0_attn_bq"], g["L0_attn_bk"]),
        "bv": np.tile(g["L0_attn_bv"], (P, 1)),
        "bo": np.tile(g["L0_attn_bo"], (P, 1)),
        "wg": g["L0_ffn_Wg"], "w1": g["L0_ffn_W1"], "w2": g["L0_ffn_W2"],
        "b1": g["L0_ffn_b1"].reshape(NE, HID // P, P).transpose(0, 2, 1),
        "b2": g["L0_ffn_b2"].reshape(NE, KC, P).transpose(0, 2, 1),
        "w1q": g["L1_attn_Wq"].T, "w1v": g["L1_attn_Wv"].T, "w1o": g["L1_attn_Wo"].T, "w1g": g["L1_attn_Wg"].T,
        "bexp": np.repeat(g["L1_attn_beta"], HD).reshape(KC, P).T,
        "gb": columns(g["L1_attn_ln_gamma"], g["L1_attn_ln_beta"]),
        "wgt": g["L1_ffn_w_gate"].T, "wup": g["L1_ffn_w_up"].T, "wdn": g["L1_ffn_w_down"].T,
    }
    arrays = {"in_" + k: np.ascontiguousarray(v) for k, v in arrays.items()}
    nc = bacc.Bacc("TRN2", target_bir_lowering=False, num_devices=1)
    T = {k[3:]: nc.dram_tensor(k, a.shape, mybir.dt.from_np(a.dtype), kind="ExternalInput").ap()
         for k, a in arrays.items()}
    T["out"] = nc.dram_tensor("out", (NB, S, D), F32, kind="ExternalOutput").ap()
    build(nc, T)
    return run_bass_kernel_spmd(nc, [arrays], core_ids=[0]).results[0]["out"]
```

```python
from contextlib import ExitStack

import numpy as np

import concourse.bass as bass
from concourse import mybir

F32 = mybir.dt.float32
F32R = mybir.dt.float32r
BF16 = mybir.dt.bfloat16
I32 = mybir.dt.int32
U32 = mybir.dt.uint32
ALU = mybir.AluOpType
ACT = mybir.ActivationFunctionType
AX_X = mybir.AxisListType.X

P = 128
NB, S, D = 8, 1024, 256
NH, HD = 16, 16
KC = D // P
NT = S // P
HALF = 512
UH = NH // 2
GH = 4
VS = HD + 1
VW = (NH - 1) * VS + 32
NE, TOPK = 8, 2
CAP = 2151
SLOTS = 2160
EPS = 1e-5
HUGE = 1.0e30

Q_PARTS = (0, 0, 1, 0, 2, 1)
K_PARTS = (0, 1, 0, 2, 0, 1)
NSTACK = len(Q_PARTS) * HD
NROWS = NSTACK + 3

STEPS = 24


def step_block(s):
    grp, r = divmod(s, 12)
    c = 0 if r < 4 else 1
    kb = r if r < 4 else r - 4
    return grp, c, kb, max(0, kb - 4 * c) * P, kb == 4 * c + 3


def max_tiles():
    blocks = [(t, 0, (t + 1) * P, t) for t in range(4)]
    blocks += [(t, 0, HALF, t) for t in range(4, 8)]
    blocks += [(t, HALF, (t - 3) * P, t + 4) for t in range(4, 8)]
    tiles = []
    for t, k0, w, col in blocks:
        n = max(1, HALF // w)
        tiles += [(range(h, h + n), t, k0, w, col) for h in range(0, GH, n)]
    return tiles


GROUP_TILES = max_tiles()
NM = len(GROUP_TILES)

PER_SEQ = {"qk": 8, "v": 4, "g": 8, "m": 4, "ct": 4, "wo": 4, "xt": 4, "lg": 1, "pf": 1}


G_OPS, M_OPS, LG_OPS, PF_OPS, STAT_OPS = 2, 5, 14, 18, 4
LG_PARTS, PF_PARTS = 4, 4
PF_PLACES = 13

CHUNKS = {"qk": (4 * HALF,) * KC, "v": (4 * KC * D,) * 2, "wo": (4 * KC * D,) * 2, "g": (2 * HALF,), "ct": (2 * HALF,),
          "xt": (2 * HALF,), "m": (2 * P,), "lg": (4 * 4 * P,) * 4, "pf": (2 * P,)}
FLOOR = 7 * HALF


def items_of(g, first, last):
    it = {}

    def put(step, place, kind, const, *what):
        it.setdefault((step, place), []).append((kind, const) + what)

    nxt = not (last and g == 1)
    db, g2 = (0, 1) if g == 0 else (1, 0)
    if nxt:
        for j, (s, pl) in enumerate(((0, 1), (1, 1), (2, 1), (3, 1))):
            put(s, pl, "qk", 8 * db + 4 * g2 + j, db, g2, j)
    if not (first and g == 0):
        put(1, 0, "g", 4 * g - 1, 1 - g, 1, 1)
    put(7, 0, "g", 4 * g, g, 0, 0)
    put(13, 0, "g", 4 * g + 1, g, 0, 1)
    put(17, 0, "g", 4 * g + 2, g, 1, 0)
    put(8, 0, "m", 2 * g + 1, 0, g, 1)
    if nxt:
        put(20, 0, "m", 4 * db + 2 * g2, db, g2, 0)
    if g == 1 and not last:
        for j, s in enumerate((6, 9, 10, 11)):
            put(s, 0, "v", 4 + j, j)
    if g == 0 and not first:
        for j, (s, pl) in enumerate(((4, 1), (5, 0), (5, 1), (6, 0))):
            put(s, pl, "ct", j - 4, j)
        for j, (s, pl) in enumerate(((6, 1), (7, 1), (9, 0), (10, 0))):
            put(s, pl, "wo", j - 4, j)
        for j, (s, pl) in enumerate(((15, 1), (16, 0), (16, 1), (18, 0))):
            put(s, pl, "xt", j - 4, j)
        put(19, 0, "lg", -1)
    if g == 1 and not first:
        put(4, 0, "pf", -1)
    return it


def jobs_of(g, first, last):
    jobs = {}

    def put(step, kind, const, part):
        jobs.setdefault(step, []).append((kind, const, part))

    nxt = not (last and g == 1)
    if nxt:
        for j, s in enumerate((1, 2, 3, 4)):
            for n in range(3):
                put(s, "split", 4 * (g + 1) + j, n)
    if g == 0:
        for part, s in ((1, 1), (2, 1), (3, 2)):
            put(s, "v_switch", 0, part)
        if not first:
            for j, s in enumerate((7, 8, 10, 11)):
                for u in range(2):
                    put(s, "stat", j - 4, (j, u))
            put(12, "vare", -1, 0)
            for q, s in enumerate((12, 13, 13, 14)):
                put(s, "norm", -1, q)
            for part, s in enumerate((20, 21, 22, 23)):
                put(s, "lg", -1, part + 1)
    if g == 1 and not first:
        for part, s in enumerate((5, 5, 6, 7)):
            put(s, "pf", -1, part + 1)
    return jobs


def chunks_of(g, s, first, last):
    def queries(step):
        return HALF - step_block(step)[3]

    items = items_of(g, first, last)
    _, c, kb, _, _ = step_block(s)
    half_step = 2 * queries(s) + (2 * P if kb >= 4 * c else 0)
    before = 2 * queries((s - 1) % STEPS)
    out = [(half_step, ("scores", 0)), (half_step, ("scores", 1))]
    for place in (0, 1):
        for it in items.get((s, place), []):
            out += [(columns, ("item", it, i, 0)) for i, columns in enumerate(CHUNKS[it[0]])]
        if place == 0 and not (first and g == 0 and s == 0):
            out += [(before, ("values", 0)), (before, ("values", 1))]
    return out


def tile_steps(u):
    def weights(v, steps):
        return [(v, s, max(FLOOR, sum(columns for columns, _ in chunks_of(v, s, False, False)))) for s in steps]

    def cut(places):
        total, at, out = sum(w for *_, w in places), 0.0, {}
        for v, s, w in places:
            lo, hi = round(NM * at / total), round(NM * (at + w) / total)
            out[v, s] = (lo, hi)
            at += w
        return out

    return (cut(weights(1 - u, range(20, 24)) + weights(u, range(0, 8))), cut(weights(1 - u, range(8, 20))))


TILE_STEPS = [tile_steps(u) for u in range(2)]
EARLY = TILE_STEPS[0][0][1, 23][1]


def tiles_of(g, s, last):
    db, g2 = (0, 1) if g == 0 else (1, 0)
    if s < 8:
        return [(0, g, 1, k) for k in range(*TILE_STEPS[g][0][g, s])]
    if last and g == 1:
        return []
    grp = 1 if s > 19 else 0
    return [(db, g2, grp, k) for k in range(*TILE_STEPS[g2][1 - grp][g, s])]


def plan_of(g, s, first, last):
    chunks = chunks_of(g, s, first, last)
    total = sum(columns for columns, _ in chunks)
    tiles = tiles_of(g, s, last)
    jobs = jobs_of(g, first, last).get(s, [])
    extra = [((k + 0.3) / len(tiles), ("tile", t)) for k, t in enumerate(tiles)]
    extra += [((k + 0.8) / len(jobs), ("job", j)) for k, j in enumerate(jobs)]
    extra.sort(key=lambda e: e[0])
    out, at = [], 0.0
    for columns, what in chunks:
        out.append(what)
        at += columns
        while extra and extra[0][0] * total <= at:
            out.append(extra.pop(0)[1])
    out += [e for _, e in extra]
    if g == 0 and s == 0:
        out.append(("job", ("v_switch", 0, 0)))
    db, g2 = (0, 1) if g == 0 else (1, 0)
    if s == 7:
        out.append(("job", ("gather", 2 * g + 1, (0, g, 1))))
    if s == 19 and not (last and g == 1):
        out.append(("job", ("gather", 4 * db + 2 * g2, (db, g2, 0))))
    return out


def in_order(work, banks):
    out, n = [], 0
    for w in work:
        if w[0] == "item":
            out += [("item", w[1], i, n % banks) for i in range(len(CHUNKS[w[1][0]]))]
            n += 1
        else:
            out.append(w)
    return out


def head_of_qk(j):
    return [("item", ("qk", j, 0, 0, j))] + ([("job", ("split", j - 1, n)) for n in range(3)] if j else [])


HEAD = in_order([w for j in range(4) for w in head_of_qk(j)]
                + [("item", ("v", 0, 0))] + [("job", ("split", 3, n)) for n in range(3)]
                + [("item", ("v", j, j)) for j in range(1, 4)], 2)
TAIL = in_order([("item", ("g", 7, 1, 1, 1))] + [("item", ("ct", j, j)) for j in range(4)]
                + [w for j in range(4) for w in (("item", ("wo", j, j)), ("job", ("stat", j, (j, 0))), ("job", ("stat", j, (j, 1))))]
                + [("job", ("vare", 0, 0))]
                + [("job", ("norm", 0, q)) for q in range(4)]
                + [("item", ("xt", j, j)) for j in range(4)] + [("item", ("lg", 0))]
                + [("job", ("lg", 0, p)) for p in range(1, LG_PARTS + 1)] + [("item", ("pf", 0))]
                + [("job", ("pf", 0, p)) for p in range(1, PF_PARTS + 1)], 2)


def count(b, per_seq, const):
    return b * per_seq + const


def wait_apart(eng, semaphore, value):
    if not isinstance(value, int):
        value = eng.to_reg(value)
        eng.wait_ge(semaphore, 1)
    eng.wait_ge(semaphore, value)


def phase_attention(nc, T, load_ahead=None):
    with ExitStack() as ctx:
        def sb(name, shape, dt=F32):
            return ctx.enter_context(nc.sbuf_tensor("a_" + name, shape, dt))

        def sem(name):
            return ctx.enter_context(nc.semaphore("a_" + name))

        cf = sb("cf", [P, 4 * P + 64])
        identF = cf[:, 0:P]
        cb = sb("cb", [P, 5 * P], BF16)
        identB, maskK, maskQ, before, onesB = (cb[:, i * P:(i + 1) * P] for i in range(5))
        desc = cf[:, 4 * P:4 * P + 64]
        wq, wk, wv, wo = (sb(n, [P, KC, D]) for n in ("wq", "wk", "wv", "wo"))
        wg = sb("wg", [P, KC, NE])
        bqk = sb("bqk", [P, 2, KC])
        bqk_in = sb("bqk_in", [P, 2, KC])
        bv = sb("bv", [P, D])
        bo = sb("bo", [P, D])
        xT = sb("xT", [P, KC, S])
        qk_stack = [[sb(f"stack{s}{t}", [NROWS, UH, S], BF16) for t in range(2)] for s in range(2)]
        v_now = sb("v_now", [P, NT, VW])
        v_next = sb("v_next", [P, NT, VW])
        probs = [sb(f"probs{i}", [P, GH, HALF]) for i in range(2)]
        qf = [sb(f"qf{i}", [P, HALF]) for i in range(2)]
        parts = [sb(f"parts{i}", [P, 3, HALF], BF16) for i in range(2)]
        rest = [sb(f"rest{i}", [P, HALF]) for i in range(2)]
        pmax = sb("pmax", [P, 2, GH, 12])
        mcol = sb("mcol", [P, P])
        nmax = sb("nmax", [32, P])
        nrest = sb("nrest", [32, P])
        nparts = sb("nparts", [32, 3, P], BF16)
        ctx_raw = sb("ctx_raw", [P, HALF])
        rden = sb("rden", [P, 4, GH])
        ctxn = sb("ctxn", [P, NT, D])
        actT = sb("actT", [P, KC, S])
        xb = sb("xb", [P, NT, D])
        x1 = sb("x1", [P, NT, D])
        stats = sb("stats", [P, NT, 6])
        mv = sb("mv", [P, NT, 2])
        vare = sb("vare", [P, NT])
        mhalf = sb("mhalf", [P, NT])
        rstd = sb("rstd", [P, NT])
        zeros = sb("zeros", [P, 2304])
        lg = sb("lg", [P, NT, NE])
        lg2 = sb("lg2", [P, NT, NE])
        sel = sb("sel", [P, NT, NE])
        oh = [sb(f"oh{k}", [P, NT, NE]) for k in range(2)]
        ohb = sb("ohb", [P, NT, NE], BF16)
        top = sb("top", [P, NT, 2])
        pick = sb("pick", [P, NT, 2])
        dlt = sb("dlt", [P, NT])
        expd = sb("expd", [P, NT])
        den = sb("den", [P, NT])
        gates = sb("gates", [P, NT, 2])
        tot = sb("tot", [P, NE, NT + 1])
        base = sb("base", [P, NE, NT + 1])
        anew = sb("anew", [P, NE, NT + 1])
        pos = sb("pos", [P, NT, NE])
        posk = sb("posk", [P, NT, 2])
        keep = sb("keep", [P, NT, 2])
        dest = sb("dest", [P, NT, 2])
        idx_s = sb("idx_s", [P, NT, 2], I32)
        idx_g = sb("idx_g", [P, NT, 2], I32)

        st = ctx.enter_context(nc.psum_tensor("a_st", [P, 4, HALF], F32))
        pv = ctx.enter_context(nc.psum_tensor("a_pv", [P, HALF], F32))
        mx = ctx.enter_context(nc.psum_tensor("a_mx", [P, 2, HALF], F32))
        misc = ctx.enter_context(nc.psum_tensor("a_misc", [P, HALF], F32))

        qk_consts_in = sem("qk_consts_in")
        consts_in = sem("consts_in")
        consts_ready = sem("consts_ready")
        biases_ready = sem("biases_ready")
        ones_ready = sem("ones_ready")
        xT_in = sem("xT_in")
        x_in = sem("x_in")
        xb_ready = sem("xb_ready")
        ready = {k: sem(k + "_ready") for k in PER_SEQ}
        act_took = {k: sem(k + "_copied") for k in ("qk", "ct", "xt")}
        v_taken = sem("v_taken")
        qf_ready = sem("qf_ready")
        split_seq = sem("split_seq")
        parts_out = [sem(f"parts_out{i}") for i in range(2)]
        stack_in = sem("stack_in")
        v_switched = sem("v_switched")
        st_ready = sem("st_ready")
        probs_ready = sem("probs_ready")
        pv_done = sem("pv_done")
        mx_ready = sem("mx_ready")
        mx_done = sem("mx_done")
        mcol_seq = sem("mcol_seq")
        m_seq = sem("m_seq")
        mrow_out = sem("mrow_out")
        mrow_in = sem("mrow_in")
        raw_ready = sem("raw_ready")
        g_seq = sem("g_seq")
        wo_seq = sem("wo_seq")
        stat_seq = sem("stat_seq")
        ve_ready = sem("ve_ready")
        rstd_ready = sem("rstd_ready")
        x1_ready = sem("x1_ready")
        x1_out = sem("x1_out")
        lg_seq = sem("lg_seq")
        pf_seq = sem("pf_seq")
        expd_ready = sem("expd_ready")
        scat = sem("scat")
        route_out = sem("route_out")
        zero_ready = sem("zero_ready")
        cleared = sem("cleared")
        zero_out = sem("zero_out")

        N_QK_CONST, N_CONST = 3, 6
        ZERO_COLS = zeros.shape[1]
        N_CLEAR = NE * SLOTS // P * D // ZERO_COLS
        N_ZERO = N_CLEAR + 1
        STACK_DMAS = 4 * 6
        taken = {"qk": (act_took["qk"], 1, 1), "ct": (act_took["ct"], 1, 1), "xt": (act_took["xt"], 1, 1),
                 "v": (v_taken, 1, 1), "g": (g_seq, G_OPS, G_OPS), "m": (m_seq, M_OPS, 1),
                 "wo": (wo_seq, 1, 1), "lg": (lg_seq, LG_OPS, 1), "pf": (pf_seq, PF_OPS, 2)}

        item_banks = (misc[:], mx[:, 0, :])

        def max_bank(idx, start):
            return st[:, idx % 4, :] if start else mx[:, idx % 2, :]

        block = ctx.enter_context(nc.Block())

        @block.sync
        def _(sp):
            sp.dma_start(xT[:], T["xT"][0].rearrange("(k p) n -> p k n", p=P)).then_inc(xT_in, 16)
            for dst, src in ((bqk_in[:], T["bqk"]),
                             (wq[:], T["wq"].rearrange("(k p) n -> p k n", p=P)),
                             (wk[:], T["wk"].rearrange("(k p) n -> p k n", p=P))):
                sp.dma_start(dst, src).then_inc(qk_consts_in, 16)
            for dst, src in ((wv[:], T["wv"].rearrange("(k p) n -> p k n", p=P)), (cf[:], T["consts"]),
                             (bv[:], T["bv"]), (bo[:], T["bo"]),
                             (wo[:], T["wo"].rearrange("(k p) n -> p k n", p=P)),
                             (wg[:], T["wg"].rearrange("(k p) n -> p k n", p=P))):
                sp.dma_start(dst, src).then_inc(consts_in, 16)

            def parts_write(b, const, j, g2):
                wait_apart(sp, split_seq, count(b, 3 * 8, 3 * (const + 1)))
                sp.dma_start(T["qk_scr"][g2, j].rearrange("r p n -> p r n"), parts[const % 2][:]).then_inc(parts_out[const % 2], 16)

            def stack_read(b, const, j, g2):
                t, n = j % 2, j // 2
                wait_apart(sp, parts_out[const % 2], count(b, 16 * 4, 16 * (const // 2 + 1)))
                for r, part in enumerate((Q_PARTS, K_PARTS)[t]):
                    sp.dma_start(qk_stack[g2][t][r * HD:(r + 1) * HD, :, n * HALF:(n + 1) * HALF],
                                 T["qk_scr"][g2, j, part].rearrange("(i d) n -> d i n", d=HD)).then_inc(stack_in, 16)

            def m_rows(b, const, g2, grp):
                wait_apart(sp, m_seq, count(b, M_OPS * 4, M_OPS * (const + 1)))
                sp.dma_start(T["m_scr"][g2, grp].rearrange("r (a n) -> a r n", a=32), nparts[:]).then_inc(mrow_out, 16)
                wait_apart(sp, mrow_out, count(b, 16 * 4, 16 * (const + 1)))
                sp.dma_start(qk_stack[g2][0][NSTACK:NROWS, grp * GH:(grp + 1) * GH, :],
                             T["m_scr"][g2, grp].rearrange("r (h n) -> r h n", h=GH)).then_inc(mrow_in, 16)

            def store_rows(b, const):
                wait_apart(sp, x1_ready, b + const + 1)
                sp.dma_start(T["x1"][b + const].rearrange("(t p) d -> p t d", p=P), x1[:]).then_inc(x1_out, 16)

            def store_routes(b, const):
                wait_apart(sp, pf_seq, count(b, PF_OPS, PF_OPS * (const + 1)))
                sp.dma_start(T["gates"][b + const], gates[:]).then_inc(route_out, 16)
                sp.dma_start(T["dest"][b + const], idx_g[:]).then_inc(route_out, 16)

            def run(b, what):
                if what[0] == "job":
                    kind, const, part = what[1]
                    if kind == "split" and part == 2:
                        j, g2 = const % 4, (const // 4) % 2
                        parts_write(b, const, j, g2)
                        if j > 0:
                            stack_read(b, const - 1, j - 1, g2)
                        if j == 3:
                            stack_read(b, const, j, g2)
                    if kind == "norm" and part == 3:
                        store_rows(b, const)
                    if kind == "pf" and part == PF_PARTS:
                        store_routes(b, const)
                elif what[0] == "item" and what[1][0] == "m":
                    m_rows(b, what[1][1], what[1][3], what[1][4])

            def body(b, first, last):
                for g in range(2):
                    for s in range(STEPS):
                        if s == 0 and not (first and g == 0):
                            wait_apart(sp, pv_done, count(b, 48, 24 * g))
                        for what in plan_of(g, s, first, last):
                            run(b, what)
                        if g == 0 and s == 4 and not last:
                            wait_apart(sp, ready["qk"], count(b, 8, 8))
                            sp.dma_start(xT[:], T["xT"][b + 1].rearrange("(k p) n -> p k n", p=P)).then_inc(xT_in, 16)
                        if g == 1 and s == 8:
                            if not first:
                                wait_apart(sp, wo_seq, count(b, 4, 0))
                                wait_apart(sp, x1_out, count(b, 16, 0))
                                wait_apart(sp, route_out, count(b, 32, 0))
                            sp.dma_start(xb[:], T["x"][b].rearrange("(t p) d -> p t d", p=P)).then_inc(x_in, 16)

            for what in HEAD:
                run(0, what)
            m_rows(0, 0, 0, 0)
            body(0, True, False)
            with sp.Fori(1, NB - 1) as b:
                body(b, False, False)
            body(NB - 1, False, True)
            if load_ahead:
                load_ahead(sp)
            for what in TAIL:
                run(NB - 1, what)
            wait_apart(sp, x1_out, 16 * NB)
            wait_apart(sp, route_out, 32 * NB)
            wait_apart(sp, scat, 16 * 16 * NB)
            wait_apart(sp, zero_out, 16 * N_ZERO)

        @block.tensor
        def _(pe):
            last_item = [None, None]

            def mm(out, a, bb, start, stop):
                return pe.matmul(out, a, bb, start=start, stop=stop, skip_group_check=True)

            def chunk(b, it, i, place=0):
                kind, const = it[0], it[1]
                bank = item_banks[place]
                if i == 0:
                    if last_item[place] is not None:
                        k0, c0 = last_item[place]
                        read, per, nth = taken[k0]
                        pe.wait_ge(read, count(b, per * PER_SEQ[k0], per * c0 + nth))
                    last_item[place] = (kind, const)
                if kind == "qk":
                    _, _, db, g2, j = it
                    t, n = j % 2, j // 2
                    if j == 0 and i == 0:
                        pe.wait_ge(xT_in, count(b, 16, 16 * (db + 1)))
                    m = mm(bank, (wq, wk)[t][:, i, g2 * P:(g2 + 1) * P], xT[:, i, n * HALF:(n + 1) * HALF], i == 0, i == KC - 1)
                elif kind == "v":
                    t = 2 * it[2] + i
                    for k in range(KC):
                        m = mm(bank[:, i * D:(i + 1) * D], xT[:, k, t * P:(t + 1) * P], wv[:, k, :], k == 0, k == KC - 1)
                elif kind == "g":
                    pe.wait_ge(raw_ready, count(b, 8, const + 1))
                    for q in range(4):
                        m = pe.transpose(bank[:, q * P:(q + 1) * P], ctx_raw[:, q * P:(q + 1) * P], identF)
                elif kind == "m":
                    pe.wait_ge(mcol_seq, count(b, 2 * 4, 2 * (const + 1)))
                    m = pe.transpose(bank[:, 0:P], mcol[:], identF)
                elif kind == "ct":
                    j = it[2]
                    pe.wait_ge(g_seq, count(b, 8 * G_OPS, 8 * G_OPS * ((const - j) // 4 + 1)))
                    for q in range(4):
                        m = pe.transpose(bank[:, q * P:(q + 1) * P], ctxn[:, 4 * (j // 2) + q, (j % 2) * P:(j % 2 + 1) * P], identF)
                elif kind == "wo":
                    j = it[2]
                    if i == 0:
                        pe.wait_ge(act_took["ct"], count(b, 4, const - j + 2 * (j // 2) + 2))
                    t = 2 * j + i
                    for k in range(KC):
                        m = mm(bank[:, i * D:(i + 1) * D], actT[:, k, t * P:(t + 1) * P], wo[:, k, :], k == 0, k == KC - 1)
                elif kind == "xt":
                    j = it[2]
                    pe.wait_ge(x1_ready, count(b, 1, (const - j) // 4 + 1))
                    for q in range(4):
                        m = pe.transpose(bank[:, q * P:(q + 1) * P], x1[:, 4 * (j // 2) + q, (j % 2) * P:(j % 2 + 1) * P], identF)
                elif kind == "lg":
                    if i == 0:
                        pe.wait_ge(act_took["xt"], count(b, 4, 4 * const + 4))
                    for t in (2 * i, 2 * i + 1):
                        for k in range(KC):
                            m = mm(bank[:, t * NE:(t + 1) * NE], actT[:, k, t * P:(t + 1) * P], wg[:, k, :], k == 0, k == KC - 1)
                elif kind == "pf":
                    pe.wait_ge(lg_seq, count(b, LG_OPS, LG_OPS * (const + 1)))
                    mm(bank[:, 0:64], before, ohb[:].rearrange("p t e -> p (t e)"), True, True)
                    m = mm(bank[:, 64:128], onesB, ohb[:].rearrange("p t e -> p (t e)"), True, True)
                if i == len(CHUNKS[kind]) - 1:
                    m.then_inc(ready[kind], 1)

            def tile(b, db, g2, grp, k, start=False):
                heads, t, k0, w, _ = GROUP_TILES[k]
                idx = NM * (4 * db + 2 * g2 + grp) + k
                if k == 0 and grp == 0:
                    pe.wait_ge(stack_in, count(b, 2 * 16 * STACK_DMAS, 16 * STACK_DMAS * (2 * db + g2 + 1)))
                if start and k >= 4:
                    pe.wait_ge(mx_done, k - 3)
                elif not start and (idx >= 2 or not isinstance(b, int) or b > 0):
                    pe.wait_ge(mx_done, count(b, 4 * NM, idx - 1))
                bank = max_bank(idx, start)
                q, kk = qk_stack[g2]
                diag = k0 + w == (t + 1) * P
                for n, h in enumerate(heads):
                    i = grp * GH + h
                    m = mm(bank[:, n * w:(n + 1) * w], q[0:NSTACK, i, t * P:(t + 1) * P], kk[0:NSTACK, i, k0:k0 + w],
                           True, not diag)
                    if diag:
                        m = mm(bank[:, (n + 1) * w - P:(n + 1) * w], identB, maskK, False, True)
                m.then_inc(mx_ready, 1)

            def scores(b, g, s, p, n0):
                grp, c, kb, off, _ = step_block(s)
                if p == 0 and s % 12 == 0:
                    pe.wait_ge(mrow_in, count(b, 16 * 4, 16 * (2 * g + grp + 1)))
                if n0 >= 0:
                    pe.wait_ge(probs_ready, count(b, 96, 2 * (24 * g + s - 1) + p + 1))
                q, kk = qk_stack[g]
                for h in range(2):
                    i = grp * GH + 2 * p + h
                    diag = kb >= 4 * c
                    m = mm(st[:, 2 * p + h, off:HALF], kk[0:NROWS, i, kb * P:(kb + 1) * P],
                           q[0:NROWS, i, c * HALF + off:(c + 1) * HALF], True, not diag)
                    if diag:
                        m = mm(st[:, 2 * p + h, off:off + P], identB, maskQ, False, True)
                m.then_inc(st_ready, 1)

            def values(b, g, s, rel, half):
                grp, c, kb, off, is_last = step_block(s)
                if half == 0:
                    if kb == 0:
                        done = 4 * g + 2 * grp + c + (8 * (rel // 48))
                        if not (isinstance(b, int) and b == 0 and done == 0):
                            pe.wait_ge(raw_ready, count(b, 8, done))
                    if g == 0 and grp == 0 and kb % 2 == 0:
                        pe.wait_ge(v_switched, count(b, 4, kb // 2 + 1))
                    pe.wait_ge(probs_ready, count(b, 96, 2 * rel + 2))
                for h in (2 * half, 2 * half + 1):
                    head = g * UH + grp * GH + h
                    m = pe.matmul(pv[32 * h:32 * h + 32, off:HALF], v_now[:, kb, head * VS:head * VS + 32],
                                  probs[rel % 2][:, h, off:HALF], start=kb == 0, stop=is_last, skip_group_check=True)
                if half == 1:
                    m.then_inc(pv_done, 1)

            def body(b, first, last):
                if last_item[0] is not None:
                    k0, c0 = last_item[0]
                    last_item[0] = (k0, c0 - PER_SEQ[k0])
                for g in range(2):
                    for s in range(STEPS):
                        n = 24 * g + s
                        for what in plan_of(g, s, first, last):
                            if what[0] == "scores":
                                scores(b, g, s, what[1], -1 if first and n == 0 else 0)
                            elif what[0] == "item":
                                chunk(b, *what[1:])
                            elif what[0] == "tile":
                                db, g2, grp, k = what[1]
                                tile(b, db, g2, grp, k)
                            elif what[0] == "values":
                                values(b, (n - 1) // 24 % 2, (n - 1) % 24, n - 1, what[1])

            pe.wait_ge(qk_consts_in, 16 * N_QK_CONST)
            for what in HEAD:
                if what == ("item", ("v", 0, 0), 0, 0):
                    pe.wait_ge(consts_in, 16 * N_CONST)
                    pe.wait_ge(consts_ready, 1)
                if what[0] == "item":
                    chunk(0, *what[1:])
            pe.wait_ge(ones_ready, 2)
            for k in range(NM):
                tile(0, 0, 0, 0, k, start=True)
            chunk(0, ("m", 0, 0, 0, 0), 0)
            for k in range(EARLY):
                tile(0, 0, 0, 1, k)
            last_item[:] = ("m", PER_SEQ["m"]), None
            body(0, True, False)
            with pe.Fori(1, NB - 1) as b:
                body(b, False, False)
            body(NB - 1, False, True)
            for half in range(2):
                values(NB - 1, 1, 23, 47, half)
            for what in TAIL:
                if what[0] == "item":
                    chunk(NB - 1, *what[1:])

        @block.scalar
        def _(act):
            act.wait_ge(qk_consts_in, 16 * N_QK_CONST)
            nc.scalar.activation(bqk[:, 0, :], bqk_in[:, 0, :], ACT.Copy, scale=0.25).then_inc(biases_ready, 1)
            nc.scalar.activation(bqk[:, 1, :], bqk_in[:, 1, :], ACT.Copy).then_inc(biases_ready, 1)
            act.wait_ge(biases_ready, 2)

            def exps(b, g, s, p):
                grp, c, kb, off, _ = step_block(s)
                n = 24 * g + s
                act.wait_ge(st_ready, count(b, 96, 2 * n + p + 1))
                if not (isinstance(b, int) and b == 0 and n < 2):
                    act.wait_ge(pv_done, count(b, 48, n - 1))
                nc.scalar.activation(probs[n % 2][:, 2 * p:2 * p + 2, off:HALF], st[:, 2 * p:2 * p + 2, off:HALF],
                                     ACT.Exp).then_inc(probs_ready, 1)

            def item(b, it, place):
                kind, const = it[0], it[1]
                bank = item_banks[place]
                if kind == "qk":
                    _, _, db, g2, j = it
                    t = j % 2
                    act.wait_ge(ready["qk"], count(b, 8, const + 1))
                    if not (isinstance(b, int) and b == 0 and const < 2):
                        act.wait_ge(split_seq, count(b, 3 * 8, 3 * (const - 1)))
                        act.wait_ge(parts_out[const % 2], count(b, 16 * 4, 16 * (const // 2)))
                    kw = dict(bias=bqk[:, t, g2:g2 + 1], scale=(0.25, 1.0)[t])
                    nc.scalar.activation(qf[const % 2][:], bank, ACT.Identity, **kw).then_inc(qf_ready, 1)
                    nc.scalar.activation(parts[const % 2][:, 0, :], bank, ACT.Identity, **kw).then_inc(act_took["qk"], 1)
                if kind in ("ct", "xt"):
                    j = it[2]
                    act.wait_ge(ready[kind], count(b, 4, const + 1))
                    nc.scalar.activation(actT[:, j % 2, (j // 2) * HALF:(j // 2 + 1) * HALF], bank, ACT.Copy)\
                        .then_inc(act_took[kind], 1)

            def raw(b, rel, const):
                act.wait_ge(pv_done, count(b, 48, rel + 1))
                nc.scalar.activation(ctx_raw[:], pv[:], ACT.Copy).then_inc(raw_ready, 1)

            def router_exp(b, const):
                act.wait_ge(lg_seq, count(b, LG_OPS, LG_OPS * (const + 1)))
                nc.scalar.activation(expd[:], dlt[:], ACT.Exp).then_inc(expd_ready, 1)

            def run(b, what):
                if what[0] == "item" and what[2] == len(CHUNKS[what[1][0]]) - 1:
                    item(b, what[1], what[3])
                if what[0] == "job" and what[1][0] == "lg" and what[1][2] == LG_PARTS:
                    router_exp(b, what[1][1])

            def body(b, first, last):
                for g in range(2):
                    for s in range(STEPS):
                        n = 24 * g + s
                        for what in plan_of(g, s, first, last):
                            if what[0] == "scores":
                                exps(b, g, s, what[1])
                            elif what == ("values", 1):
                                if s in (4, 12, 16):
                                    raw(b, n - 1, 4 * g + {4: 0, 12: 1, 16: 2}[s])
                                if s == 0 and not (first and g == 0):
                                    raw(b, n - 1, 4 * g - 1)
                            else:
                                run(b, what)

            for what in HEAD:
                run(0, what)
            body(0, True, False)
            with act.Fori(1, NB - 1) as b:
                body(b, False, False)
            body(NB - 1, False, True)
            raw(NB - 1, 47, 7)
            for what in TAIL:
                run(NB - 1, what)

        @block.gpsimd
        def _(pool):
            for s in range(2):
                nc.gpsimd.memset(qk_stack[s][1][NSTACK:NROWS, :, :], 1.0).then_inc(ones_ready, 1)
                pool.wait_ge(ones_ready, s + 1)

            def clear_rows():
                pool.wait_ge(zero_ready, 1)
                flat = T["buf"].rearrange("(p r) d -> p (r d)", p=P)
                for z in range(N_CLEAR):
                    if z % 3 == 0:
                        pool.wait_ge(mrow_in, 16 * (z // 3 + 1))
                    pool.dma_start(flat[:, z * ZERO_COLS:(z + 1) * ZERO_COLS], zeros[:]).then_inc(zero_out, 16)
                pool.dma_start(T["y"][NE * SLOTS:NE * SLOTS + 1, :], zeros[0:1, 0:D]).then_inc(zero_out, 16)

            def residual(b):
                pool.wait_ge(x_in, count(b, 16, 16))
                for t in range(NT):
                    ins = nc.gpsimd.tensor_tensor(xb[:, t, :], xb[:, t, :], bo[:], ALU.add)
                ins.then_inc(xb_ready, 1)

            def root(b, const):
                pool.wait_ge(ve_ready, b + const + 1)
                nc.gpsimd.tensor_tensor(rstd[:], vare[:], mhalf[:], ALU.pow).then_inc(rstd_ready, 1)

            def scatter(b, const):
                wait_apart(pool, pf_seq, count(b, PF_OPS, PF_OPS * const + PF_PLACES))
                for t in range(NT):
                    for k in range(TOPK):
                        pool.indirect_dma_start(
                            T["buf"], bass.IndirectOffsetOnAxis(ap=idx_s[:, t, k:k + 1].bitcast(U32), axis=0),
                            x1[:, t, :], None, bounds_check=NE * SLOTS - 1, oob_is_err=False).then_inc(scat, 16)

            pool.wait_ge(ones_ready, 2)
            pool.wait_ge(consts_in, 16 * N_CONST)
            clear_rows()
            residual(0)
            pool.wait_ge(zero_out, 16 * N_ZERO)
            with pool.Fori(1, NB) as b:
                root(b, -1)
                scatter(b, -1)
                wait_apart(pool, scat, count(b, 256, 0))
                residual(b)
            root(NB - 1, 0)
            scatter(NB - 1, 0)

        @block.vector
        def _(dve):
            V = nc.vector

            class Chain:

                def __init__(self, sem_, per_item):
                    self.sem, self.per = sem_, per_item

                def begin(self, b, kind_per, const, done=0):
                    self.b, self.kp, self.c, self.n = b, kind_per, const, done

                def link(self, ins, apart=False):
                    self.n += 1
                    ins.then_inc(self.sem, 1)
                    value = count(self.b, self.kp * self.per, self.per * self.c + self.n)
                    if apart:
                        wait_apart(dve, self.sem, value)
                    else:
                        dve.wait_ge(self.sem, value)

                def end(self, ins):
                    self.n += 1
                    ins.then_inc(self.sem, 1)
                    assert self.n == self.per, (self.n, self.per)

            split = Chain(split_seq, 3)
            msplit = Chain(m_seq, M_OPS)
            gch = Chain(g_seq, G_OPS)
            stats_ch = Chain(stat_seq, STAT_OPS)
            lgch = Chain(lg_seq, LG_OPS)
            pfch = Chain(pf_seq, PF_OPS)

            def item(b, it, place=0):
                kind, const = it[0], it[1]
                bank = item_banks[place]
                if kind == "v":
                    j = it[2]
                    dve.wait_ge(ready["v"], count(b, 4, const + 1))
                    for u in range(2):
                        t = 2 * j + u
                        ins = V.tensor_tensor(
                            v_next[:, t, 0:NH * VS].rearrange("p (h c) -> p h c", c=VS)[:, :, 0:HD],
                            bank[:, u * D:(u + 1) * D].rearrange("p (h c) -> p h c", c=HD),
                            bv[:].rearrange("p (h c) -> p h c", c=HD), ALU.add)
                    ins.then_inc(v_taken, 1)
                elif kind == "g":
                    _, _, g, grp, c = it
                    dve.wait_ge(ready["g"], count(b, 8, const + 1))
                    if g == 0 and grp == 0 and c == 0 and not (isinstance(b, int) and b == 0):
                        dve.wait_ge(ready["ct"], count(b, 4, 0))
                    gch.begin(b, 8, const)
                    v4 = bank.rearrange("p (q h c) -> p q h c", q=4, h=GH)
                    gch.link(V.reciprocal(rden[:], v4[:, :, :, HD]))
                    col = (2 * g + grp) * GH * HD
                    ins = V.tensor_tensor(
                        ctxn[:, 4 * c:4 * c + 4, col:col + GH * HD].rearrange("p q (h c) -> p q h c", h=GH),
                        v4[:, :, :, 0:HD], rden[:].unsqueeze(3).to_broadcast([P, 4, GH, HD]), ALU.mult)
                    gch.end(ins)
                elif kind == "m":
                    _, _, db, g2, grp = it
                    dve.wait_ge(ready["m"], count(b, 4, const + 1))
                    if not (isinstance(b, int) and b == 0 and const == 0):
                        dve.wait_ge(mrow_out, count(b, 64, 16 * const))
                    msplit.begin(b, 4, const)
                    msplit.link(V.tensor_scalar(nmax[:], bank[0:32, 0:P], -1.0, None, ALU.mult))
                    msplit.link(V.tensor_copy(nparts[:, 0, :], nmax[:]))
                    msplit.link(V.tensor_tensor(nrest[:], nmax[:], nparts[:, 0, :], ALU.subtract))
                    msplit.link(V.tensor_copy(nparts[:, 1, :], nrest[:]))
                    msplit.end(V.tensor_tensor(nparts[:, 2, :], nrest[:], nparts[:, 1, :], ALU.subtract))
                elif kind == "wo":
                    j = it[2]
                    dve.wait_ge(ready["wo"], count(b, 4, const + 1))
                    dve.wait_ge(xb_ready, count(b, 1, (const - j) // 4 + 1))
                    V.tensor_tensor(x1[:, 2 * j:2 * j + 2, :], bank.rearrange("p (t d) -> p t d", t=2),
                                    xb[:, 2 * j:2 * j + 2, :], ALU.add).then_inc(wo_seq, 1)
                elif kind == "lg":
                    dve.wait_ge(ready["lg"], b + const + 1)
                    lgch.begin(b, 1, const)
                    lgch.link(V.tensor_copy(lg[:], bank[:, 0:64].rearrange("p (t e) -> p t e", t=NT)))
                elif kind == "pf":
                    dve.wait_ge(ready["pf"], b + const + 1)
                    pfch.begin(b, 1, const)
                    pfch.link(V.tensor_copy(tot[:, :, 1:NT + 1], bank[:, 64:128].rearrange("p (t e) -> p e t", t=NT)))
                    pfch.link(V.tensor_copy(pos[:], bank[:, 0:64].rearrange("p (t e) -> p t e", t=NT)))

            def split_job(b, const, n):
                i = const % 2
                split.begin(b, 8, const, n)
                if n == 0:
                    dve.wait_ge(qf_ready, count(b, 8, const + 1))
                    dve.wait_ge(act_took["qk"], count(b, 8, const + 1))
                    split.link(V.tensor_tensor(rest[i][:], qf[i][:], parts[i][:, 0, :], ALU.subtract))
                elif n == 1:
                    split.link(V.tensor_copy(parts[i][:, 1, :], rest[i][:]))
                else:
                    split.end(V.tensor_tensor(parts[i][:, 2, :], rest[i][:], parts[i][:, 1, :], ALU.subtract))

            def stat_job(b, const, j, u):
                t = 2 * j + u
                dve.wait_ge(wo_seq, count(b, 4, const + 1))
                stats_ch.begin(b, 4, const, 2 * u)
                stats_ch.link(V.bn_stats(stats[:, t, :], x1[:, t, :]), apart=True)
                aggregated = V.bn_aggr(mv[:, t, :], stats[:, t, :])
                stats_ch.end(aggregated) if u else stats_ch.link(aggregated)

            def norm_job(b, const, q):
                if q == 0:
                    dve.wait_ge(rstd_ready, b + const + 1)
                for t in (2 * q, 2 * q + 1):
                    ins = V.tensor_scalar(x1[:, t, :], x1[:, t, :], mv[:, t, 0:1], rstd[:, t:t + 1],
                                          ALU.subtract, ALU.mult)
                if q == 3:
                    ins.then_inc(x1_ready, 1)

            def switch_job(b, part):
                if part == 0:
                    if not (isinstance(b, int) and b == 0):
                        dve.wait_ge(pv_done, count(b, 48, 0))
                    dve.wait_ge(v_taken, count(b, 4, 4))
                rows = slice(2 * part, 2 * part + 2)
                V.tensor_copy(v_now[:, rows, :], v_next[:, rows, :]).then_inc(v_switched, 1)

            def lg_job(b, const, part):
                L, shp = lgch, [P, NT, NE]
                d3 = desc.rearrange("p (t e) -> p t e", t=NT)
                k = (part - 1) // 2
                src = (lg, lg2)[k]
                L.begin(b, 1, const, (1, 3, 6, 9)[part - 1])
                if part == 3:
                    L.link(V.scalar_tensor_tensor(out=lg2[:], in0=oh[0][:], scalar=-3.0e38, in1=lg[:],
                                                  op0=ALU.mult, op1=ALU.add))
                if part in (1, 3):
                    L.link(V.tensor_reduce(top[:, :, k:k + 1], src[:], AX_X, ALU.max))
                    L.link(V.tensor_tensor(sel[:], src[:], top[:, :, k:k + 1].to_broadcast(shp), ALU.is_equal))
                else:
                    L.link(V.tensor_tensor(sel[:], sel[:], d3, ALU.mult))
                    L.link(V.tensor_reduce(pick[:, :, k:k + 1], sel[:], AX_X, ALU.max))
                    L.link(V.tensor_tensor(oh[k][:], d3, pick[:, :, k:k + 1].to_broadcast(shp), ALU.is_equal))
                if part == 4:
                    L.link(V.tensor_tensor(dlt[:], top[:, :, 1], top[:, :, 0], ALU.subtract))
                    L.end(V.tensor_tensor(ohb[:], oh[0][:], oh[1][:], ALU.add))

            def pf_job(b, const, part):
                Q = pfch
                Q.begin(b, 1, const, (2, 5, 9, 14)[part - 1])
                if part == 1:
                    Q.link(V.tensor_copy(tot[:, :, 0], base[:, :, NT]))
                    Q.link(V.tensor_tensor_scan(base[:].rearrange("p e t -> p (e t)"), anew[:].rearrange("p e t -> p (e t)"),
                                                tot[:].rearrange("p e t -> p (e t)"), 0.0, ALU.mult, ALU.add))
                    Q.link(V.tensor_tensor(pos[:], pos[:], base[:, :, 0:NT].rearrange("p e t -> p t e"), ALU.add))
                if part == 2:
                    for k in range(2):
                        Q.link(V.tensor_tensor(sel[:], oh[k][:], pos[:], ALU.mult))
                        Q.link(V.tensor_reduce(posk[:, :, k:k + 1], sel[:], AX_X, ALU.add))
                if part == 3:
                    Q.link(V.tensor_scalar(keep[:], posk[:], float(CAP), None, ALU.is_lt))
                    Q.link(V.scalar_tensor_tensor(out=dest[:], in0=pick[:], scalar=-float(SLOTS), in1=posk[:],
                                                  op0=ALU.mult, op1=ALU.add))
                    Q.link(V.scalar_tensor_tensor(out=dest[:], in0=keep[:], scalar=-float(NE * SLOTS), in1=dest[:],
                                                  op0=ALU.mult, op1=ALU.add))
                    Q.link(V.tensor_scalar(idx_s[:], dest[:], float(2 * NE * SLOTS), None, ALU.add))
                    Q.link(V.tensor_scalar(idx_g[:], dest[:], float(2 * NE * SLOTS), float(NE * SLOTS), ALU.add, ALU.min))
                if part == 4:
                    dve.wait_ge(expd_ready, b + const + 1)
                    Q.link(V.tensor_scalar(den[:], expd[:], 1.0, None, ALU.add))
                    Q.link(V.reciprocal(gates[:, :, 0], den[:]))
                    Q.link(V.tensor_tensor(gates[:, :, 1], gates[:, :, 0], expd[:], ALU.mult))
                    Q.end(V.tensor_tensor(gates[:], gates[:], keep[:], ALU.mult))

            def tile(b, db, g2, grp, k, start=False):
                heads, _, _, w, col = GROUP_TILES[k]
                n = len(heads)
                idx = NM * (4 * db + 2 * g2 + grp) + k
                dve.wait_ge(mx_ready, count(b, 4 * NM, idx + 1))
                V.tensor_reduce(pmax[:, grp, heads[0]:heads[0] + n, col:col + 1],
                                max_bank(idx, start)[:, 0:n * w].rearrange("p (h w) -> p h w", h=n), AX_X, ALU.max).then_inc(mx_done, 1)

            def gather_max(b, db, g2, grp):
                const = 4 * db + 2 * g2 + grp
                dve.wait_ge(mx_done, count(b, 4 * NM, NM * (4 * db + 2 * g2 + grp + 1)))
                if not (isinstance(b, int) and b == 0 and const == 0):
                    dve.wait_ge(ready["m"], count(b, 4, const))
                m3 = mcol[:, 0:32].rearrange("p (h t) -> p h t", h=GH)
                V.tensor_copy(m3[:, :, 0:4], pmax[:, grp, :, 0:4]).then_inc(mcol_seq, 1)
                V.tensor_tensor(m3[:, :, 4:8], pmax[:, grp, :, 4:8], pmax[:, grp, :, 8:12], ALU.max).then_inc(mcol_seq, 1)

            def job(b, kind, const, part):
                if kind == "split":
                    split_job(b, const, part)
                elif kind == "stat":
                    stat_job(b, const, *part)
                elif kind == "vare":
                    dve.wait_ge(stat_seq, count(b, 4 * STAT_OPS, 4 * STAT_OPS * (const + 1)))
                    V.tensor_scalar(vare[:], mv[:, :, 1], EPS, None, ALU.add).then_inc(ve_ready, 1)
                elif kind == "norm":
                    norm_job(b, const, part)
                elif kind == "v_switch":
                    switch_job(b, part)
                elif kind == "lg":
                    lg_job(b, const, part)
                elif kind == "pf":
                    pf_job(b, const, part)
                elif kind == "gather":
                    gather_max(b, *part)

            def run(b, what):
                if what[0] == "item" and what[2] == len(CHUNKS[what[1][0]]) - 1:
                    item(b, what[1], what[3])
                elif what[0] == "job":
                    job(b, *what[1])
                elif what[0] == "tile":
                    tile(b, *what[1])

            def body(b, first, last):
                for g in range(2):
                    for s in range(STEPS):
                        for what in plan_of(g, s, first, last):
                            run(b, what)

            V.memset(zeros[:], 0.0).then_inc(zero_ready, 1)
            V.memset(mcol[:], 0.0).then_inc(cleared, 1)
            V.memset(base[:], 0.0).then_inc(cleared, 1)
            V.memset(v_next[:], 1.0).then_inc(cleared, 1)
            V.memset(mhalf[:], -0.5).then_inc(cleared, 1)
            V.memset(anew[:], 1.0).then_inc(cleared, 1)
            dve.wait_ge(cleared, 5)
            V.memset(anew[:, :, 0], 0.0).then_inc(cleared, 1)
            dve.wait_ge(cleared, 6)
            dve.wait_ge(consts_in, 16 * N_CONST)
            V.tensor_copy(cb[:, 0:4 * P], cf[:, 0:4 * P])
            V.memset(onesB, 1.0).then_inc(consts_ready, 1)
            dve.wait_ge(consts_ready, 1)
            for what in HEAD:
                run(0, what)
            for k in range(NM):
                tile(0, 0, 0, 0, k, start=True)
            gather_max(0, 0, 0, 0)
            item(0, ("m", 0, 0, 0, 0))
            for k in range(EARLY):
                tile(0, 0, 0, 1, k)
            body(0, True, False)
            with dve.Fori(1, NB - 1) as b:
                body(b, False, False)
            body(NB - 1, False, True)
            for what in TAIL:
                run(NB - 1, what)


HID = 1024
MH = HID // P
CH = 432
NCH = SLOTS // CH
SUB = CH // 4


class ExpertWeights:

    def __init__(self, nc, ctx, T):
        self.T = T
        self.raw1 = ctx.enter_context(nc.sbuf_tensor("b_raw1", [P, KC, HID], F32))
        self.raw2 = ctx.enter_context(nc.sbuf_tensor("b_raw2", [P, MH, D], F32))
        self.b1 = [ctx.enter_context(nc.sbuf_tensor(f"b_b1_{s}", [P, MH], F32)) for s in range(2)]
        self.b2 = [ctx.enter_context(nc.sbuf_tensor(f"b_b2_{s}", [P, KC], F32)) for s in range(2)]
        self.raw_in = ctx.enter_context(nc.semaphore("b_raw_in"))
        self.bias_in = [ctx.enter_context(nc.semaphore(f"b_bias_in{s}")) for s in range(2)]

    def load(self, sp, e, slot):
        T = self.T
        sp.dma_start(self.raw1[:], T["w1"][e].rearrange("(k p) n -> p k n", p=P)).then_inc(self.raw_in, 16)
        sp.dma_start(self.raw2[:], T["w2"][e].rearrange("(k p) n -> p k n", p=P)).then_inc(self.raw_in, 16)
        sp.dma_start(self.b1[slot][:], T["b1"][e]).then_inc(self.bias_in[slot], 16)
        sp.dma_start(self.b2[slot][:], T["b2"][e]).then_inc(self.bias_in[slot], 16)


def phase_experts(nc, T, held):

    with ExitStack() as ctx:
        def sb(name, shape, dt=F32):
            return ctx.enter_context(nc.sbuf_tensor("b_" + name, shape, dt))

        def sem(name):
            return ctx.enter_context(nc.semaphore("b_" + name))

        def psum(name, shape):
            return ctx.enter_context(nc.psum_tensor("b_" + name, shape, F32))

        identF = sb("ident", [P, P])
        raw1, raw2, b1, b2, raw_in, bias_in = held.raw1, held.raw2, held.b1, held.b2, held.raw_in, held.bias_in
        w1 = [[sb(f"w1_{s}{p}", [P, KC, HID], F32R) for p in range(2)] for s in range(2)]
        w2 = [[sb(f"w2_{s}{p}", [P, MH, D], F32R) for p in range(2)] for s in range(2)]
        xin = [sb(f"xin{i}", [SUB, 4, D]) for i in range(2)]
        xp = [[sb(f"xp{i}{p}", [P, KC, CH], F32R) for p in range(2)] for i in range(2)]
        hf = [sb(f"hf{i}", [P, CH]) for i in range(2)]
        hp = [[sb(f"hp{i}{p}", [P, MH, CH], F32R) for p in range(2)] for i in range(2)]
        yT = [sb(f"yT{i}", [P, KC, CH]) for i in range(2)]
        yo = [sb(f"yo{i}", [SUB, 4, D]) for i in range(2)]
        p_x = psum("p_x", [P, KC, HALF])
        p_h = psum("p_h", [P, 2, HALF])
        p_y = psum("p_y", [P, KC, HALF])
        p_t = psum("p_t", [P, 2, HALF])

        ident_in = sem("ident_in")
        w_seq = sem("w_seq")
        xin_in = [sem(f"xin_in{i}") for i in range(2)]
        xt_ready = sem("xt_ready")
        xh_ready = sem("xh_ready")
        xl_ready = sem("xl_ready")
        h_ready = sem("h_ready")
        hf_ready = sem("hf_ready")
        hh_ready = sem("hh_ready")
        hl_ready = sem("hl_ready")
        y_ready = sem("y_ready")
        yT_ready = sem("yT_ready")
        yt_ready = sem("yt_ready")
        yo_ready = sem("yo_ready")
        y_out = [sem(f"y_out{i}") for i in range(2)]
        N2 = 2 * NCH
        NALL = NE * NCH

        def rows(i, c):
            return (i * 2 + c // NCH) * SLOTS + (c % NCH) * CH

        block = ctx.enter_context(nc.Block())

        @block.sync
        def _(sp):
            def load(i, c):
                sp.dma_start(xin[c % 2][:], T["buf"][bass.ds(rows(i, c), CH), :].rearrange("(q p) d -> p q d", p=SUB))\
                    .then_inc(xin_in[c % 2], 16)

            def store(i, c):
                wait_apart(sp, yo_ready, count(i, N2, c + 1))
                sp.dma_start(T["y"][bass.ds(rows(i, c) if c >= 0 else rows(i, c + N2) - 2 * SLOTS, CH), :]
                             .rearrange("(q p) d -> p q d", p=SUB), yo[c % 2][:]).then_inc(y_out[c % 2], 16)

            def body(i, first, last):
                for c in range(N2):
                    if not (last and c == N2 - 1):
                        if not (first and c == 0):
                            wait_apart(sp, xt_ready, count(i, N2, c))
                        if c < N2 - 1:
                            load(i, c + 1)
                        else:
                            load(i + 1, 0)
                    if c % NCH == 1 and not (last and c >= NCH):
                        half = c // NCH
                        wait_apart(sp, w_seq, count(i, 16, 8 * (half + 1)))
                        if not (first and half == 0):
                            wait_apart(sp, yT_ready, count(i, 2 * N2, 2 * (half * NCH)))
                        held.load(sp, 2 * i + half + 1, 1 - half)
                    if c >= 2 or not first:
                        store(i, c - 2)

            sp.dma_start(identF[:], T["consts"][:, 0:P]).then_inc(ident_in, 16)
            load(0, 0)
            body(0, True, False)
            with sp.Fori(1, NE // 2 - 1) as i:
                body(i, False, False)
            body(NE // 2 - 1, False, True)
            store(NE // 2 - 1, N2 - 2)
            store(NE // 2 - 1, N2 - 1)
            wait_apart(sp, y_out[0], 16 * NALL // 2)
            wait_apart(sp, y_out[1], 16 * NALL // 2)

        @block.tensor
        def _(pe):
            def mm(out, a, bb, start, stop):
                return pe.matmul(out, a, bb, start=start, stop=stop)

            def turn_in(i, c):
                pe.wait_ge(xin_in[c % 2], count(i, 16 * NCH, 16 * (c // 2 + 1)))
                if not (isinstance(i, int) and i == 0 and c == 0):
                    pe.wait_ge(xl_ready, count(i, N2, c))
                for k in range(KC):
                    for q in range(4):
                        m = pe.transpose(p_x[:, k, q * SUB:(q + 1) * SUB], xin[c % 2][:, q, k * P:(k + 1) * P],
                                         identF[0:SUB, 0:SUB])
                m.then_inc(xt_ready, 1)

            def turn_out(i, c):
                pe.wait_ge(yT_ready, count(i, 2 * N2, 2 * (c + 1)))
                if not (isinstance(i, int) and i == 0 and c == 0):
                    pe.wait_ge(yo_ready, count(i, N2, c))
                for q in range(4):
                    for k in range(KC):
                        m = pe.transpose(p_t[0:SUB, q // 2, (q % 2) * D + k * P:(q % 2) * D + (k + 1) * P],
                                         yT[c % 2][:, k, q * SUB:(q + 1) * SUB], identF[:])
                m.then_inc(yt_ready, 1)

            def hidden(i, c, m):
                slot = c // NCH
                if m == 0:
                    pe.wait_ge(xl_ready, count(i, N2, c + 1))
                    if c % NCH == 0:
                        pe.wait_ge(w_seq, count(i, 16, 8 * slot + 4))
                n = MH * c + m
                if not (isinstance(i, int) and i == 0 and n < 2):
                    pe.wait_ge(hh_ready, count(i, MH * N2, n - 1))
                x = xp[c % 2]
                o = p_h[:, m % 2, 0:CH]
                terms = [(wp, xq, k) for wp, xq in ((0, 0), (0, 1), (1, 0)) for k in range(KC)]
                for t, (wp, xq, k) in enumerate(terms):
                    r = mm(o, w1[slot][wp][:, k, m * P:(m + 1) * P], x[xq][:, k, :], t == 0, t == len(terms) - 1)
                r.then_inc(h_ready, 1)

            def output(i, c, part):
                slot = (c // NCH) % 2
                k, first = part // 4, (part % 4) * 2
                if part == 0 and c % NCH == 0:
                    pe.wait_ge(w_seq, count(i, 16, 8 * (c // NCH + 1)))
                if part % 4 == 0 and not (isinstance(i, int) and i == 0 and c == 0):
                    pe.wait_ge(yT_ready, count(i, 2 * N2, 2 * c + k - 1))
                for j in (first, first + 1):
                    if k == 0:
                        pe.wait_ge(hl_ready, count(i, MH * N2, MH * c + j + 1))
                    for t, (wp, hq) in enumerate(((0, 0), (0, 1), (1, 0))):
                        r = mm(p_y[:, k, 0:CH], w2[slot][wp][:, j, k * P:(k + 1) * P], hp[c % 2][hq][:, j, :],
                               j == 0 and t == 0, j == MH - 1 and t == 2)
                if part % 4 == 3:
                    r.then_inc(y_ready, 1)

            def body(i, first, last):
                for c in range(N2):
                    for m in range(MH):
                        hidden(i, c, m)
                        if m == 3 and not (last and c == N2 - 1):
                            turn_in(i, c + 1)
                        if c > 0 or not first:
                            output(i, c - 1, m)
                        if m == 1 and (c > 1 or not first):
                            turn_out(i, c - 2)

            pe.wait_ge(ident_in, 16)
            turn_in(0, 0)
            body(0, True, False)
            with pe.Fori(1, NE // 2 - 1) as i:
                body(i, False, False)
            body(NE // 2 - 1, False, True)
            for part in range(MH):
                if part == 1:
                    turn_out(NE // 2 - 1, N2 - 2)
                output(NE // 2 - 1, N2 - 1, part)
            turn_out(NE // 2 - 1, N2 - 1)

        @block.scalar
        def _(act):
            A = nc.scalar

            def high(i, c):
                act.wait_ge(xt_ready, count(i, N2, c + 1))
                A.activation(xp[c % 2][0][:], p_x[:, :, 0:CH], ACT.Copy).then_inc(xh_ready, 1)

            def gelu(i, c, m):
                n = MH * c + m
                act.wait_ge(h_ready, count(i, MH * N2, n + 1))
                if not (isinstance(i, int) and i == 0 and n < 2):
                    act.wait_ge(hl_ready, count(i, MH * N2, n - 1))
                bias = b1[c // NCH][:, m:m + 1]
                A.activation(hf[m % 2][:], p_h[:, m % 2, 0:CH], ACT.Gelu_apprx_tanh, bias=bias).then_inc(hf_ready, 1)
                A.activation(hp[c % 2][0][:, m, :], p_h[:, m % 2, 0:CH], ACT.Gelu_apprx_tanh, bias=bias).then_inc(hh_ready, 1)

            def out(i, c, k):
                act.wait_ge(y_ready, count(i, 2 * N2, 2 * c + k + 1))
                slot = (c // NCH) % 2
                A.activation(yT[c % 2][:, k, :], p_y[:, k, 0:CH], ACT.Identity, bias=b2[slot][:, k:k + 1]).then_inc(yT_ready, 1)

            def body(i, first, last):
                for c in range(N2):
                    for m in range(MH):
                        if m == 0 and c % NCH == 0:
                            act.wait_ge(bias_in[c // NCH], count(i, 32, 32))
                        gelu(i, c, m)
                        if m == 3 and not (last and c == N2 - 1):
                            high(i, c + 1)
                        if m == 3 and (c > 0 or not first):
                            out(i, c - 1, 0)
                    if c > 0 or not first:
                        out(i, c - 1, 1)

            high(0, 0)
            body(0, True, False)
            with act.Fori(1, NE // 2 - 1) as i:
                body(i, False, False)
            body(NE // 2 - 1, False, True)
            out(NE // 2 - 1, N2 - 1, 0)
            out(NE // 2 - 1, N2 - 1, 1)

        @block.vector
        def _(dve):
            V = nc.vector

            def low(i, c):
                dve.wait_ge(xh_ready, count(i, N2, c + 1))
                V.tensor_tensor(xp[c % 2][1][:], p_x[:, :, 0:CH], xp[c % 2][0][:].bitcast(F32), ALU.subtract)\
                    .then_inc(xl_ready, 1)

            def hlow(i, c, m):
                dve.wait_ge(hf_ready, count(i, MH * N2, MH * c + m + 1))
                dve.wait_ge(hh_ready, count(i, MH * N2, MH * c + m + 1))
                V.tensor_tensor(hp[c % 2][1][:, m, :], hf[m % 2][:], hp[c % 2][0][:, m, :].bitcast(F32), ALU.subtract)\
                    .then_inc(hl_ready, 1)

            def rows_out(i, c):
                dve.wait_ge(yt_ready, count(i, N2, c + 1))
                if not (isinstance(i, int) and i == 0 and c < 2):
                    dve.wait_ge(y_out[c % 2], count(i, 16 * NCH, 16 * (c // 2)))
                V.tensor_copy(yo[c % 2][:].rearrange("p (a q) d -> p a (q d)", a=2), p_t[0:SUB, :, :]).then_inc(yo_ready, 1)

            def weights(i, slot, piece):
                if piece == 0:
                    dve.wait_ge(raw_in, count(i, 64, 32 * (slot + 1)))
                w, raw, h = (w1, raw1, slice(piece, piece + 1)) if piece < 2 else (w2, raw2, slice(4 * (piece - 2), 4 * (piece - 1)))
                s = slot % 2
                V.tensor_copy(w[s][0][:, h, :], raw[:, h, :]).then_inc(w_seq, 1)
                dve.wait_ge(w_seq, count(i, 16, 8 * slot + 2 * piece + 1))
                V.tensor_tensor(w[s][1][:, h, :], raw[:, h, :], w[s][0][:, h, :].bitcast(F32), ALU.subtract).then_inc(w_seq, 1)

            def body(i, first, last):
                for c in range(N2):
                    for m in range(MH):
                        hlow(i, c, m)
                        if m == 3 and not (last and c == N2 - 1):
                            low(i, c + 1)
                        if m == 2 and (c > 1 or not first):
                            rows_out(i, c - 2)
                        if m == 5 and c % NCH >= 1 and not (last and c >= NCH):
                            if c % NCH == 1:
                                if not (first and c < NCH):
                                    dve.wait_ge(y_ready, count(i, 2 * N2, 2 * (c - 1)))
                            weights(i, c // NCH + 1, c % NCH - 1)

            for piece in range(4):
                weights(0, 0, piece)
            low(0, 0)
            body(0, True, False)
            with dve.Fori(1, NE // 2 - 1) as i:
                body(i, False, False)
            body(NE // 2 - 1, False, True)
            rows_out(NE // 2 - 1, N2 - 2)
            rows_out(NE // 2 - 1, N2 - 1)


FH = 768
FM = FH // P
N_FF = 2 * FM
SCALE = 1.0 / 127.0
TINY = 1.1754943508222875e-38

C_SEQ = {"xt": 4, "v": 4, "q": 4, "g": 4, "rt": 4, "zt": 4, "wo": 4, "d1": 4, "ff": N_FF, "dn": 4}
RING = {"xt": "turn", "d1": "turn", "rt": "turn", "zt": "turn", "v": "prod", "q": "prod", "g": "prod",
        "wo": "prod", "dn": "prod", "ff": "pair"}
LATE = ("d1", "ff", "dn")


STEP = """g0 g1 g2 g3 v0 v1 v2 v3 q0 d10 q1 d11 q2 d12 q3 d13 x20
    ff0 rt0 ff1 rt1 ff2 rt2 ff3 rt3 rt_var0 ff4 sum_a0 ff5 rt_norm0 rt_norm1 sum_b0 ff6 dn0 sum_a1 zt0 ff7 sum_b1 zt1 dn1
    sum_a2 zt2 ff8 sum_b2 zt3 ff9 sum_a3 wo0 ff10 sum_b3 sum_var0 ff11 wo1 sum_norm0 sum_norm1 dn2 xt0 xt1 dn3 dn_var0
    xt2 wo2 xt3 wo3 wo_var0 """
STEP_NORMS = ("dn_norm0 dn_norm1 wo_norm0 wo_norm1", "wo_norm0 wo_norm1 dn_norm0 dn_norm1")
HEAD_STEP = """g0 g1 g2 g3 v0 v1 v2 v3 q0 q1 q2 q3 x20 rt0 rt1 rt2 rt3 rt_var0 rt_norm0 rt_norm1
    zt0 zt1 zt2 zt3 sum_a0 sum_b0 sum_a1 sum_b1
    wo0 wo1 sum_a2 sum_b2 wo2 wo3 sum_a3 sum_b3 sum_var0 wo_var0 sum_norm0 sum_norm1 xt0 xt1 xt2 xt3 wo_norm0 wo_norm1"""


def order(head, tail, combine):
    items = []
    for word in (HEAD_STEP if head else STEP + STEP_NORMS[not combine]).split():
        kind, j = word[:-1], int(word[-1])
        if word[:2] == "ff":
            kind, j = "ff", int(word[2:])
        if kind[:3] == "sum" or kind == "xt":
            there = combine
        else:
            there = not head if kind[:2] in ("d1", "ff", "dn") else not tail
        if there:
            items.append((kind, j))
    return items


SUM_OPS, RT_OPS, ADD_OPS = 8, 4, 5
PREP_FIRST, PREP = 8, 10
PREP_ACT = 5


def run_steps(eng, step):
    step(0, True, False, True, True)
    with eng.Fori(1, NB - 2) as b:
        step(b, False, False, True, True)
    step(NB - 2, False, False, True, False)
    step(NB - 1, False, False, False, False)
    step(NB, False, True, False, False)


def phase_layer1(nc, T):
    with ExitStack() as ctx:
        def sb(name, shape, dt=F32):
            return ctx.enter_context(nc.sbuf_tensor("c_" + name, shape, dt))

        def sem(name):
            return ctx.enter_context(nc.semaphore("c_" + name))

        identF = sb("ident", [P, P])
        wp = {k: [sb(f"w{k}{p}", [P, KC, D], F32R) for p in range(2)] for k in ("q", "v", "g")}
        wo = sb("wo", [P, KC, D])
        wgt = [sb(f"wgt{p}", [P, KC, FH], F32R) for p in range(2)]
        wup = [sb(f"wup{p}", [P, KC, FH], F32R) for p in range(2)]
        wdn = sb("wdn", [P, FM, D])
        gb = sb("gb", [P, 2, KC])
        bexp = sb("bexp", [P, KC])
        lam = sb("lam", [P, KC])
        x1t = sb("x1t", [P, NT, D])
        yg = [sb(f"yg{k}", [P, NT, D]) for k in range(TOPK)]
        gates = sb("gates", [P, NT, TOPK])
        idx = sb("idx", [P, NT, TOPK], I32)
        xn = sb("xn", [P, NT, D])
        x2 = sb("x2", [P, NT, D])
        x3 = sb("x3", [P, NT, D])
        o = sb("o", [P, NT, D])
        xp = [sb(f"xp{p}", [P, KC, S], F32R) for p in range(2)]
        x3p = [sb(f"x3p{p}", [P, KC, S], F32R) for p in range(2)]
        ret = sb("ret", [P, KC, S])
        gT = sb("gT", [P, KC, S])
        rt = sb("rt", [P, NT, D])
        zT = sb("zT", [P, KC, S])
        h = sb("h", [P, FM, S])
        sg = [sb(f"sg{i}", [P, HALF]) for i in range(2)]
        LNS = ("sum", "rt", "wo", "dn")
        stats = {k: sb("stats_" + k, [P, NT, 6]) for k in LNS}
        mv = {k: sb("mv_" + k, [P, NT, 2]) for k in LNS}
        vare = {k: sb("vare_" + k, [P, NT]) for k in LNS}
        rstd = {k: sb("rstd_" + k, [P, NT]) for k in LNS}
        mhalf = sb("mhalf", [P, NT])
        stage = h[:].rearrange("p m n -> p (m n)")

        p_turn = ctx.enter_context(nc.psum_tensor("c_turn", [P, 2, HALF], F32))
        p_prod = ctx.enter_context(nc.psum_tensor("c_prod", [P, 2, HALF], F32))
        p_pair = ctx.enter_context(nc.psum_tensor("c_pair", [P, 2, 2, HALF], F32))

        const_in = sem("const_in")
        bexp_in = sem("bexp_in")
        stage_in = {integer: sem(f"stage{int(integer)}_in") for integer in (False, True)}
        prep = sem("prep")
        prep_pool = sem("prep_pool")
        prep_act = sem("prep_act")
        lam_exp = sem("lam_exp")
        ready = {k: sem(k + "_ready") for k in C_SEQ}
        act_took = {k: sem(k + "_copied") for k in ("xt", "g", "rt", "zt", "d1")}
        silu_ready = sem("silu_ready")
        xl_ready = sem("xl_ready")
        x3l_ready = sem("x3l_ready")
        scanned = sem("scanned")
        ret_ready = sem("ret_ready")
        h_ready = sem("h_ready")
        z_ready = sem("z_ready")
        seq = {k: sem(k + "_seq") for k in LNS}
        ve_ready = {k: sem(k + "_ve") for k in LNS}
        rstd_ready = {k: sem(k + "_rstd") for k in LNS}
        normed = {k: sem(k + "_normed") for k in LNS}
        gathered = sem("gathered")
        gathered_0 = [sem(f"gathered_0{half}") for half in range(2)]
        idx_in = sem("idx_in")
        x1_in = sem("x1_in")
        x2_ready = sem("x2_ready")
        o_free = sem("o_free")

        taken = {"xt": (xl_ready, 1, 1), "d1": (x3l_ready, 1, 1), "rt": (act_took["rt"], 1, 1),
                 "zt": (act_took["zt"], 1, 1), "v": (scanned, 1, 1), "q": (ret_ready, 1, 1), "g": (act_took["g"], 1, 1),
                 "wo": (seq["wo"], ADD_OPS, 1), "dn": (seq["dn"], ADD_OPS, 1), "ff": (h_ready, 1, 1)}

        def const_of(kind, j):
            return j - C_SEQ[kind] if kind in LATE else j + C_SEQ[kind] if kind == "xt" else j

        block = ctx.enter_context(nc.Block())

        def staged():
            for k in ("q", "v", "g"):
                yield T["w1" + k].rearrange("(k p) n -> p k n", p=P), KC * D, wp[k], False
            for src, dst in ((T["wgt"], wgt), (T["wup"], wup)):
                yield src.rearrange("(k p) n -> p k n", p=P), KC * FH, dst, True
            yield T["wdn"].rearrange("(k p) n -> p k n", p=P), FM * D, wdn, True

        STAGED = list(staged())
        offs, at = [], 0
        for src, cols, dst, integer in STAGED:
            offs.append(at)
            at += cols
        assert at <= FM * S

        @block.sync
        def _(sp):
            def load_idx(b, db):
                sp.dma_start(idx[:], T["dest"][b + db]).then_inc(idx_in, 16)

            def load_x1(b, db):
                sp.dma_start(x1t[:], T["x1"][b + db].rearrange("(t p) d -> p t d", p=P)).then_inc(x1_in, 16)
                sp.dma_start(gates[:], T["gates"][b + db]).then_inc(x1_in, 16)

            def load_stage(which):
                for (src, cols, dst, integer), off in list(zip(STAGED, offs))[which]:
                    v = stage[:, off:off + cols].rearrange("p (k n) -> p k n", k=src.shape[1])
                    sp.dma_start(v.bitcast(I32) if integer else v, src).then_inc(stage_in[integer], 16)

            load_idx(0, 0)
            sp.dma_start(bexp[:], T["bexp"]).then_inc(bexp_in, 16)
            load_stage(slice(0, 3))
            load_x1(0, 0)
            sp.dma_start(identF[:], T["consts"][:, 0:P]).then_inc(const_in, 16)
            sp.dma_start(gb[:], T["gb"]).then_inc(const_in, 16)
            sp.dma_start(wo[:], T["w1o"].rearrange("(k p) n -> p k n", p=P)).then_inc(const_in, 16)
            load_stage(slice(3, 6))
            for half in range(2):
                wait_apart(sp, gathered_0[half], 128)
            load_idx(0, 1)
            wait_apart(sp, normed["sum"], 1)
            load_x1(0, 1)

            def step(b, head, tail, combine, gather):
                if gather:
                    wait_apart(sp, gathered, count(b, 256, 256))
                    load_idx(b, 2)
                    wait_apart(sp, normed["sum"], count(b, 1, 2))
                    load_x1(b, 2)
                if not head:
                    wait_apart(sp, normed["dn"], count(b, 1, 0))
                    sp.dma_start(T["out"][b - 1].rearrange("(t p) d -> p t d", p=P), o[:]).then_inc(o_free, 16)

            run_steps(sp, step)
            wait_apart(sp, o_free, 16 * (NB + 1))

        @block.tensor
        def _(pe):
            hist = {"turn": [], "prod": [], "pair": []}

            def mm(out, a, bb, start, stop):
                return pe.matmul(out, a, bb, start=start, stop=stop, skip_group_check=True)

            def split_product(out, w, x, cols, n):
                terms = [(a, c, k) for a, c in ((0, 0), (0, 1), (1, 0)) for k in range(KC)]
                for t, (a, c, k) in enumerate(terms):
                    r = mm(out, w[a][:, k, cols], x[c][:, k, n * HALF:(n + 1) * HALF], t == 0, t == len(terms) - 1)
                return r

            def turn(bank, src, j):
                for q in range(4):
                    r = pe.transpose(bank[:, q * P:(q + 1) * P], src[:, 4 * (j // 2) + q, (j % 2) * P:(j % 2 + 1) * P], identF[:])
                return r

            def item(b, kind, j):
                const = const_of(kind, j)
                ring = RING[kind]
                past = hist[ring]
                slot = j % 2
                if len(past) >= 2:
                    k0, c0 = past[-2]
                    read, per, nth = taken[k0]
                    if not (kind == "ff" and j < 2):
                        pe.wait_ge(read, count(b, per * C_SEQ[k0], per * c0 + nth))
                past.append((kind, const))
                n, m = j // 2, j % 2
                if kind == "xt":
                    if j == 0:
                        pe.wait_ge(normed["sum"], count(b, 1, 2))
                    r = turn(p_turn[:, slot, :], xn, j)
                elif kind == "d1":
                    if j == 0:
                        pe.wait_ge(normed["wo"], count(b, 1, 0))
                    r = turn(p_turn[:, slot, :], x3, j)
                elif kind in ("v", "q", "g"):
                    pe.wait_ge(xl_ready, count(b, 4, 2 * n + 2))
                    r = split_product(p_prod[:, slot, :], wp[kind], xp, slice(m * P, (m + 1) * P), n)
                elif kind == "rt":
                    pe.wait_ge(ret_ready, count(b, 4, 2 * (j // 2) + 2))
                    bank = p_turn[:, slot, :].rearrange("p (t d) -> p t d", t=2)
                    for u in range(2):
                        t = 2 * j + u
                        for k in range(KC):
                            r = pe.transpose(bank[:, u, k * P:(k + 1) * P], ret[:, k, t * P:(t + 1) * P], identF[:])
                elif kind == "zt":
                    if j == 0:
                        pe.wait_ge(normed["rt"], count(b, 1, 1))
                    r = turn(p_turn[:, slot, :], rt, j)
                elif kind == "wo":
                    pe.wait_ge(z_ready, count(b, 4, 2 * (j // 2) + 2))
                    for u in range(2):
                        t = 2 * j + u
                        for k in range(KC):
                            r = mm(p_prod[:, slot, u * D:(u + 1) * D], zT[:, k, t * P:(t + 1) * P], wo[:, k, :], k == 0, k == KC - 1)
                elif kind == "ff":
                    n, m = divmod(j, FM)
                    if j == 0:
                        pe.wait_ge(prep, PREP)
                        pe.wait_ge(prep_act, PREP_ACT)
                    if m == 0:
                        pe.wait_ge(x3l_ready, count(b, 4, 2 * n + 2 - 4))
                    split_product(p_pair[:, slot, 0, :], wgt, x3p, slice(m * P, (m + 1) * P), n)
                    r = split_product(p_pair[:, slot, 1, :], wup, x3p, slice(m * P, (m + 1) * P), n)
                elif kind == "dn":
                    pe.wait_ge(h_ready, count(b, N_FF, FM * (j // 2 + 1) - N_FF))
                    for u in range(2):
                        t = 2 * j + u
                        for k in range(FM):
                            r = mm(p_prod[:, slot, u * D:(u + 1) * D], h[:, k, t * P:(t + 1) * P], wdn[:, k, :], k == 0, k == FM - 1)
                r.then_inc(ready[kind], 1)

            def step(b, head, tail, combine, gather):
                for ring in hist:
                    hist[ring] = [(k, c - C_SEQ[k]) for k, c in hist[ring][-2:]]
                for kind, j in order(head, tail, combine):
                    if kind in C_SEQ:
                        item(b, kind, j)

            pe.wait_ge(const_in, 48)
            for j in range(4):
                item(-1, "xt", j)
            pe.wait_ge(prep, PREP_FIRST)
            run_steps(pe, step)

        @block.scalar
        def _(act):
            A = nc.scalar
            act.wait_ge(bexp_in, 16)
            A.activation(lam[:], bexp[:], ACT.Exp, scale=-0.6931471805599453).then_inc(lam_exp, 1)

            def item(b, kind, j):
                const = const_of(kind, j)
                slot = j % 2
                n, m = j // 2, j % 2
                cols = slice(n * HALF, (n + 1) * HALF)
                if kind in ("xt", "d1"):
                    act.wait_ge(ready[kind], count(b, 4, const + 1))
                    A.activation((xp if kind == "xt" else x3p)[0][:, m, cols], p_turn[:, slot, :], ACT.Copy)\
                        .then_inc(act_took[kind], 1)
                elif kind == "g":
                    act.wait_ge(ready[kind], count(b, 4, const + 1))
                    A.activation(gT[:, m, cols], p_prod[:, slot, :], ACT.Silu).then_inc(act_took["g"], 1)
                elif kind == "rt":
                    act.wait_ge(ready[kind], count(b, 4, const + 1))
                    A.activation(rt[:, 2 * j:2 * j + 2, :], p_turn[:, slot, :].rearrange("p (t d) -> p t d", t=2), ACT.Copy)\
                        .then_inc(act_took["rt"], 1)
                elif kind == "zt":
                    act.wait_ge(ready[kind], count(b, 4, const + 1))
                    A.activation(zT[:, m, cols], p_turn[:, slot, :], ACT.Identity,
                                 scale=gb[:, 0, m:m + 1], bias=gb[:, 1, m:m + 1]).then_inc(act_took["zt"], 1)
                elif kind == "ff":
                    act.wait_ge(ready[kind], count(b, N_FF, const + 1))
                    A.activation(sg[j % 2][:], p_pair[:, slot, 0, :], ACT.Silu).then_inc(silu_ready, 1)

            def integer_weights():
                act.wait_ge(stage_in[True], 48)
                done = 0
                for (src, cols, dst, integer), off in zip(STAGED, offs):
                    if integer:
                        raw = stage[:, off:off + cols]
                        flat = wdn if dst is wdn else dst[0]
                        flat = flat[:].rearrange("p k n -> p (k n)")
                        if dst is not wdn:
                            A.activation(raw, raw.bitcast(I32), ACT.Copy, scale=SCALE).then_inc(prep_act, 1)
                            done += 1
                            act.wait_ge(prep_act, done)
                            A.activation(flat, raw, ACT.Copy).then_inc(prep_act, 1)
                        else:
                            A.activation(flat, raw.bitcast(I32), ACT.Copy, scale=SCALE).then_inc(prep_act, 1)
                        done += 1
                assert done == PREP_ACT

            def step(b, head, tail, combine, gather):
                for kind, j in order(head, tail, combine):
                    if kind in C_SEQ:
                        item(b, kind, j)
                    if head and kind == "g" and j == 3:
                        integer_weights()

            act.wait_ge(const_in, 48)
            for j in range(4):
                item(-1, "xt", j)
            run_steps(act, step)

        @block.gpsimd
        def _(pool):
            def gather(b, db, tiles, signal):
                if tiles[0] == 0:
                    wait_apart(pool, idx_in, count(b, 16, 16 * (db + 1)))
                for t in tiles:
                    for k in range(TOPK):
                        pool.indirect_dma_start(yg[k][:, t, :], None, T["y"],
                                                bass.IndirectOffsetOnAxis(ap=idx[:, t, k:k + 1].bitcast(U32), axis=0))\
                            .then_inc(signal, 16)

            def root(b, kind, const):
                pool.wait_ge(ve_ready[kind], count(b, 1, const + 1))
                nc.gpsimd.tensor_tensor(rstd[kind][:], vare[kind][:], mhalf[:], ALU.pow).then_inc(rstd_ready[kind], 1)

            def gate(b, j):
                n, m = j // 2, j % 2
                pool.wait_ge(act_took["zt"], count(b, 4, j + 1))
                pool.wait_ge(act_took["g"], count(b, 4, j + 1))
                v = zT[:, m, n * HALF:(n + 1) * HALF]
                nc.gpsimd.tensor_tensor(v, v, gT[:, m, n * HALF:(n + 1) * HALF], ALU.mult).then_inc(z_ready, 1)

            def step(b, head, tail, combine, gather_):
                for kind, j in order(head, tail, combine):
                    if kind == "zt":
                        gate(b, j)
                    elif kind in ("rt_var", "sum_var", "dn_var", "wo_var"):
                        root(b, kind[:-4], {"sum": 1, "dn": -1}.get(kind[:-4], 0))
                        if gather_ and kind == "sum_var":
                            gather(b, 2, range(0, NT // 2), gathered)
                        if gather_ and kind == ("sum_var" if head else "wo_var"):
                            gather(b, 2, range(NT // 2, NT), gathered)

            nc.gpsimd.memset(mhalf[:], -0.5).then_inc(prep_pool, 1)
            pool.wait_ge(prep_pool, 1)
            gather(0, 0, range(0, NT // 2), gathered_0[0])
            gather(0, 0, range(NT // 2, NT), gathered_0[1])
            root(0, "sum", 0)
            gather(0, 1, range(NT), gathered)
            run_steps(pool, step)

        @block.vector
        def _(dve):
            V = nc.vector

            def wrote(kind, b, const, per, n, wait=dve.wait_ge):
                wait(seq[kind], count(b, 4 * per, per * const + n))

            def stats_of(kind, b, const, per, n, src, tiles):
                for t in tiles:
                    V.bn_stats(stats[kind][:, t, :], src[:, t, :]).then_inc(seq[kind], 1)
                wrote(kind, b, const, per, n + 2, lambda semaphore, value: wait_apart(dve, semaphore, value))
                for t in tiles:
                    V.bn_aggr(mv[kind][:, t, :], stats[kind][:, t, :]).then_inc(seq[kind], 1)

            def variance(b, kind, const, per):
                dve.wait_ge(seq[kind], count(b, 4 * per, 4 * per * (const + 1)))
                V.tensor_scalar(vare[kind][:], mv[kind][:, :, 1], EPS, None, ALU.add).then_inc(ve_ready[kind], 1)

            def norm(b, kind, const, half, src, dst):
                if half == 0:
                    dve.wait_ge(rstd_ready[kind], count(b, 1, const + 1))
                for t in range(4 * half, 4 * half + 4):
                    ins = V.tensor_scalar(dst[:, t, :], src[:, t, :], mv[kind][:, t, 0:1], rstd[kind][:, t:t + 1],
                                          ALU.subtract, ALU.mult)
                if half == 1:
                    ins.then_inc(normed[kind], 1)

            def combine_rows(b, db, j):
                if db == 0 and j % 2 == 0:
                    dve.wait_ge(gathered_0[j // 2], 128)
                elif j == 0:
                    dve.wait_ge(gathered, count(b, 256, 256 * db))
                if j == 0:
                    dve.wait_ge(x1_in, count(b, 32, 32 * (db + 1)))
                for k in range(TOPK):
                    for t in (2 * j, 2 * j + 1):
                        V.scalar_tensor_tensor(out=x1t[:, t, :], in0=yg[k][:, t, :], scalar=gates[:, t, k:k + 1],
                                               in1=x1t[:, t, :], op0=ALU.mult, op1=ALU.add).then_inc(seq["sum"], 1)
                    wrote("sum", b, 4 * db + j, SUM_OPS, 2 * k + 2)

            def combine_stats(b, db, j):
                stats_of("sum", b, 4 * db + j, SUM_OPS, 4, x1t, [2 * j, 2 * j + 1])

            def item(b, kind, j):
                const = const_of(kind, j)
                slot = j % 2
                n, m = j // 2, j % 2
                cols = slice(n * HALF, (n + 1) * HALF)
                if kind in ("xt", "d1"):
                    hi, lo = xp if kind == "xt" else x3p
                    dve.wait_ge(act_took[kind], count(b, 4, const + 1))
                    V.tensor_tensor(lo[:, m, cols], p_turn[:, slot, :], hi[:, m, cols].bitcast(F32), ALU.subtract)\
                        .then_inc(xl_ready if kind == "xt" else x3l_ready, 1)
                elif kind == "v":
                    dve.wait_ge(ready["v"], count(b, 4, const + 1))
                    if n:
                        dve.wait_ge(scanned, count(b, 4, j - 1))
                    V.tensor_tensor_scan(ret[:, m, cols], lam[:, m:m + 1].to_broadcast([P, HALF]), p_prod[:, slot, :],
                                         ret[:, m, n * HALF - 1:n * HALF] if n else 0.0, ALU.mult, ALU.add)\
                        .then_inc(scanned, 1)
                elif kind == "q":
                    dve.wait_ge(ready["q"], count(b, 4, const + 1))
                    if j == 0:
                        dve.wait_ge(scanned, count(b, 4, 4))
                    V.tensor_tensor(ret[:, m, cols], p_prod[:, slot, :], ret[:, m, cols], ALU.mult).then_inc(ret_ready, 1)
                elif kind == "rt":
                    dve.wait_ge(act_took["rt"], count(b, 4, const + 1))
                    stats_of("rt", b, const, RT_OPS, 0, rt, [2 * j, 2 * j + 1])
                elif kind == "ff":
                    n, m = divmod(j, FM)
                    dve.wait_ge(silu_ready, count(b, N_FF, const + 1))
                    V.tensor_tensor(h[:, m, n * HALF:(n + 1) * HALF], p_pair[:, slot, 1, :], sg[j % 2][:], ALU.mult)\
                        .then_inc(h_ready, 1)
                elif kind in ("wo", "dn"):
                    dst, base = (x3, x2) if kind == "wo" else (o, x3)
                    dve.wait_ge(ready[kind], count(b, 4, const + 1))
                    if kind == "dn" and j == 0:
                        dve.wait_ge(o_free, count(b, 16, 0))
                    if kind == "wo" and j == 0:
                        dve.wait_ge(x2_ready, count(b, 1, 1))
                    V.tensor_tensor(dst[:, 2 * j:2 * j + 2, :], p_prod[:, slot, :].rearrange("p (t d) -> p t d", t=2),
                                    base[:, 2 * j:2 * j + 2, :], ALU.add).then_inc(seq[kind], 1)
                    wrote(kind, b, const, ADD_OPS, 1)
                    stats_of(kind, b, const, ADD_OPS, 1, dst, [2 * j, 2 * j + 1])

            def step(b, head, tail, combine, gather):
                for kind, j in order(head, tail, combine):
                    if kind in C_SEQ:
                        item(b, kind, j)
                    elif kind == "x2":
                        dve.wait_ge(normed["sum"], count(b, 1, 1))
                        V.tensor_copy(x2[:], xn[:]).then_inc(x2_ready, 1)
                    elif kind == "sum_a":
                        combine_rows(b, 1, j)
                    elif kind == "sum_b":
                        combine_stats(b, 1, j)
                    elif kind == "sum_var":
                        variance(b, "sum", 1, SUM_OPS)
                    elif kind == "rt_var":
                        variance(b, "rt", 0, RT_OPS)
                    elif kind == "wo_var":
                        variance(b, "wo", 0, ADD_OPS)
                    elif kind == "dn_var":
                        variance(b, "dn", -1, ADD_OPS)
                    elif kind == "sum_norm":
                        norm(b, "sum", 1, j, x1t, xn)
                    elif kind == "rt_norm":
                        norm(b, "rt", 0, j, rt, rt)
                    elif kind == "wo_norm":
                        norm(b, "wo", 0, j, x3, x3)
                    elif kind == "dn_norm":
                        norm(b, "dn", -1, j, o, o)
                    if head and kind in ("rt_var", "wo_var"):
                        low_part(3 if kind == "rt_var" else 4)

            k = [0]

            def link(ins):
                k[0] += 1
                ins.then_inc(prep, 1)
                dve.wait_ge(prep, k[0])

            dve.wait_ge(lam_exp, 1)
            link(V.tensor_scalar(lam[:], lam[:], -1.0, 1.0, ALU.mult, ALU.add))
            link(V.tensor_scalar(lam[:], lam[:], TINY, 1.0 - 1e-9, ALU.max, ALU.min))

            def low_part(i):
                if i >= 3:
                    dve.wait_ge(prep_act, 2 * (i - 2))
                raw = stage[:, offs[i]:offs[i] + STAGED[i][1]]
                hi, lo = (d[:].rearrange("p k n -> p (k n)") for d in STAGED[i][2])
                link(V.tensor_tensor(lo, raw, hi.bitcast(F32), ALU.subtract))

            dve.wait_ge(stage_in[False], 48)
            for i in range(3):
                link(V.tensor_copy(STAGED[i][2][0][:].rearrange("p k n -> p (k n)"), stage[:, offs[i]:offs[i] + STAGED[i][1]]))
                low_part(i)
            assert k[0] == PREP_FIRST
            V.memset(o[0:1, 0, 0:1], 0.0).then_inc(o_free, 16)
            for j in range(4):
                combine_rows(0, 0, j)
                combine_stats(0, 0, j)
            variance(0, "sum", 0, SUM_OPS)
            for half in range(2):
                norm(0, "sum", 0, half, x1t, xn)
            for j in range(4):
                item(-1, "xt", j)
            run_steps(dve, step)


def build(nc, T):
    def scratch(name, shape, dt=F32):
        return nc.dram_tensor(name, shape, dt, kind="Internal").ap()

    T["qk_scr"] = scratch("qk_scr", (2, 4, 3, P, HALF), BF16)
    T["m_scr"] = scratch("m_scr", (2, 2, 3, GH * S), BF16)
    T["x1"] = scratch("x1", (NB, S, D))
    T["gates"] = scratch("gates", (NB, P, NT, TOPK))
    T["dest"] = scratch("dest", (NB, P, NT, TOPK), I32)
    T["buf"] = scratch("buf", (NE * SLOTS, D))
    T["y"] = scratch("y", (NE * SLOTS + 1, D))
    with ExitStack() as ctx:
        held = ExpertWeights(nc, ctx, T)
        phase_attention(nc, T, lambda sp: held.load(sp, 0, 0))
        phase_experts(nc, T, held)
    phase_layer1(nc, T)


def constants():
    i = np.arange(P)
    parts = [np.eye(P), np.where(i[None, :] > i[:, None], -HUGE, 0.0), np.where(i[None, :] < i[:, None], -HUGE, 0.0),
             i[:, None] < i[None, :], np.tile(NE - np.arange(NE), (P, NT))]
    return np.concatenate([p.astype(np.float32) for p in parts], axis=1)


def kernel(**inputs):
    import concourse.bacc as bacc
    from concourse.bass_utils import run_bass_kernel_spmd

    g = {k: np.asarray(v) for k, v in inputs.items()}

    def columns(*vectors):
        return np.stack(vectors).reshape(len(vectors), KC, P).transpose(2, 0, 1)

    x = g["L0_attn_x"]
    arrays = {
        "consts": constants(),
        "x": x,
        "xT": x.transpose(0, 2, 1),
        "wq": g["L0_attn_Wq"], "wk": g["L0_attn_Wk"], "wv": g["L0_attn_Wv"], "wo": g["L0_attn_Wo"],
        "bqk": columns(g["L0_attn_bq"], g["L0_attn_bk"]),
        "bv": np.tile(g["L0_attn_bv"], (P, 1)),
        "bo": np.tile(g["L0_attn_bo"], (P, 1)),
        "wg": g["L0_ffn_Wg"], "w1": g["L0_ffn_W1"], "w2": g["L0_ffn_W2"],
        "b1": g["L0_ffn_b1"].reshape(NE, HID // P, P).transpose(0, 2, 1),
        "b2": g["L0_ffn_b2"].reshape(NE, KC, P).transpose(0, 2, 1),
        "w1q": g["L1_attn_Wq"].T, "w1v": g["L1_attn_Wv"].T, "w1o": g["L1_attn_Wo"].T, "w1g": g["L1_attn_Wg"].T,
        "bexp": np.repeat(g["L1_attn_beta"], HD).reshape(KC, P).T,
        "gb": columns(g["L1_attn_ln_gamma"], g["L1_attn_ln_beta"]),
        "wgt": g["L1_ffn_w_gate"].T, "wup": g["L1_ffn_w_up"].T, "wdn": g["L1_ffn_w_down"].T,
    }
    arrays = {"in_" + k: np.ascontiguousarray(v) for k, v in arrays.items()}
    nc = bacc.Bacc("TRN2", target_bir_lowering=False, num_devices=1)
    T = {k[3:]: nc.dram_tensor(k, a.shape, mybir.dt.from_np(a.dtype), kind="ExternalInput").ap()
         for k, a in arrays.items()}
    T["out"] = nc.dram_tensor("out", (NB, S, D), F32, kind="ExternalOutput").ap()
    build(nc, T)
    return run_bass_kernel_spmd(nc, [arrays], core_ids=[0]).results[0]["out"]
```
